# Optimizing a Trainium2 kernel written in Bass

```python
import numpy as np
import jax
import jax.numpy as jnp

def _softmax(x, axis=-1):
    return jax.nn.softmax(x, axis=axis)

def _gelu(x):
    return jax.nn.gelu(x, approximate=True)

def _silu(x):
    return jax.nn.silu(x)

def _sigmoid(x):
    return jax.nn.sigmoid(x)

def _layernorm(x, axis=-1, eps=1e-05):
    m = jnp.mean(x, axis=axis, keepdims=True)
    v = jnp.var(x, axis=axis, keepdims=True)
    return (x - m) / jnp.sqrt(v + eps)

def _scatter_add(tgt, idx, src, axis=0):
    return tgt.at[idx].add(src)

def _segment_sum(src, seg, n):
    return jax.ops.segment_sum(src, seg, n)
kernel_name = 'mk_prb_d1_jaxref_r4_476f96'

def setup_inputs(seed: int=0):
    np.random.seed(seed)
    _w = jnp.asarray

    def _L0_attn_setup():
        import jax, jax.numpy as jnp
        import numpy as np
        D_MODEL = 512
        D_STATE = 128
        D_CONV = 4
        EXPAND = 2
        HEADDIM = 64
        NGROUPS = 1
        CHUNK = 64
        D_INNER = EXPAND * D_MODEL
        NHEADS = D_INNER // HEADDIM
        HG = NHEADS // NGROUPS
        CONV_DIM = D_INNER + 2 * NGROUPS * D_STATE
        D_IN_PROJ = 2 * D_INNER + 2 * NGROUPS * D_STATE + NHEADS
        BATCH = 2
        SEQLEN = 512
        EPS = 1e-05

        def _mamba2(u, in_proj_w, conv_w, conv_b, dt_bias, A_log, D_skip, norm_w, out_proj_w):
            b, l, _ = u.shape
            nc = l // CHUNK
            zxbcdt = u @ in_proj_w.T
            z = zxbcdt[..., :D_INNER]
            xBC = zxbcdt[..., D_INNER:D_INNER + CONV_DIM]
            dt = jax.nn.softplus(zxbcdt[..., D_INNER + CONV_DIM:] + dt_bias)
            xp = jnp.pad(xBC, ((0, 0), (D_CONV - 1, 0), (0, 0)))
            conv = conv_b + sum((conv_w[:, k] * xp[:, k:k + l, :] for k in range(D_CONV)))
            xBC = jax.nn.silu(conv)
            x = xBC[..., :D_INNER].reshape(b, l, NHEADS, HEADDIM)
            Bm = xBC[..., D_INNER:D_INNER + NGROUPS * D_STATE].reshape(b, l, NGROUPS, D_STATE)
            Cm = xBC[..., D_INNER + NGROUPS * D_STATE:].reshape(b, l, NGROUPS, D_STATE)
            A = -jnp.exp(A_log)
            xc = x.reshape(b, nc, CHUNK, NGROUPS, HG, HEADDIM)
            dtc = dt.reshape(b, nc, CHUNK, NGROUPS, HG)
            Bc = Bm.reshape(b, nc, CHUNK, NGROUPS, D_STATE)
            Cc = Cm.reshape(b, nc, CHUNK, NGROUPS, D_STATE)
            dA = jnp.transpose(dtc * A.reshape(NGROUPS, HG), (0, 3, 4, 1, 2))
            dA_cs = jnp.cumsum(dA, axis=-1)
            seg = dA_cs[..., :, None] - dA_cs[..., None, :]
            tri = jnp.tril(jnp.ones((CHUNK, CHUNK), bool))
            Lmat = jnp.where(tri, jnp.exp(seg), 0.0)
            xdt = xc * dtc[..., None]
            CB = jnp.einsum('bclgn,bcsgn->bcgls', Cc, Bc)
            Y_diag = jnp.einsum('bcgls,bgHcls,bcsgHp->bclgHp', CB, Lmat, xdt)
            decay_states = jnp.exp(dA_cs[..., -1:] - dA_cs)
            states = jnp.einsum('bcsgn,bgHcs,bcsgHp->bcgHpn', Bc, decay_states, xdt)
            chunk_decay = jnp.exp(dA_cs[..., -1])

            def step(carry, inp):
                st, dec = inp
                return (carry * dec[..., None, None] + st, carry)
            _, prev = jax.lax.scan(step, jnp.zeros_like(states[:, 0]), (jnp.moveaxis(states, 1, 0), jnp.moveaxis(chunk_decay, -1, 0)))
            prev = jnp.moveaxis(prev, 0, 1)
            Y_off = jnp.einsum('bclgn,bcgHpn,bgHcl->bclgHp', Cc, prev, jnp.exp(dA_cs))
            y = (Y_diag + Y_off).reshape(b, l, NHEADS, HEADDIM) + x * D_skip[None, None, :, None]
            y = y.reshape(b, l, D_INNER)
            y = y * jax.nn.silu(z)
            yg = y.reshape(b, l, NGROUPS, D_INNER // NGROUPS)
            yg = yg * jax.lax.rsqrt(jnp.mean(yg * yg, axis=-1, keepdims=True) + EPS)
            y = yg.reshape(b, l, D_INNER) * norm_w
            return y @ out_proj_w.T
        ks = jax.random.split(jax.random.key(seed), 8)
        u = jax.random.normal(ks[0], (BATCH, SEQLEN, D_MODEL), jnp.float32)
        in_proj_w = jax.random.normal(ks[1], (D_IN_PROJ, D_MODEL), jnp.float32) * D_MODEL ** (-0.5)
        conv_w = jax.random.normal(ks[2], (CONV_DIM, D_CONV), jnp.float32) * D_CONV ** (-0.5)
        conv_b = jax.random.normal(ks[3], (CONV_DIM,), jnp.float32) * 0.1
        dt = jnp.exp(jax.random.uniform(ks[4], (NHEADS,), jnp.float32) * (np.float32(np.log(0.1)) - np.float32(np.log(0.001))) + np.float32(np.log(0.001)))
        dt = jnp.clip(dt, 0.0001, None)
        dt_bias = dt + jnp.log(-jnp.expm1(-dt))
        A_log = jnp.log(jax.random.uniform(ks[5], (NHEADS,), jnp.float32, minval=1.0, maxval=16.0))
        D_skip = jnp.ones((NHEADS,), jnp.float32)
        norm_w = jnp.ones((D_INNER,), jnp.float32)
        out_proj_w = jax.random.normal(ks[6], (D_MODEL, D_INNER), jnp.float32) * D_INNER ** (-0.5)
        return dict(u=u, in_proj_w=in_proj_w, conv_w=conv_w, conv_b=conv_b, dt_bias=dt_bias, A_log=A_log, D_skip=D_skip, norm_w=norm_w, out_proj_w=out_proj_w)
    _L0_attn_in = _L0_attn_setup()

    def _L0_ffn_setup():
        import jax, jax.numpy as jnp
        import numpy as np
        TOP_K = 2

        def moe_forward(x, w_gate_router, w_gate_proj, w_up_proj, w_down_proj):
            E = w_gate_router.shape[0]
            scores = jnp.einsum('bsd,ed->bse', x, w_gate_router)
            topk_scores, topk_idx = jax.lax.top_k(scores, TOP_K)
            topk_probs = jax.nn.softmax(topk_scores, axis=-1)
            weights = jnp.sum(topk_probs[..., None] * jax.nn.one_hot(topk_idx, E, dtype=x.dtype), axis=-2)
            gate = jnp.einsum('bsd,efd->bsef', x, w_gate_proj)
            up = jnp.einsum('bsd,efd->bsef', x, w_up_proj)
            hidden = jax.nn.silu(gate) * up
            out = jnp.einsum('bsef,edf,bse->bsd', hidden, w_down_proj, weights)
            return out
        key = jax.random.key(seed)
        k1, k2, k3, k4, k5 = jax.random.split(key, 5)
        B, S, D, E, F = (2, 256, 512, 8, 192)
        scale_in = 1.0 / np.sqrt(D)
        scale_ff = 1.0 / np.sqrt(F)
        return {'x': jax.random.normal(k1, (B, S, D), dtype=jnp.float32), 'w_gate_router': jax.random.normal(k2, (E, D), dtype=jnp.float32) * scale_in, 'w_gate_proj': jax.random.normal(k3, (E, F, D), dtype=jnp.float32) * scale_in, 'w_up_proj': jax.random.normal(k4, (E, F, D), dtype=jnp.float32) * scale_in, 'w_down_proj': jax.random.normal(k5, (E, D, F), dtype=jnp.float32) * scale_ff}
    _L0_ffn_in = _L0_ffn_setup()
    _d = {'L0_attn_u': _L0_attn_in['u'], 'L0_attn_in_proj_w': _L0_attn_in['in_proj_w'], 'L0_attn_conv_w': _L0_attn_in['conv_w'], 'L0_attn_conv_b': _L0_attn_in['conv_b'], 'L0_attn_dt_bias': _L0_attn_in['dt_bias'], 'L0_attn_A_log': _L0_attn_in['A_log'], 'L0_attn_D_skip': _L0_attn_in['D_skip'], 'L0_attn_norm_w': _L0_attn_in['norm_w'], 'L0_attn_out_proj_w': _L0_attn_in['out_proj_w'], 'L0_ffn_w_gate_router': _L0_ffn_in['w_gate_router'], 'L0_ffn_w_gate_proj': _L0_ffn_in['w_gate_proj'], 'L0_ffn_w_up_proj': _L0_ffn_in['w_up_proj'], 'L0_ffn_w_down_proj': _L0_ffn_in['w_down_proj']}
    _x0 = _d['L0_attn_u']
    _d['L0_attn_u'] = jax.random.normal(jax.random.fold_in(jax.random.key(seed), 1), (1, 2048, 512), dtype=_x0.dtype)
    del _x0
    return _d

def reference(L0_attn_u, L0_attn_in_proj_w, L0_attn_conv_w, L0_attn_conv_b, L0_attn_dt_bias, L0_attn_A_log, L0_attn_D_skip, L0_attn_norm_w, L0_attn_out_proj_w, L0_ffn_w_gate_router, L0_ffn_w_gate_proj, L0_ffn_w_up_proj, L0_ffn_w_down_proj):

    def _L0_attn_ref(u, in_proj_w, conv_w, conv_b, dt_bias, A_log, D_skip, norm_w, out_proj_w):
        import jax, jax.numpy as jnp
        import numpy as np
        D_MODEL = 512
        D_STATE = 128
        D_CONV = 4
        EXPAND = 2
        HEADDIM = 64
        NGROUPS = 1
        CHUNK = 64
        D_INNER = EXPAND * D_MODEL
        NHEADS = D_INNER // HEADDIM
        HG = NHEADS // NGROUPS
        CONV_DIM = D_INNER + 2 * NGROUPS * D_STATE
        D_IN_PROJ = 2 * D_INNER + 2 * NGROUPS * D_STATE + NHEADS
        BATCH = 2
        SEQLEN = 512
        EPS = 1e-05

        def _mamba2(u, in_proj_w, conv_w, conv_b, dt_bias, A_log, D_skip, norm_w, out_proj_w):
            b, l, _ = u.shape
            nc = l // CHUNK
            zxbcdt = u @ in_proj_w.T
            z = zxbcdt[..., :D_INNER]
            xBC = zxbcdt[..., D_INNER:D_INNER + CONV_DIM]
            dt = jax.nn.softplus(zxbcdt[..., D_INNER + CONV_DIM:] + dt_bias)
            xp = jnp.pad(xBC, ((0, 0), (D_CONV - 1, 0), (0, 0)))
            conv = conv_b + sum((conv_w[:, k] * xp[:, k:k + l, :] for k in range(D_CONV)))
            xBC = jax.nn.silu(conv)
            x = xBC[..., :D_INNER].reshape(b, l, NHEADS, HEADDIM)
            Bm = xBC[..., D_INNER:D_INNER + NGROUPS * D_STATE].reshape(b, l, NGROUPS, D_STATE)
            Cm = xBC[..., D_INNER + NGROUPS * D_STATE:].reshape(b, l, NGROUPS, D_STATE)
            A = -jnp.exp(A_log)
            xc = x.reshape(b, nc, CHUNK, NGROUPS, HG, HEADDIM)
            dtc = dt.reshape(b, nc, CHUNK, NGROUPS, HG)
            Bc = Bm.reshape(b, nc, CHUNK, NGROUPS, D_STATE)
            Cc = Cm.reshape(b, nc, CHUNK, NGROUPS, D_STATE)
            dA = jnp.transpose(dtc * A.reshape(NGROUPS, HG), (0, 3, 4, 1, 2))
            dA_cs = jnp.cumsum(dA, axis=-1)
            seg = dA_cs[..., :, None] - dA_cs[..., None, :]
            tri = jnp.tril(jnp.ones((CHUNK, CHUNK), bool))
            Lmat = jnp.where(tri, jnp.exp(seg), 0.0)
            xdt = xc * dtc[..., None]
            CB = jnp.einsum('bclgn,bcsgn->bcgls', Cc, Bc)
            Y_diag = jnp.einsum('bcgls,bgHcls,bcsgHp->bclgHp', CB, Lmat, xdt)
            decay_states = jnp.exp(dA_cs[..., -1:] - dA_cs)
            states = jnp.einsum('bcsgn,bgHcs,bcsgHp->bcgHpn', Bc, decay_states, xdt)
            chunk_decay = jnp.exp(dA_cs[..., -1])

            def step(carry, inp):
                st, dec = inp
                return (carry * dec[..., None, None] + st, carry)
            _, prev = jax.lax.scan(step, jnp.zeros_like(states[:, 0]), (jnp.moveaxis(states, 1, 0), jnp.moveaxis(chunk_decay, -1, 0)))
            prev = jnp.moveaxis(prev, 0, 1)
            Y_off = jnp.einsum('bclgn,bcgHpn,bgHcl->bclgHp', Cc, prev, jnp.exp(dA_cs))
            y = (Y_diag + Y_off).reshape(b, l, NHEADS, HEADDIM) + x * D_skip[None, None, :, None]
            y = y.reshape(b, l, D_INNER)
            y = y * jax.nn.silu(z)
            yg = y.reshape(b, l, NGROUPS, D_INNER // NGROUPS)
            yg = yg * jax.lax.rsqrt(jnp.mean(yg * yg, axis=-1, keepdims=True) + EPS)
            y = yg.reshape(b, l, D_INNER) * norm_w
            return y @ out_proj_w.T
        return _mamba2(u, in_proj_w, conv_w, conv_b, dt_bias, A_log, D_skip, norm_w, out_proj_w)

    def _L0_ffn_ref(x, w_gate_router, w_gate_proj, w_up_proj, w_down_proj):
        import jax, jax.numpy as jnp
        import numpy as np
        TOP_K = 2

        def moe_forward(x, w_gate_router, w_gate_proj, w_up_proj, w_down_proj):
            E = w_gate_router.shape[0]
            scores = jnp.einsum('bsd,ed->bse', x, w_gate_router)
            topk_scores, topk_idx = jax.lax.top_k(scores, TOP_K)
            topk_probs = jax.nn.softmax(topk_scores, axis=-1)
            weights = jnp.sum(topk_probs[..., None] * jax.nn.one_hot(topk_idx, E, dtype=x.dtype), axis=-2)
            gate = jnp.einsum('bsd,efd->bsef', x, w_gate_proj)
            up = jnp.einsum('bsd,efd->bsef', x, w_up_proj)
            hidden = jax.nn.silu(gate) * up
            out = jnp.einsum('bsef,edf,bse->bsd', hidden, w_down_proj, weights)
            return out
        return moe_forward(x, w_gate_router, w_gate_proj, w_up_proj, w_down_proj)
    x = L0_attn_u
    xn = _layernorm(x, axis=-1)
    x = x + _L0_attn_ref(xn, L0_attn_in_proj_w, L0_attn_conv_w, L0_attn_conv_b, L0_attn_dt_bias, L0_attn_A_log, L0_attn_D_skip, L0_attn_norm_w, L0_attn_out_proj_w) + _L0_ffn_ref(xn, L0_ffn_w_gate_router, L0_ffn_w_gate_proj, L0_ffn_w_up_proj, L0_ffn_w_down_proj)
    return x

_drawn_inputs = setup_inputs


def setup_inputs(seed=0):
    import zlib

    import numpy as np

    out = dict(_drawn_inputs(seed))
    spreads = {'L0_attn_D_skip': (1.0, 0.2), 'L0_attn_norm_w': (1.0, 0.2)}
    factors = {}
    for name, (base, spread) in spreads.items():
        noise = np.random.default_rng([zlib.crc32(name.encode()), seed]).standard_normal(out[name].shape)
        drawn = base * np.exp(spread * noise) if base else spread * noise
        out[name] = jnp.asarray(drawn.astype(out[name].dtype))
    for name, factor in factors.items():
        out[name] = (out[name] * factor).astype(out[name].dtype)
    return out
```

```python
from contextlib import ExitStack

import concourse.bass as bass
from concourse import mybir

ALU = mybir.AluOpType
ACT = mybir.ActivationFunctionType
AX = mybir.AxisListType
F32 = mybir.dt.float32
F32R = mybir.dt.float32r

P = 128
TOKENS, D = 2048, 512
KD = D // P
INNER, STATE, HEADS, HD, TAPS = 1024, 128, 16, 64, 4
XB = INNER // P
CB = XB + 2
E, F = 8, 192
FH = F // 2
T = TOKENS // P
G = T // 2
GT = 2 * P
Q = 4
EPS = 1e-5
BIG = 1.0e30


def front_and_rest(nc, x, w_in, w_dtr, w_out, conv_w, conv_b, dt_bias, a_log, d_skip, norm_w,
                   w_gu, w_down, ident_in, tri_in, rank_in, out):
    ctx = ExitStack()
    with ctx:
        def sem(name):
            return ctx.enter_context(nc.semaphore(name))

        def dram(name, shape, dt=F32):
            return nc.dram_tensor(name, shape, dt, kind="Internal").ap()

        xn_d = dram("xn_d", (T, P, D))
        xth_d = dram("xth_d", (G, P, KD, GT))
        xtl_d = dram("xtl_d", (G, P, KD, GT))
        cs_d = dram("cs_d", (T, HEADS, P))
        moe_d = dram("moe_d", (T, P, D))

        def alloc(stack):
            def sb(name, shape, dt=F32):
                return stack.enter_context(nc.sbuf_tensor(name, shape, dt))

            def pb(name, shape):
                return stack.enter_context(nc.psum_tensor(name, shape, F32))
            return sb, pb

        sb, _ = alloc(ctx)
        ident = sb("ident", [P, P])
        tri = sb("tri", [P, P])
        cs_tok = sb("cs_tok", [P, T, HEADS])
        dt_tok = sb("dt_tok", [P, T, HEADS])
        wts = sb("wts", [P, T, E])

        consts_in = sem("consts_in")
        front(nc, alloc, sem, x, w_dtr, dt_bias, a_log, ident_in, tri_in, rank_in,
              xn_d, xth_d, xtl_d, cs_d, ident, tri, cs_tok, dt_tok, wts, consts_in)
        experts(nc, alloc, sem, w_gu, w_down, xn_d, moe_d, ident, wts)
        mamba(nc, alloc, sem, x, w_in, w_out, conv_w, conv_b, d_skip, norm_w,
              xth_d, xtl_d, cs_d, moe_d, ident, tri, cs_tok, dt_tok, out)


def front(nc, alloc, sem, x, w_dtr_in, dt_bias, a_log, ident_in, tri_in, rank_in,
          xn_d, xth_d, xtl_d, cs_d, ident, tri, cs_tok, dt_tok, wts, consts_in):
    TQ = T // Q
    C = HEADS + E
    with ExitStack() as ctx:
        sb, pb = alloc(ctx)
        xin = sb("xin", [P, TQ, D])
        xn = sb("xn", [P, TQ, D])
        stats = sb("stats", [P, TQ, 6])
        mv = sb("mv", [P, TQ, 2])
        veps = sb("veps", [P, TQ])
        rstd = sb("rstd", [P, TQ])
        nhalf = sb("nhalf", [P, TQ])
        xth = sb("xth", [P, KD, TQ * P], F32R)
        xtl = sb("xtl", [P, KD, TQ * P], F32R)
        wr = sb("wr", [P, KD, C])
        wrh = sb("wrh", [P, KD, C], F32R)
        wrl = sb("wrl", [P, KD, C], F32R)
        rt = sb("rt", [C, TQ * P])
        rr = sb("rr", [P, T, C])
        bias_bc = sb("bias_bc", [P, HEADS])
        alog_bc = sb("alog_bc", [P, HEADS])
        a_bc = sb("a_bc", [P, HEADS])
        rank = sb("rank", [P, E])
        big = [sb(f"sp{i}", [P, T, HEADS]) for i in range(6)]
        e8 = [sb(f"rt8_{i}", [P, T, E]) for i in range(5)]
        t1 = [sb(f"rt1_{i}", [P, T]) for i in range(6)]
        cst_rows = sb("cst_rows", [HEADS, T, P])
        pt = [pb(f"pt{i}", [P, KD, P]) for i in range(2)]
        pr = pb("pr", [C, TQ * P])
        prt = pb("prt", [P, TQ, C])
        pcs = pb("pcs", [P, T, HEADS])
        pct = [pb(f"pct{i}", [HEADS, 4, P]) for i in range(2)]

        x_in = [sem(f"x_in{j}") for j in range(TQ)]
        mv_done = sem("mv_done")
        rstd_done = sem("rstd_done")
        xn_done = sem("xn_done")
        xn_out = sem("xn_out")
        tr_done = sem("tr_done")
        hi_done = sem("hi_done")
        lo_done = sem("lo_done")
        xt_out = sem("xt_out")
        r_done = sem("r_done")
        rt_done = sem("rt_done")
        rtr_done = sem("rtr_done")
        rr_done = sem("rr_done")
        st_chain = sem("st_chain")
        setup = sem("f_setup")
        wrh_done = sem("wrh_done")
        a_done = sem("a_done")
        nh_done = sem("nh_done")
        e1 = sem("e1")
        b1 = sem("b1")
        cs_ready = sem("cs_ready")
        cs_copied = sem("cs_copied")
        ct_done = sem("ct_done")
        ct_copied = sem("ct_copied")
        cs_out = sem("cs_out")
        chain = sem("f_chain")
        block = ctx.enter_context(nc.Block())
        bc = lambda ap, n: ap.unsqueeze(2).broadcast_to([P, T, n])

        @block.sync
        def _(sp):
            sp.dma_start(ident[:, :], ident_in).then_inc(consts_in, 16)
            sp.dma_start(tri[:, :], tri_in).then_inc(consts_in, 16)
            sp.dma_start(wr[:, :, :], w_dtr_in).then_inc(consts_in, 16)
            sp.dma_start(rank[:, :], rank_in.broadcast_to([P, E])).then_inc(consts_in, 16)
            sp.dma_start(bias_bc[:, :], dt_bias.broadcast_to([P, HEADS])).then_inc(consts_in, 16)
            sp.dma_start(alog_bc[:, :], a_log.broadcast_to([P, HEADS])).then_inc(consts_in, 16)
            xt = x.rearrange("(t p) d -> t p d", p=P)
            sp.sem_inc(xn_out, 16 * TQ)
            sp.sem_inc(xt_out, 64)
            with sp.Fori(0, Q) as q:
                for j in range(TQ):
                    sp.wait_ge(xn_done, q * TQ + j + 1)
                    sp.dma_start(xin[:, j, :], xt[q * TQ + j]).then_inc(x_in[j], 16)
                for j in range(TQ):
                    sp.wait_ge(xn_done, q * TQ + j + 1 + TQ)
                    sp.dma_start(xn_d[q * TQ + j], xn[:, j, :]).then_inc(xn_out, 16)
                sp.wait_ge(lo_done, q * TQ + TQ + 2)
                for h in range(2):
                    sp.dma_start(xth_d[q * 2 + h], xth[:, :, h * GT:(h + 1) * GT].bitcast(F32)).then_inc(xt_out, 16)
                    sp.dma_start(xtl_d[q * 2 + h], xtl[:, :, h * GT:(h + 1) * GT].bitcast(F32)).then_inc(xt_out, 16)
            sp.wait_ge(ct_copied, 4)
            sp.dma_start(cs_d.rearrange("t h l -> h t l"), cst_rows[:, :, :]).then_inc(cs_out, 16)
            sp.wait_ge(cs_out, 16)
            sp.wait_ge(xn_out, 16 * (T + TQ))
            sp.wait_ge(xt_out, 64 * (Q + 1))

        @block.gpsimd
        def _(pool):
            pool.memset(nhalf[:, :], -0.5).then_inc(nh_done, 1)
            pool.wait_ge(nh_done, 1)
            with pool.Fori(0, Q) as q:
                pool.wait_ge(mv_done, q + 1)
                pool.tensor_tensor(rstd[:, :], veps[:, :], nhalf[:, :], ALU.pow).then_inc(rstd_done, 1)

        @block.scalar
        def _(act):
            act.wait_ge(consts_in, 96)
            act.copy(wrh[:, :, :], wr[:, :, :]).then_inc(wrh_done, 1)
            act.activation(a_bc[:, :], alog_bc[:, :], ACT.Exp).then_inc(a_done, 1)
            with act.Fori(0, Q) as q:
                for j in range(TQ):
                    act.wait_ge(tr_done, q * TQ + j + 1)
                    if j == 0:
                        act.wait_ge(xt_out, q * 64 + 64)
                        act.wait_ge(r_done, q + 1)
                    act.copy(xth[:, :, j * P:(j + 1) * P], pt[j % 2][:, :, :]).then_inc(hi_done, 1)
            act.wait_ge(b1, 1)
            act.activation(big[1][:, :, :], big[1][:, :, :], ACT.Exp).then_inc(e1, 1)
            act.wait_ge(b1, 2)
            act.activation(t1[2][:, :], t1[2][:, :], ACT.Exp).then_inc(e1, 1)
            for k in range(4):
                act.wait_ge(ct_done, k + 1)
                act.copy(cst_rows[:, 4 * k:4 * k + 4, :], pct[k % 2][:, :, :]).then_inc(ct_copied, 1)

        @block.vector
        def _(dve):
            dve.sem_inc(xn_done, TQ)
            dve.sem_inc(lo_done, 2)
            n_chain = [0]

            def link(ins):
                n_chain[0] += 1
                ins.then_inc(chain, 1)
                dve.wait_ge(chain, n_chain[0])

            dve.wait_ge(wrh_done, 1)
            dve.tensor_tensor(wrl[:, :, :], wr[:, :, :], wrh[:, :, :].bitcast(F32), ALU.subtract).then_inc(setup, 1)
            with dve.Fori(0, Q) as q:
                for j in range(TQ):
                    dve.wait_ge(x_in[j], q * 16 + 16)
                    dve.bn_stats(stats[:, j, :], xin[:, j, :]).then_inc(st_chain, 1)
                even, odd = stats[:, :, 1], stats[:, :, 4]
                base = q * (TQ + 4) + TQ
                dve.wait_ge(st_chain, base)
                dve.tensor_tensor(mv[:, :, 0], even, odd, ALU.add).then_inc(st_chain, 1)
                dve.tensor_tensor(mv[:, :, 1], even, odd, ALU.subtract).then_inc(st_chain, 1)
                dve.tensor_tensor(veps[:, :], stats[:, :, 2], stats[:, :, 5], ALU.add).then_inc(st_chain, 1)
                dve.wait_ge(st_chain, base + 3)
                dve.tensor_scalar(mv[:, :, 0], mv[:, :, 0], 0.5, None, ALU.mult)
                dve.scalar_tensor_tensor(out=mv[:, :, 1], in0=mv[:, :, 1], scalar=0.25, in1=mv[:, :, 1],
                                         op0=ALU.mult, op1=ALU.mult)
                dve.tensor_scalar(veps[:, :], veps[:, :], 1.0 / D, EPS, ALU.mult, ALU.add).then_inc(st_chain, 1)
                dve.wait_ge(st_chain, base + 4)
                dve.tensor_tensor(veps[:, :], veps[:, :], mv[:, :, 1], ALU.add).then_inc(mv_done, 1)
                dve.wait_ge(rstd_done, q + 1)
                for j in range(TQ):
                    dve.wait_ge(xn_out, q * (16 * TQ) + 16 * TQ)
                    dve.wait_ge(tr_done, q * TQ + j + 0 + 0) if False else None
                    dve.tensor_scalar(xn[:, j, :], xin[:, j, :], mv[:, j, 0:1], rstd[:, j:j + 1],
                                      ALU.subtract, ALU.mult).then_inc(xn_done, 1)
                for j in range(TQ):
                    dve.wait_ge(hi_done, q * TQ + j + 1)
                    if j == 0:
                        dve.wait_ge(r_done, q + 1)
                    dve.tensor_tensor(xtl[:, :, j * P:(j + 1) * P], pt[j % 2][:, :, :],
                                      xth[:, :, j * P:(j + 1) * P].bitcast(F32), ALU.subtract).then_inc(lo_done, 1)
                dve.wait_ge(r_done, q + 2)
                dve.tensor_copy(rt[:, :], pr[:, :]).then_inc(rt_done, 1)
                dve.wait_ge(rtr_done, q + 1)
                dve.tensor_copy(rr[:, bass.ds(q * TQ, TQ), :], prt[:, :, :]).then_inc(rr_done, 1)
            dve.wait_ge(rr_done, Q)

            v, ex, s, s2, acc, den = big
            bias3 = bias_bc[:, :].unsqueeze(1).broadcast_to([P, T, HEADS])
            link(dve.tensor_tensor(v[:, :, :], rr[:, :, 0:HEADS], bias3, ALU.add))
            dve.scalar_tensor_tensor(out=ex[:, :, :], in0=v[:, :, :], scalar=-1.0, in1=v[:, :, :],
                                     op0=ALU.mult, op1=ALU.min).then_inc(b1, 1)
            sc = rr[:, :, HEADS:C]
            rank3 = rank[:, :].unsqueeze(1).broadcast_to([P, T, E])
            one1, one2, w1, s_rest, w2 = e8
            m1, i1, m2, p1, p2, i2 = t1
            link(dve.tensor_reduce(m1[:, :], sc, AX.X, ALU.max))
            link(dve.tensor_tensor(w1[:, :, :], sc, bc(m1[:, :], E), ALU.is_equal))
            link(dve.tensor_tensor(w2[:, :, :], w1[:, :, :], rank3, ALU.mult))
            link(dve.tensor_reduce(i1[:, :], w2[:, :, :], AX.X, ALU.max))
            link(dve.tensor_tensor(one1[:, :, :], rank3, bc(i1[:, :], E), ALU.is_equal))
            link(dve.scalar_tensor_tensor(out=s_rest[:, :, :], in0=one1[:, :, :], scalar=-BIG, in1=sc,
                                          op0=ALU.mult, op1=ALU.add))
            link(dve.tensor_reduce(p2[:, :], s_rest[:, :, :], AX.X, ALU.max))
            link(dve.tensor_tensor(w1[:, :, :], s_rest[:, :, :], bc(p2[:, :], E), ALU.is_equal))
            link(dve.tensor_tensor(w2[:, :, :], w1[:, :, :], rank3, ALU.mult))
            link(dve.tensor_reduce(i2[:, :], w2[:, :, :], AX.X, ALU.max))
            link(dve.tensor_tensor(one2[:, :, :], rank3, bc(i2[:, :], E), ALU.is_equal))
            dve.tensor_tensor(m2[:, :], p2[:, :], m1[:, :], ALU.subtract).then_inc(b1, 1)

            dve.wait_ge(e1, 1)
            link(dve.tensor_scalar(den[:, :, :], ex[:, :, :], 2.0, None, ALU.add))
            link(dve.reciprocal(acc[:, :, :], den[:, :, :]))
            link(dve.tensor_tensor(s[:, :, :], ex[:, :, :], acc[:, :, :], ALU.mult))
            link(dve.tensor_tensor(s2[:, :, :], s[:, :, :], s[:, :, :], ALU.mult))
            link(dve.tensor_scalar(acc[:, :, :], s2[:, :, :], 1.0 / 17, None, ALU.mult))
            for k in (15, 13, 11, 9, 7, 5, 3):
                link(dve.scalar_tensor_tensor(out=acc[:, :, :], in0=acc[:, :, :], scalar=1.0 / k, in1=s2[:, :, :],
                                              op0=ALU.add, op1=ALU.mult))
            link(dve.scalar_tensor_tensor(out=acc[:, :, :], in0=acc[:, :, :], scalar=1.0, in1=s[:, :, :],
                                          op0=ALU.add, op1=ALU.mult))
            link(dve.tensor_scalar(den[:, :, :], v[:, :, :], 0.0, None, ALU.max))
            link(dve.scalar_tensor_tensor(out=dt_tok[:, :, :], in0=acc[:, :, :], scalar=2.0, in1=den[:, :, :],
                                          op0=ALU.mult, op1=ALU.add))
            dve.wait_ge(a_done, 1)
            dve.scalar_tensor_tensor(out=s[:, :, :], in0=dt_tok[:, :, :], scalar=-1.0,
                                     in1=a_bc[:, :].unsqueeze(1).broadcast_to([P, T, HEADS]),
                                     op0=ALU.mult, op1=ALU.mult).then_inc(setup, 1)
            dve.wait_ge(cs_ready, 1)
            dve.tensor_copy(cs_tok[:, :, :], pcs[:, :, :]).then_inc(cs_copied, 1)

            dve.wait_ge(e1, 2)
            link(dve.tensor_scalar(p1[:, :], m2[:, :], 1.0, None, ALU.add))
            link(dve.reciprocal(i1[:, :], p1[:, :]))
            link(dve.tensor_scalar(p1[:, :], i1[:, :], 0.5, None, ALU.mult))
            link(dve.tensor_tensor(i2[:, :], p1[:, :], m2[:, :], ALU.mult))
            link(dve.tensor_tensor(w1[:, :, :], one1[:, :, :], bc(p1[:, :], E), ALU.mult))
            link(dve.tensor_tensor(w2[:, :, :], one2[:, :, :], bc(i2[:, :], E), ALU.mult))
            link(dve.tensor_tensor(wts[:, :, :], w1[:, :, :], w2[:, :, :], ALU.add))

        @block.tensor
        def _(pe):
            pe.sem_inc(r_done, 1)
            pe.wait_ge(consts_in, 96)
            pe.wait_ge(setup, 1)
            with pe.Fori(0, Q) as q:
                for j in range(TQ):
                    pe.wait_ge(xn_done, q * TQ + j + 1 + TQ)
                    pe.wait_ge(lo_done, q * TQ + j + 1)
                    for k in range(KD):
                        tr = pe.transpose(pt[j % 2][:, k, :], xn[:, j, k * P:(k + 1) * P], ident[:, :])
                    tr.then_inc(tr_done, 1)
                pe.wait_ge(lo_done, q * TQ + TQ + 2)
                pe.wait_ge(rt_done, q) if False else None
                n = 0
                for wx, xx in ((wrh, xth), (wrl, xth), (wrh, xtl)):
                    for k in range(KD):
                        mm = pe.matmul(pr[:, :], wx[:, k, :], xx[:, k, :], start=n == 0, stop=n == 11)
                        n += 1
                mm.then_inc(r_done, 1)
                pe.wait_ge(rt_done, q + 1)
                pe.matmul(prt[:, 0, :], rt[:, 0:P], ident[0:C, 0:C], start=True, stop=True)
                for j in range(1, TQ):
                    tr = pe.transpose(prt[:, j, :], rt[:, j * P:(j + 1) * P], ident[0:C, 0:C])
                tr.then_inc(rtr_done, 1)
            pe.wait_ge(setup, 2)
            pe.matmul(pcs[:, :, :].rearrange("p t h -> p (t h)"), tri[:, :],
                      big[2][:, :, :].rearrange("p t h -> p (t h)"), start=True, stop=True).then_inc(cs_ready, 1)
            pe.wait_ge(cs_copied, 1)
            for k in range(4):
                if k >= 2:
                    pe.wait_ge(ct_copied, k - 1)
                for j in range(4):
                    tr = pe.transpose(pct[k % 2][:, j, :], cs_tok[:, 4 * k + j, :], ident[:, :])
                tr.then_inc(ct_done, 1)


def experts(nc, alloc, sem, w_gu, w_down, xn_d, moe_d, ident, wts):
    with ExitStack() as ctx:
        sb, pb = alloc(ctx)
        guh = sb("guh", [P, E, KD, 2 * F], F32R)
        gul = sb("gul", [P, E, KD, 2 * F], F32R)
        dh = sb("dh", [FH, E, 2, D], F32R)
        dl = sb("dl", [FH, E, 2, D], F32R)
        gur = [sb(f"gur{i}", [P, KD, 2 * F]) for i in range(1)]
        dr = [sb(f"dr{i}", [FH, 2, D]) for i in range(1)]
        xg = [sb(f"xg{i}", [P, D]) for i in range(2)]
        xgh = [sb(f"xgh{i}", [P, KD, P], F32R) for i in range(2)]
        xgl = [sb(f"xgl{i}", [P, KD, P], F32R) for i in range(2)]
        th = sb("th", [P, F])
        hg = sb("hg", [P, F])
        h = [sb(f"h{i}", [P, F]) for i in range(2)]
        hh = [sb(f"hh{i}", [FH, 2, P], F32R) for i in range(2)]
        hl = [sb(f"hl{i}", [FH, 2, P], F32R) for i in range(2)]
        wt = [sb(f"wt{i}", [P, E]) for i in range(2)]
        acc = [sb(f"acc{i}", [P, D]) for i in range(2)]
        px = [pb(f"px{i}", [P, KD, P]) for i in range(2)]
        pg = [pb(f"pg{i}", [P, 2 * F]) for i in range(2)]
        ph = [pb(f"ph{i}", [FH, 2, P]) for i in range(2)]
        pd = [pb(f"pd{i}", [P, D]) for i in range(2)]

        w_in = sem("ew_in")
        w_hi = sem("ew_hi")
        w_lo = sem("ew_lo")
        xg_in = [sem(f"xg_in{i}") for i in range(2)]
        xtr = sem("xtr")
        x_hi = sem("x_hi")
        x_lo = sem("x_lo")
        gu = sem("gu")
        th_done = sem("th_done")
        hg_done = sem("hg_done")
        h_done = sem("h_done")
        htr = sem("htr")
        h_hi = sem("h_hi")
        h_lo = sem("h_lo")
        down = sem("down")
        acc_done = sem("acc_done")
        wt_done = sem("wt_done")
        moe_out = [sem(f"moe_out{i}") for i in range(2)]
        block = ctx.enter_context(nc.Block())

        @block.sync
        def _(sp):
            for e in range(E):
                if e:
                    sp.wait_ge(w_lo, 2 * e)
                sp.dma_start(gur[0][:, :, :], w_gu[e]).then_inc(w_in, 16)
                sp.dma_start(dr[0][:, :, :], w_down[e]).then_inc(w_in, 16)
            with sp.Fori(0, T // 2) as i:
                for c in range(2):
                    sp.wait_ge(xtr, i * 2 + c + 1)
                    sp.dma_start(xg[c][:, :], xn_d[i * 2 + c]).then_inc(xg_in[c], 16)
                for c in range(2):
                    sp.wait_ge(acc_done, i * (2 * E) + (c + 1) * E + 2)
                    sp.dma_start(moe_d[i * 2 + c], acc[c][:, :]).then_inc(moe_out[c], 16)
            for c in range(2):
                sp.wait_ge(moe_out[c], 16 * (T // 2 + 1))

        @block.scalar
        def _(act):
            for e in range(E):
                act.wait_ge(w_in, 32 * (e + 1))
                act.copy(guh[:, e, :, :], gur[0][:, :, :]).then_inc(w_hi, 1)
                act.copy(dh[:, e, :, :], dr[0][:, :, :]).then_inc(w_hi, 1)
            with act.Fori(0, T // 2) as i:
                for c in range(2):
                    act.wait_ge(xtr, i * 2 + c + 3)
                    act.copy(xgh[c][:, :, :], px[c][:, :, :]).then_inc(x_hi, 1)
                    for e in range(E):
                        n = i * (2 * E) + (c * E + e)
                        act.wait_ge(gu, n + 1)
                        act.wait_ge(hg_done, n + 1)
                        act.activation(th[:, :], pg[e % 2][:, 0:F], ACT.Tanh, scale=0.5).then_inc(th_done, 1)
                        act.wait_ge(htr, n + 1)
                        act.copy(hh[e % 2][:, :, :], ph[e % 2][:, :, :]).then_inc(h_hi, 1)

        @block.vector
        def _(dve):
            dve.sem_inc(hg_done, 1)
            dve.sem_inc(h_lo, 2)
            dve.sem_inc(h_done, 2)
            dve.sem_inc(acc_done, 2)
            dve.sem_inc(x_lo, 2)
            for e in range(E):
                dve.wait_ge(w_hi, 2 * (e + 1))
                dve.tensor_tensor(gul[:, e, :, :], gur[0][:, :, :], guh[:, e, :, :].bitcast(F32),
                                  ALU.subtract).then_inc(w_lo, 1)
                dve.tensor_tensor(dl[:, e, :, :], dr[0][:, :, :], dh[:, e, :, :].bitcast(F32),
                                  ALU.subtract).then_inc(w_lo, 1)
            with dve.Fori(0, T // 2) as i:
                for c in range(2):
                    dve.wait_ge(x_hi, i * 2 + c + 1)
                    dve.tensor_tensor(xgl[c][:, :, :], px[c][:, :, :], xgh[c][:, :, :].bitcast(F32),
                                      ALU.subtract).then_inc(x_lo, 1)
                    dve.tensor_copy(wt[c][:, :], wts[:, bass.ds(i * 2 + c, 1), :].rearrange("p t e -> p (t e)")
                                    ).then_inc(wt_done, 1)
                    for e in range(E):
                        n = i * (2 * E) + (c * E + e)
                        dve.wait_ge(th_done, n + 1)
                        dve.scalar_tensor_tensor(out=hg[:, :], in0=th[:, :], scalar=1.0, in1=pg[e % 2][:, 0:F],
                                                 op0=ALU.add, op1=ALU.mult).then_inc(hg_done, 1)
                        dve.wait_ge(hg_done, n + 2)
                        dve.tensor_tensor(h[e % 2][:, :], hg[:, :], pg[e % 2][:, F:2 * F], ALU.mult).then_inc(h_done, 1)
                        dve.wait_ge(h_hi, n + 1)
                        dve.tensor_tensor(hl[e % 2][:, :, :], ph[e % 2][:, :, :], hh[e % 2][:, :, :].bitcast(F32),
                                          ALU.subtract).then_inc(h_lo, 1)
                        dve.wait_ge(down, n + 1)
                        if e == 0:
                            dve.wait_ge(wt_done, i * 2 + c + 1)
                            dve.wait_ge(moe_out[c], i * 16 + 16)
                            dve.tensor_scalar(acc[c][:, :], pd[e % 2][:, :], wt[c][:, 0:1], None,
                                              ALU.mult).then_inc(acc_done, 1)
                        else:
                            dve.wait_ge(acc_done, n + 2)
                            dve.scalar_tensor_tensor(out=acc[c][:, :], in0=pd[e % 2][:, :], scalar=wt[c][:, e:e + 1],
                                                     in1=acc[c][:, :], op0=ALU.mult, op1=ALU.add).then_inc(acc_done, 1)

        @block.gpsimd
        def _(pool):
            pool.sem_inc(moe_out[0], 16)
            pool.sem_inc(moe_out[1], 16)

        @block.tensor
        def _(pe):
            pe.sem_inc(xtr, 2)
            pe.wait_ge(w_lo, 2 * E)
            with pe.Fori(0, T // 2) as i:
                for c in range(2):
                    pe.wait_ge(xg_in[c], i * 16 + 16)
                    pe.wait_ge(x_lo, i * 2 + c + 1)
                    for k in range(KD):
                        tr = pe.transpose(px[c][:, k, :], xg[c][:, k * P:(k + 1) * P], ident[:, :])
                    tr.then_inc(xtr, 1)
                    pe.wait_ge(x_lo, i * 2 + c + 3)

                    def gate_up(e):
                        n = i * (2 * E) + (c * E + e)
                        pe.wait_ge(h_done, n + 1)
                        m = 0
                        for xx, ww in ((xgh, guh), (xgh, gul), (xgl, guh)):
                            for k in range(KD):
                                mm = pe.matmul(pg[e % 2][:, :], xx[c][:, k, :], ww[:, e, k, :],
                                               start=m == 0, stop=m == 11)
                                m += 1
                        mm.then_inc(gu, 1)

                    def finish(e):
                        n = i * (2 * E) + (c * E + e)
                        pe.wait_ge(h_done, n + 3)
                        pe.wait_ge(h_lo, n + 1)
                        for j in range(2):
                            tr = pe.transpose(ph[e % 2][:, j, :], h[e % 2][:, j * FH:(j + 1) * FH], ident[:, :])
                        tr.then_inc(htr, 1)
                        pe.wait_ge(h_lo, n + 3)
                        pe.wait_ge(acc_done, n + 1)
                        m = 0
                        for xx, ww in ((hh, dh), (hh, dl), (hl, dh)):
                            for j in range(2):
                                mm = pe.matmul(pd[e % 2][:, :], xx[e % 2][:, j, :], ww[:, e, j, :],
                                               start=m == 0, stop=m == 5)
                                m += 1
                        mm.then_inc(down, 1)

                    gate_up(0)
                    for e in range(E):
                        if e + 1 < E:
                            gate_up(e + 1)
                        finish(e)


def mamba(nc, alloc, sem, x, w_in, w_out_in, conv_w_in, conv_b_in, d_skip_in, norm_w_in,
          xth_d, xtl_d, cs_d, moe_d, ident, tri, cs_tok, dt_tok, out):
    NX, NZ = CB // 2, XB // 2
    NP = NX + NZ
    PAIRS = ((0, 1, 2, 3, 4), (5, 6, 7, 8))
    with ExitStack() as ctx:
        sb, pb = alloc(ctx)
        wh = sb("wh", [P, KD, (CB + XB) * P], F32R)
        wl = sb("wl", [P, KD, (CB + XB) * P], F32R)
        wo = sb("wo", [P, XB, D])
        conv_w = sb("conv_w", [P, CB, TAPS])
        conv_b = sb("conv_b", [P, CB])
        d_skip = sb("d_skip", [P, XB])
        norm_w = sb("norm_w", [P, XB])
        ones = sb("ones", [P, 1])
        nhalf = sb("nhalf1", [P, 1])
        xh = sb("xh", [P, KD, GT], F32R)
        xl = sb("xl", [P, KD, GT], F32R)
        HALO = TAPS - 1
        raw = sb("raw", [P, CB, HALO + GT])
        xs = [sb(f"xs{i}", [P, CB, GT]) for i in range(2)]
        zs = [sb(f"zs{i}", [P, XB, GT]) for i in range(2)]
        tx = [sb(f"tx{i}", [P, 2, GT]) for i in range(2)]
        tz = [sb(f"tz{i}", [P, 2, GT]) for i in range(2)]
        m = sb("m", [P, HEADS, P])
        e2 = sb("e2", [P, XB, P])
        cst = sb("cst", [P, HEADS])
        dec = sb("dec", [P, HEADS])
        cd = sb("cd", [P, HEADS])
        xdt = sb("xdt", [P, XB, 2, HD])
        xdd = sb("xdd", [P, XB, 2, HD])
        btok = sb("btok", [P, P])
        cbm = sb("cbm", [P, P])
        carry = sb("carry", [P, XB, 2, HD])
        y = sb("y", [P, XB, P])
        ysq = sb("ysq", [P, XB, P])
        var = sb("var", [P, 1])
        rstd = sb("rstdy", [P, 1])
        res = sb("res", [P, D])
        moe = sb("moe", [P, D])
        o = sb("o", [P, D])
        wraw = sb("wraw", [P, (CB + XB) * P])
        pi = [pb(f"pi{i}", [P, 2, GT]) for i in range(2)]
        pxb = [pb(f"pxb{i}", [P, 4, P]) for i in range(2)]
        py = [pb(f"py{i}", [P, 4, P]) for i in range(2)]
        pk = pb("pk", [P, 4, P])
        po = pb("po", [P, D])

        w_in_s = sem("w_in_s")
        w_hi = sem("w_hi")
        w_lo = sem("w_lo")
        c_in = sem("c_in")
        prep = sem("prep")
        nh_done = sem("nh_done_m")
        xg_in = sem("xg_in")
        bc_in = sem("bc_in")
        e2_in = sem("e2_in")
        res_in = sem("res_in")
        moe_in = sem("moe_in")
        in_full = sem("in_full")
        inx_free = sem("inx_free")
        tz_done = sem("tz_done")
        inz_free = sem("inz_free")
        halo = sem("halo")
        tap = sem("tap")
        ctap = sem("ctap")
        txd = sem("txd")
        xs_done = sem("xs_done")
        btr = sem("btr")
        btok_done = sem("btok_done")
        xtr = sem("xtr_m")
        xdt_done = sem("xdt_done")
        cst_done = sem("cst_done")
        dsub = sem("dsub")
        dec_done = sem("dec_done")
        seg = sem("seg")
        me = sem("me")
        e2_done = sem("e2_done")
        cbt = sem("cbt")
        cbm_done = sem("cbm_done")
        m_done = sem("m_done")
        xdd_done = sem("xdd_done")
        st = sem("st")
        yoff = sem("yoff")
        ydiag = sem("ydiag")
        ye = sem("ye")
        yd = sem("yd")
        cdec = sem("cdec")
        cadd = sem("cadd")
        yadd = sem("yadd")
        ygate = sem("ygate")
        ysqd = sem("ysqd")
        tree = sem("tree")
        op = sem("op")
        ss = sem("ss")
        var_done = sem("var_done")
        rstd_done = sem("rstd_done_m")
        res_done = sem("res_done")
        o_done = sem("o_done")
        o_out = sem("o_out")
        CR = 1
        block = ctx.enter_context(nc.Block())
        out_t = out.rearrange("(t p) d -> t p d", p=P)
        x_t = x.rearrange("(t p) d -> t p d", p=P)

        def groups(eng, body):
            body(0, 0)
            with eng.Fori(0, (G - 2) // 2) as i:
                body(i * 2 + 1, 1)
                body(i * 2 + 2, 0)
            body(G - 1, 1)

        def is_last(g):
            return isinstance(g, int) and g == G - 1

        @block.sync
        def _(sp):
            for k in range(KD):
                if k:
                    sp.wait_ge(w_lo, k)
                sp.dma_start(wraw[:, :], w_in[:, k, :]).then_inc(w_in_s, 16)
            sp.dma_start(wo[:, :, :], w_out_in).then_inc(c_in, 16)
            sp.dma_start(conv_w[:, :, :], conv_w_in).then_inc(c_in, 16)
            sp.dma_start(conv_b[:, :], conv_b_in).then_inc(c_in, 16)
            sp.dma_start(d_skip[:, :], d_skip_in).then_inc(c_in, 16)
            sp.dma_start(norm_w[:, :], norm_w_in).then_inc(c_in, 16)

            def load_x(g):
                sp.dma_start(xh[:, :, :].bitcast(F32), xth_d[g]).then_inc(xg_in, 16)
                sp.dma_start(xl[:, :, :].bitcast(F32), xtl_d[g]).then_inc(xg_in, 16)

            def load_decays(t):
                sp.dma_start(m[:, :, :], cs_d[t].unsqueeze(0).broadcast_to([P, HEADS, P])).then_inc(bc_in, 16)

            def load_decays2(t):
                for half in range(2):
                    sp.dma_start(e2[half * HD:(half + 1) * HD, :, :],
                                 cs_d[t][half * XB:(half + 1) * XB, :].unsqueeze(0).broadcast_to([HD, XB, P])
                                 ).then_inc(e2_in, 16)

            def store(t):
                sp.wait_ge(o_done, t + 1 + CR)
                sp.dma_start(out_t[t], o[:, :]).then_inc(o_out, 16)

            load_x(0)
            load_decays(0)
            load_decays2(0)
            sp.wait_ge(in_full, NP + CR)
            load_x(1)

            def body(g, par):
                for c in range(2):
                    t = g * 2 + c
                    if c == 0 and not (isinstance(g, int) and g in (0, G - 1)):
                        sp.wait_ge(in_full, g * NP + NP + CR)
                        load_x(g + 1)
                    if not (isinstance(t, int) and t == 0):
                        store(t - 1)
                    sp.dma_start(res[:, :], x_t[t]).then_inc(res_in, 16)
                    sp.dma_start(moe[:, :], moe_d[t]).then_inc(moe_in, 16)
                    if is_last(g) and c == 1:
                        continue
                    sp.wait_ge(ydiag, t * 2 + 2 + CR)
                    load_decays(t + 1)
                    sp.wait_ge(yadd, t + 1 + CR)
                    load_decays2(t + 1)

            groups(sp, body)
            store(T - 1)
            sp.wait_ge(o_out, 16 * T + 16)

        @block.gpsimd
        def _(pool):
            for s in (yadd, ygate, xdd_done, cdec, res_done, rstd_done):
                pool.sem_inc(s, CR)
            pool.sem_inc(tree, 3)
            pool.memset(nhalf[:, :], -0.5).then_inc(nh_done, 1)
            pool.wait_ge(nh_done, 1)

            def out_parts(t):
                pool.wait_ge(ysqd, t + 1 + CR)
                pool.tensor_tensor(ysq[:, 0:4, :], ysq[:, 0:4, :], ysq[:, 4:8, :], ALU.add).then_inc(tree, 1)
                pool.wait_ge(tree, t * 3 + 4)
                pool.tensor_tensor(ysq[:, 0:2, :], ysq[:, 0:2, :], ysq[:, 2:4, :], ALU.add).then_inc(tree, 1)
                pool.wait_ge(tree, t * 3 + 5)
                pool.tensor_tensor(ysq[:, 0:1, :], ysq[:, 0:1, :], ysq[:, 1:2, :], ALU.add).then_inc(tree, 1)
                pool.wait_ge(var_done, t + 1 + CR)
                pool.wait_ge(o_done, t + CR)
                pool.tensor_tensor(rstd[:, :], var[:, :], nhalf[:, :], ALU.pow).then_inc(rstd_done, 1)

            def body(g, par):
                for c in range(2):
                    t = g * 2 + c
                    first = isinstance(t, int) and t == 0
                    pool.wait_ge(xdt_done, t * 2 + 2 + CR)
                    pool.wait_ge(dec_done, t + 1 + CR)
                    pool.wait_ge(st, t + CR)
                    pool.tensor_tensor(xdd[:, :, :, :], xdt[:, :, :, :],
                                       dec[:, :].rearrange("p (a b) -> p b a", a=2).unsqueeze(3)
                                       .broadcast_to([P, XB, 2, HD]), ALU.mult).then_inc(xdd_done, 1)
                    if not first:
                        out_parts(t - 1)
                    pool.wait_ge(res_in, t * 16 + 16)
                    pool.wait_ge(moe_in, t * 16 + 16)
                    pool.tensor_tensor(res[:, :], res[:, :], moe[:, :], ALU.add).then_inc(res_done, 1)
                    pool.wait_ge(yoff, t * 2 + 2 + CR)
                    pool.wait_ge(cadd, t * 2 + CR)
                    pool.tensor_tensor(carry[:, :, :, :], carry[:, :, :, :],
                                       cd[:, :].rearrange("p (a b) -> p b a", a=2).unsqueeze(3)
                                       .broadcast_to([P, XB, 2, HD]), ALU.mult).then_inc(cdec, 1)
                    pool.wait_ge(yd, t * 2 + 2 + CR)
                    pool.wait_ge(ye, t * 2 + 2 + CR)
                    pool.tensor_tensor(y[:, :, :], y[:, :, :], e2[:, :, :], ALU.add).then_inc(yadd, 1)
                    pool.wait_ge(yadd, t + 1 + CR)
                    pool.wait_ge(inz_free, g * NZ + NZ + CR)
                    pool.tensor_tensor(y[:, :, :], y[:, :, :], zs[par][:, :, c * P:(c + 1) * P],
                                       ALU.mult).then_inc(ygate, 1)

            groups(pool, body)
            out_parts(T - 1)

        def stage_x_act(act, g, i, par):
            act.wait_ge(in_full, g * NP + i + 1 + CR)
            if i == 0:
                act.wait_ge(ctap, g * (3 * CB) + CR)
                act.copy(raw[:, :, 0:HALO], raw[:, :, GT:GT + HALO]).then_inc(halo, 1)
                act.wait_ge(halo, g + 1)
            act.copy(raw[:, 2 * i:2 * i + 2, HALO:HALO + GT], pi[i % 2][:, :, :]).then_inc(inx_free, 1)
            act.wait_ge(inx_free, g * NX + i + 1 + CR)
            for b in (2 * i, 2 * i + 1):
                act.activation(xs[par][:, b, :], raw[:, b, 0:GT], ACT.Identity, bias=conv_b[:, b:b + 1],
                               scale=conv_w[:, b, 0:1]).then_inc(tap, 1)

        def tanh_x_act(act, g, i, par):
            act.wait_ge(ctap, g * (3 * CB) + 6 * i + 6 + CR)
            act.wait_ge(xs_done, g * NX + i - 1 + CR) if i >= 2 or not (isinstance(g, int) and g == 0) else None
            act.activation(tx[i % 2][:, :, :], xs[par][:, 2 * i:2 * i + 2, :], ACT.Tanh).then_inc(txd, 1)

        def stage_z_act(act, g, i):
            act.wait_ge(in_full, g * NP + i + 1 + CR)
            j = i - NX
            act.wait_ge(inz_free, g * NZ + j - 1 + CR) if j >= 2 or not (isinstance(g, int) and g == 0) else None
            act.activation(tz[j % 2][:, :, :], pi[i % 2][:, :, :], ACT.Tanh, scale=0.5).then_inc(tz_done, 1)

        def stage_act(act, g, i, par):
            if i < NX:
                stage_x_act(act, g, i, par)
            else:
                stage_z_act(act, g, i)
            if 1 <= i <= NX:
                tanh_x_act(act, g, i - 1, par)

        def stage_dve(dve, g, i, par):
            if i < NX:
                for k in range(1, TAPS):
                    for b in (2 * i, 2 * i + 1):
                        n = 6 * i + 2 * (k - 1) + (b - 2 * i)
                        if k == 1:
                            dve.wait_ge(tap, g * CB + b + 1)
                        else:
                            dve.wait_ge(ctap, g * (3 * CB) + n - 1 + CR)
                        dve.scalar_tensor_tensor(out=xs[par][:, b, :], in0=raw[:, b, k:k + GT],
                                                 scalar=conv_w[:, b, k:k + 1], in1=xs[par][:, b, :],
                                                 op0=ALU.mult, op1=ALU.add).then_inc(ctap, 1)
            else:
                j = i - NX
                dve.wait_ge(tz_done, g * NZ + j + 1)
                dve.scalar_tensor_tensor(out=zs[par][:, 2 * j:2 * j + 2, :], in0=tz[j % 2][:, :, :], scalar=1.0,
                                         in1=pi[i % 2][:, :, :], op0=ALU.add, op1=ALU.mult).then_inc(inz_free, 1)
            if 1 <= i <= NX:
                j = i - 1
                dve.wait_ge(txd, g * NX + j + 1)
                dve.scalar_tensor_tensor(out=xs[par][:, 2 * j:2 * j + 2, :], in0=tx[j % 2][:, :, :], scalar=1.0,
                                         in1=xs[par][:, 2 * j:2 * j + 2, :], op0=ALU.add,
                                         op1=ALU.mult).then_inc(xs_done, 1)

        def stage_pe(pe, g, i):
            first = isinstance(g, int) and g == 0
            if i == 0:
                pe.wait_ge(xg_in, g * 32 + 32)
            if i < 2:
                if not first:
                    pe.wait_ge(inz_free, g * NZ - (i == 1) + CR)
            elif i - 2 < NX:
                pe.wait_ge(inx_free, g * NX + i - 1 + CR)
            else:
                pe.wait_ge(inz_free, g * NZ + i - 2 - NX + 1 + CR)
            for h in range(2):
                n = 0
                cols = slice((2 * i + h) * P, (2 * i + h + 1) * P)
                for ww, xx in ((wh, xh), (wl, xh), (wh, xl)):
                    for k in range(KD):
                        mm = pe.matmul(pi[i % 2][:, h, :], ww[:, k, cols], xx[:, k, :], start=n == 0, stop=n == 11)
                        n += 1
            mm.then_inc(in_full, 1)

        @block.scalar
        def _(act):
            for s in (inx_free, btok_done, dec_done, me, e2_done, ysqd):
                act.sem_inc(s, CR)
            for k in range(KD):
                act.wait_ge(w_in_s, 16 * (k + 1))
                act.copy(wh[:, k, :], wraw[:, :]).then_inc(w_hi, 1)
            act.wait_ge(prep, 5)
            for i in range(NP):
                stage_act(act, 0, i, 0)

            def square(t):
                act.wait_ge(ygate, t + 1 + CR)
                act.wait_ge(ss, t + CR)
                act.activation(ysq[:, :, :], y[:, :, :], ACT.Square).then_inc(ysqd, 1)

            def body(g, par):
                for c in range(2):
                    t = g * 2 + c
                    first = isinstance(t, int) and t == 0
                    act.wait_ge(btr, t + 1)
                    act.wait_ge(st, t + CR)
                    act.copy(btok[:, :], pk[:, 0, :]).then_inc(btok_done, 1)
                    act.wait_ge(dsub, t + 1)
                    act.wait_ge(xdd_done, t + CR)
                    act.activation(dec[:, :], dec[:, :], ACT.Exp)
                    act.wait_ge(cdec, t + CR)
                    act.activation(cd[:, :], m[:, :, P - 1], ACT.Exp).then_inc(dec_done, 1)
                    act.wait_ge(e2_in, t * 32 + 32)
                    act.activation(e2[:, :, :], e2[:, :, :], ACT.Exp).then_inc(e2_done, 1)
                    if not first:
                        square(t - 1)
                    act.wait_ge(dec_done, t + 1 + CR)
                    for h in range(HEADS):
                        act.activation(m[:, h, :], m[:, h, :], ACT.Relu, bias=cst[:, h:h + 1],
                                       scale=-1.0).then_inc(seg, 1)
                    act.wait_ge(seg, t * HEADS + HEADS)
                    act.activation(m[:, :, :], m[:, :, :], ACT.Exp, scale=-1.0).then_inc(me, 1)
                    if not is_last(g):
                        for i in PAIRS[c]:
                            stage_act(act, g + 1, i, 1 - par)

            groups(act, body)
            square(T - 1)

        @block.vector
        def _(dve):
            for s in (inz_free, xs_done, xdt_done, cbm_done, m_done, ye, yd, cadd, var_done, o_done, ctap):
                dve.sem_inc(s, CR)
            dve.sem_inc(o_out, 16)
            dve.memset(ones[:, :], 1.0).then_inc(prep, 1)
            dve.memset(carry[:, :, :, :], 0.0).then_inc(prep, 1)
            for k in range(KD):
                dve.wait_ge(w_hi, k + 1)
                dve.tensor_tensor(wl[:, k, :], wraw[:, :], wh[:, k, :].bitcast(F32), ALU.subtract).then_inc(w_lo, 1)
            dve.memset(raw[:, :, :], 0.0).then_inc(prep, 1)
            dve.wait_ge(c_in, 80)
            dve.tensor_scalar(conv_w[:, :, :], conv_w[:, :, :], 0.5, None, ALU.mult).then_inc(prep, 1)
            dve.tensor_scalar(conv_b[:, :], conv_b[:, :], 0.5, None, ALU.mult).then_inc(prep, 1)
            for b in range(XB):
                ins = dve.tensor_scalar(wo[:, b, :], wo[:, b, :], norm_w[:, b:b + 1], 0.5, ALU.mult, ALU.mult)
            ins.then_inc(prep, 1)
            for i in range(NP):
                stage_dve(dve, 0, i, 0)

            def body(g, par):
                for c in range(2):
                    t = g * 2 + c
                    tok = slice(c * P, (c + 1) * P)
                    first = isinstance(t, int) and t == 0
                    dve.wait_ge(bc_in, t * 16 + 16)
                    dve.wait_ge(me, t + CR)
                    dve.tensor_copy(cst[:, :], cs_tok[:, bass.ds(t, 1), :].rearrange("p t h -> p (t h)")
                                    ).then_inc(cst_done, 1)
                    dve.wait_ge(cst_done, t + 1)
                    dve.wait_ge(xdd_done, t + CR)
                    dve.tensor_tensor(dec[:, :], m[:, :, P - 1], cst[:, :], ALU.subtract).then_inc(dsub, 1)
                    dve.wait_ge(ydiag, t * 2 + CR)
                    for half in range(2):
                        dve.wait_ge(xtr, t * 2 + half + 1)
                        dve.tensor_tensor(
                            xdt[:, 4 * half:4 * half + 4, :, :],
                            pxb[half][:, :, :].rearrange("p b (a d) -> p b a d", a=2),
                            dt_tok[:, bass.ds(t, 1), :].rearrange("p t (a b) -> p (t b) a", a=2)
                            [:, 4 * half:4 * half + 4, :].unsqueeze(3).broadcast_to([P, 4, 2, HD]),
                            ALU.mult).then_inc(xdt_done, 1)
                    dve.wait_ge(cbt, t + 1)
                    dve.tensor_tensor(cbm[:, :], pk[:, 1, :], tri[:, :], ALU.mult).then_inc(cbm_done, 1)
                    pairs = PAIRS[c] if not is_last(g) else ()
                    for i in pairs[:2]:
                        stage_dve(dve, g + 1, i, 1 - par)
                    dve.wait_ge(me, t + 1 + CR)
                    dve.wait_ge(cbm_done, t + 1 + CR)
                    dve.tensor_tensor(m[:, :, :], m[:, :, :],
                                      cbm[:, :].unsqueeze(1).broadcast_to([P, HEADS, P]), ALU.mult).then_inc(m_done, 1)
                    if not first:
                        finish(t - 1)
                    dve.wait_ge(e2_done, t + 1 + CR)
                    for half in range(2):
                        blocks = slice(4 * half, 4 * half + 4)
                        dve.wait_ge(yoff, t * 2 + half + 1 + CR)
                        dve.tensor_tensor(e2[:, blocks, :], py[0][:, :, :], e2[:, blocks, :], ALU.mult).then_inc(ye, 1)
                        dve.wait_ge(ydiag, t * 2 + half + 1 + CR)
                        dve.wait_ge(op, t + CR)
                        dve.wait_ge(ysqd, t + CR)
                        for b in range(4 * half, 4 * half + 4):
                            ins = dve.scalar_tensor_tensor(
                                out=y[:, b, :], in0=xs[par][:, b, tok], scalar=d_skip[:, b:b + 1],
                                in1=py[1][:, b - 4 * half, :], op0=ALU.mult, op1=ALU.add)
                        ins.then_inc(yd, 1)
                        if half == 0:
                            for i in pairs[2:3]:
                                stage_dve(dve, g + 1, i, 1 - par)
                    dve.wait_ge(cdec, t + 1 + CR)
                    for half in range(2):
                        dve.wait_ge(st, t + 1 + CR)
                        sl = carry[:, 4 * half:4 * half + 4, :, :].rearrange("p b a d -> p (b a d)")
                        dve.tensor_tensor(sl, pxb[half][:, :, :].rearrange("p b l -> p (b l)"), sl,
                                          ALU.add).then_inc(cadd, 1)
                    for i in pairs[3:]:
                        stage_dve(dve, g + 1, i, 1 - par)

            def finish(t):
                dve.wait_ge(ss, t + 1 + CR)
                dve.tensor_scalar(var[:, :], pk[:, 2, 0:1], 0.25 / INNER, EPS, ALU.mult, ALU.add).then_inc(var_done, 1)
                dve.wait_ge(rstd_done, t + 1 + CR)
                dve.wait_ge(op, t + 1 + CR)
                dve.wait_ge(res_done, t + 1 + CR)
                dve.wait_ge(o_out, t * 16 + 16)
                dve.scalar_tensor_tensor(out=o[:, :], in0=po[:, :], scalar=rstd[:, 0:1], in1=res[:, :],
                                         op0=ALU.mult, op1=ALU.add).then_inc(o_done, 1)

            groups(dve, body)
            finish(T - 1)

        @block.tensor
        def _(pe):
            for s in (in_full, st, yoff, ydiag, op, ss):
                pe.sem_inc(s, CR)
            pe.wait_ge(w_lo, KD)
            for i in range(NP):
                stage_pe(pe, 0, i)
            pe.wait_ge(prep, 6)

            def project(t):
                pe.wait_ge(ygate, t + 1 + CR)
                pe.wait_ge(o_done, t + CR)
                for b in range(XB):
                    mm = pe.matmul(po[:, :], y[:, b, :], wo[:, b, :], start=b == 0, stop=b == XB - 1)
                mm.then_inc(op, 1)
                pe.wait_ge(tree, t * 3 + 6)
                pe.wait_ge(cbm_done, t + 2 + CR) if not (isinstance(t, int) and t == T - 1) else None
                pe.matmul(pk[:, 2, 0:1], ysq[:, 0, :], ones[:, :], start=True, stop=True).then_inc(ss, 1)

            def body(g, par):
                for c in range(2):
                    t = g * 2 + c
                    tok = slice(c * P, (c + 1) * P)
                    first = isinstance(t, int) and t == 0
                    pairs = PAIRS[c] if not is_last(g) else ()
                    pe.wait_ge(xs_done, g * NX + NX + CR)
                    pe.wait_ge(var_done, t - 1 + CR) if not first and not (isinstance(t, int) and t == 1) else None
                    pe.transpose(pk[:, 0, :], xs[par][:, XB, tok], ident[:, :]).then_inc(btr, 1)
                    pe.wait_ge(cadd, t * 2 + CR)
                    for half in range(2):
                        for b in range(4):
                            tr = pe.transpose(pxb[half][:, b, :], xs[par][:, 4 * half + b, tok], ident[:, :])
                        tr.then_inc(xtr, 1)
                    for i in pairs[:1]:
                        stage_pe(pe, g + 1, i)
                    pe.wait_ge(btok_done, t + 1 + CR)
                    pe.matmul(pk[:, 1, :], xs[par][:, XB, tok], xs[par][:, XB + 1, tok], start=True,
                              stop=True).then_inc(cbt, 1)
                    for i in pairs[1:2]:
                        stage_pe(pe, g + 1, i)
                    if not first:
                        project(t - 1)
                    for i in pairs[2:3]:
                        stage_pe(pe, g + 1, i)

                    def off(half):
                        pe.wait_ge(ye, t * 2 + half + CR)
                        for b in range(4):
                            cols = carry[:, 4 * half + b, :, :].rearrange("p a d -> p (a d)")
                            mm = pe.matmul(py[0][:, b, :], cols, xs[par][:, XB + 1, tok], start=True, stop=True)
                        mm.then_inc(yoff, 1)

                    def diag(half):
                        pe.wait_ge(yd, t * 2 + half + CR)
                        for b in range(4):
                            for a in range(2):
                                mm = pe.matmul(py[1][a * HD:(a + 1) * HD, b, :], xdt[:, 4 * half + b, a, :],
                                               m[:, a * XB + 4 * half + b, :], start=True, stop=True)
                        mm.then_inc(ydiag, 1)

                    off(0)
                    pe.wait_ge(xdd_done, t + 1 + CR)
                    for half in range(2):
                        mm = pe.matmul(pxb[half][:, :, :].rearrange("p b l -> p (b l)"), btok[:, :],
                                       xdd[:, 4 * half:4 * half + 4, :, :].rearrange("p b a d -> p (b a d)"),
                                       start=True, stop=True)
                    mm.then_inc(st, 1)
                    pe.wait_ge(m_done, t + 1 + CR)
                    diag(0)
                    for i in pairs[3:4]:
                        stage_pe(pe, g + 1, i)
                    off(1)
                    diag(1)
                    for i in pairs[4:]:
                        stage_pe(pe, g + 1, i)

            groups(pe, body)
            project(T - 1)


def kernel(**inputs):
    import numpy as np
    import concourse.bacc as bacc
    from concourse.bass_utils import run_bass_kernel_spmd as run

    a = {k: np.ascontiguousarray(v) for k, v in inputs.items()}
    w = a["L0_attn_in_proj_w"]
    zw, xw, dtw = w[:INNER], w[INNER:INNER + CB * P], w[INNER + CB * P:]

    def by_half(v):
        return v.reshape(XB, 2, -1).transpose(1, 0, 2).reshape(v.shape)

    def rows(wt, n):
        return np.ascontiguousarray(wt.reshape(n, P, -1).transpose(1, 0, 2))

    gu = np.concatenate([a["L0_ffn_w_gate_proj"], a["L0_ffn_w_up_proj"]], axis=1)
    arrays = {
        "x": a["L0_attn_u"].reshape(TOKENS, D),
        "w_in": rows(np.concatenate([xw, zw]).T, KD),
        "w_dtr": rows(np.concatenate([by_half(dtw), a["L0_ffn_w_gate_router"]]).T, KD),
        "w_out": rows(a["L0_attn_out_proj_w"].T, XB),
        "conv_w": rows(a["L0_attn_conv_w"], CB),
        "conv_b": np.ascontiguousarray(a["L0_attn_conv_b"].reshape(CB, P).T),
        "dt_bias": by_half(a["L0_attn_dt_bias"]).reshape(1, HEADS),
        "a_log": by_half(a["L0_attn_A_log"]).reshape(1, HEADS),
        "d_skip": np.ascontiguousarray(np.repeat(a["L0_attn_D_skip"], HD).reshape(XB, P).T),
        "norm_w": np.ascontiguousarray(a["L0_attn_norm_w"].reshape(XB, P).T),
        "w_gu": np.ascontiguousarray(gu.transpose(0, 2, 1).reshape(E, KD, P, 2 * F).transpose(0, 2, 1, 3)),
        "w_down": np.ascontiguousarray(a["L0_ffn_w_down_proj"].transpose(0, 2, 1).reshape(E, 2, FH, D)
                                       .transpose(0, 2, 1, 3)),
        "ident_in": np.eye(P, dtype=np.float32),
        "tri_in": np.triu(np.ones((P, P), np.float32)),
        "rank_in": np.arange(E, 0, -1, dtype=np.float32).reshape(1, E),
    }
    nc = bacc.Bacc("TRN2", target_bir_lowering=False, num_devices=1)
    args = [nc.dram_tensor(f"in_{n}", v.shape, F32, kind="ExternalInput").ap() for n, v in arrays.items()]
    args.append(nc.dram_tensor("out", (TOKENS, D), F32, kind="ExternalOutput").ap())
    front_and_rest(nc, *args)
    r = run(nc, [{f"in_{n}": v for n, v in arrays.items()}], core_ids=[0])
    return r.results[0]["out"].reshape(a["L0_attn_u"].shape)
```

```python
from contextlib import ExitStack

import concourse.bass as bass
from concourse import mybir

ALU = mybir.AluOpType
ACT = mybir.ActivationFunctionType
AX = mybir.AxisListType
F32 = mybir.dt.float32
F32R = mybir.dt.float32r
BF16 = mybir.dt.bfloat16
U32 = mybir.dt.uint32
I32 = mybir.dt.int32

P = 128
TOKENS, D = 2048, 512
KD = D // P
INNER, STATE, HEADS, HD, TAPS = 1024, 128, 16, 64, 4
XB = INNER // P
CB = XB + 2
E, F = 8, 192
FH = F // 2
T = TOKENS // P
G = T // 2
GT = 2 * P
C = HEADS + E
J = 2 * T + E
SIZES = {F32: 4, F32R: 4, BF16: 2, U32: 4, I32: 4}

ROW = {}
for _name, _n in (("rank", E), ("full", T), ("before", E * E), ("tile", J), ("iota", P), ("tok_tile", 2 * T)):
    ROW[_name] = slice(sum(s.stop - s.start for s in ROW.values()), sum(s.stop - s.start for s in ROW.values()) + _n)
ROW_N = max(s.stop for s in ROW.values())
EPS = 1e-5
BIG = 1.0e30


class Area:

    def __init__(self, nc, start, end):
        self.nc, self.at, self.end = nc, start, end

    def __call__(self, name, shape, dt=F32):
        size = SIZES[dt]
        for n in shape[1:]:
            size *= n
        at, self.at = self.at, self.at + (size + 31) // 32 * 32
        assert self.at <= self.end, (name, self.at, self.end)
        return self.nc.alloc_sbuf_tensor_at(name, shape, dt, offset=at)


def block(nc, x, w_in, w_dtr, w_out, conv_w, conv_b, dt_bias, a_log, d_skip, norm_w,
          w_gu, w_down, ident_in, tri_in, stri_in, row_in, part_in, out):
    ctx = ExitStack()
    with ctx:
        def sem(name):
            return ctx.enter_context(nc.semaphore(name))

        def dram(name, shape):
            return nc.dram_tensor(name, shape, F32, kind="Internal").ap()

        xn_d = dram("xn_d", (TOKENS, D))
        xth_d = dram("xth_d", (G, P, KD, GT))
        xtl_d = dram("xtl_d", (G, P, KD, GT))
        cs_d = dram("cs_d", (T, HEADS, P))
        y_d = dram("y_d", (J * P, D))

        start = (nc.sbuf_base + 63) // 32 * 32
        top = nc.sbuf_usable_end // 32 * 32
        weights_size = E * (KD * 2 * F + 2 * D) * 2 * 4
        lasting = Area(nc, start, top)
        ident = lasting("ident", [P, P])
        tri = lasting("tri", [P, P])
        cs_tok = lasting("cs_tok", [P, T, HEADS])
        dt_tok = lasting("dt_tok", [P, T, HEADS])
        slot_u = lasting("slot_u", [P, 2, T], U32)
        prob = lasting("prob", [P, 2, T])
        idx = lasting("idx", [P, J], U32)
        eidx = lasting("eidx", [1, J], I32)
        wts = Area(nc, top - weights_size, top)
        guh = wts("guh", [P, E, KD, 2 * F], F32R)
        gul = wts("gul", [P, E, KD, 2 * F], F32R)
        dh = wts("dh", [FH, E, 2, D], F32R)
        dl = wts("dl", [FH, E, 2, D], F32R)
        gu_size, d_size = KD * 2 * F * 4, 2 * D * 4
        odd_stage = (Area(nc, top - weights_size + E * gu_size + (E - 1) * gu_size, top)("gur1", [P, KD, 2 * F]),
                     Area(nc, top - d_size, top)("dr1", [FH, 2, D]))
        win_stage = Area(nc, lasting.at, top)("win_stage", [P, KD - 1, (CB + XB) * P])
        slice_size = (CB + XB) * P * 4
        stage_in = sem("stage_in")
        front_done = sem("front_done")

        with nc.Block() as engines:
            front_parts = front(nc, Area(nc, lasting.at, top - weights_size), sem, x, w_dtr, dt_bias, a_log,
                                w_gu, w_down, ident_in, tri_in, stri_in, row_in, part_in, xn_d, xth_d, xtl_d, cs_d,
                                ident, tri, cs_tok, dt_tok, slot_u, prob, idx, eidx, guh, gul, dh, dl, odd_stage, front_done)
            expert_parts = experts(nc, Area(nc, lasting.at + PRE * slice_size, top - weights_size), sem, w_in, win_stage, stage_in,
                                   xn_d, y_d, ident, idx, eidx, guh, gul, dh, dl, front_done)
            for name in ("sync", "gpsimd", "scalar", "vector", "tensor"):
                def both(eng, name=name):
                    front_parts[name](eng)
                    expert_parts[name](eng)
                {"sync": engines.sync, "gpsimd": engines.gpsimd, "scalar": engines.scalar,
                 "vector": engines.vector, "tensor": engines.tensor}[name](both)
        mamba(nc, Area(nc, lasting.at + (KD - 1) * slice_size, top), win_stage, stage_in, sem, x, w_in, w_out, conv_w, conv_b, d_skip,
              norm_w, xth_d, xtl_d, cs_d, y_d, ident, tri, cs_tok, dt_tok, slot_u, prob, out)


PRE = 2
CR = 1


def by_twos(eng, n, body):
    body(0, 0, 0)
    with eng.Fori(0, (n - 2) // 2) as i:
        body(i * 2 + 1, 1, i)
        body(i * 2 + 2, 0, i + 1)
    body(n - 1, 1, (n - 1) // 2)


def static(i, *values):
    return isinstance(i, int) and i in values


def front(nc, area, sem, x, w_dtr_in, dt_bias, a_log, w_gu, w_down, ident_in, tri_in, stri_in, row_in, part_in,
          xn_d, xth_d, xtl_d, cs_d, ident, tri, cs_tok, dt_tok, slot_u, prob, idx, eidx, guh, gul, dh, dl,
          odd_stage, front_done):
    with ExitStack() as ctx:
        sb = area

        def pb(name, shape):
            return ctx.enter_context(nc.psum_tensor(name, shape, F32))

        row = sb("row", [P, ROW_N])
        part = sb("part", [P, 1])
        stri = sb("stri", [P, P])
        stats = [sb(f"stats{i}", [P, 2, 6]) for i in range(2)]
        mv = sb("mv", [P, 2, 2])
        veps = sb("veps", [P, 2])
        rstd = sb("rstd", [P, 2])
        nhalf = sb("nhalf", [P, 2])
        wr = sb("wr", [P, KD, C])
        wrh = sb("wrh", [P, KD, C], F32R)
        wrl = sb("wrl", [P, KD, C], F32R)
        rt = sb("rt", [C, GT])
        rr = sb("rr", [P, T, C])
        bias_bc = sb("bias_bc", [P, HEADS])
        alog_bc = sb("alog_bc", [P, HEADS])
        a_bc = sb("a_bc", [P, HEADS])
        over = Area(nc, area.at, area.end)
        xin = [sb(f"xin{i}", [P, 2, D]) for i in range(2)]
        xth = [sb(f"xth{i}", [P, KD, GT], F32R) for i in range(2)]
        xtl = [sb(f"xtl{i}", [P, KD, GT], F32R) for i in range(2)]
        gur, dr = [sb("gur0", [P, KD, 2 * F]), odd_stage[0]], [sb("dr0", [FH, 2, D]), odd_stage[1]]
        big = [over(f"sp{i}", [P, T, HEADS]) for i in range(6)]
        e8 = [over(f"rt8_{i}", [P, T, E]) for i in range(5)]
        t1 = [over(f"rt1_{i}", [P, T]) for i in range(6)]
        cst_rows = over("cst_rows", [HEADS, T, P])
        ones_b = over("ones_b", [P, P], BF16)
        earlier = over("earlier", [P, T, E], BF16)
        sums = [over(f"sums{i}", [P, T, E], BF16) for i in range(2)]
        stri_b = over("stri_b", [P, P], BF16)
        picks = over("picks", [P, T, E], BF16)
        tot = over("tot", [P, E])
        gt = over("gt", [P, E, T])
        tiles = over("tiles", [P, E])
        base = over("base", [P, E])
        end = over("end", [P, E])
        slots = over("slots", [P, 2, T])
        hi_u = over("hi_u", [P, 2 * T], U32)
        lo_u = over("lo_u", [P, 2 * T], U32)
        hi_f = over("hi_f", [P, 2 * T])
        lo_f = over("lo_f", [P, 2 * T])
        in_tile = over("in_tile", [P, 2 * T, J], BF16)
        who = over("who", [P, 2 * T, 2 * J], BF16)
        place = over("place", [P, 2 * T, P], BF16)
        tokf = over("tokf", [P, J])
        ecmp = over("ecmp", [1, J, E])
        ef = over("ef", [1, J])
        pt = [pb(f"pt{i}", [P, KD, P]) for i in range(2)]
        pr = pb("pr", [C, GT])
        prt = pb("prt", [P, 2, C])
        pcs = pb("pcs", [P, T, HEADS])
        pct = pb("pct", [HEADS, 4, P])
        ppos = pb("ppos", [P, T, E])
        ptot = pb("ptot", [P, 128])
        ptok = ptot

        consts_in = sem("consts_in")
        x_in = [sem(f"x_in{i}") for i in range(2)]
        w_in = [sem(f"ew_in{i}") for i in range(2)]
        w_hi = sem("ew_hi")
        w_lo = sem("ew_lo")
        mv_done = sem("mv_done")
        rstd_done = sem("rstd_done")
        xn_done = sem("xn_done")
        xn_out = sem("xn_out")
        tr_done = sem("tr_done")
        hi_done = sem("hi_done")
        lo_done = sem("lo_done")
        xt_out = [sem(f"xt_out{i}") for i in range(2)]
        r_done = sem("r_done")
        rt_done = sem("rt_done")
        rtr_done = sem("rtr_done")
        rr_done = sem("rr_done")
        st_chain = sem("st_chain")
        setup = sem("f_setup")
        wrh_done = sem("wrh_done")
        a_done = sem("a_done")
        nh_done = sem("nh_done")
        e1 = sem("e1")
        b1 = sem("b1")
        rows_stored = sem("rows_stored")
        idx_done = sem("idx_done")
        picks_done = sem("picks_done")
        earlier_done = sem("earlier_done")
        pos_done = sem("pos_done")
        who_done = sem("who_done")
        tok_done = sem("tok_done")
        decay_done = sem("decay_done")
        cs_ready = sem("cs_ready")
        cs_copied = sem("cs_copied")
        ct_done = sem("ct_done")
        ct_copied = sem("ct_copied")
        cs_out = sem("cs_out")
        chain = sem("f_chain")
        NQ = T // 2
        assert NQ == E
        xr = x.rearrange("(q t p) d -> q p t d", p=P, t=2)
        xnr = xn_d.rearrange("(q t p) d -> q p t d", p=P, t=2)

        def sync(sp):
            sp.dma_start(xin[0][:, :, :], xr[0]).then_inc(x_in[0], 16)
            sp.dma_start(ident[:, :], ident_in).then_inc(consts_in, 16)
            sp.dma_start(wr[:, :, :], w_dtr_in).then_inc(consts_in, 16)
            sp.dma_start(row[:, :], row_in.broadcast_to([P, ROW_N])).then_inc(consts_in, 16)
            sp.dma_start(bias_bc[:, :], dt_bias.broadcast_to([P, HEADS])).then_inc(consts_in, 16)
            sp.dma_start(alog_bc[:, :], a_log.broadcast_to([P, HEADS])).then_inc(consts_in, 16)
            sp.dma_start(tri[:, :], tri_in).then_inc(consts_in, 16)
            sp.dma_start(stri[:, :], stri_in).then_inc(consts_in, 16)
            sp.dma_start(part[:, :], part_in).then_inc(consts_in, 16)

            def body(q, par, r):
                if not static(q, NQ - 1):
                    if not static(q, 0):
                        sp.wait_ge(xn_out, q * 16)
                    sp.dma_start(xin[1 - par][:, :, :], xr[q + 1]).then_inc(x_in[1 - par], 16)
                sp.wait_ge(xn_done, q + 1)
                sp.dma_start(xnr[q], xin[par][:, :, :]).then_inc(xn_out, 16)
                sp.wait_ge(lo_done, q * 2 + 2 + 2)
                sp.dma_start(xth_d[q], xth[par][:, :, :].bitcast(F32)).then_inc(xt_out[par], 16)
                sp.dma_start(xtl_d[q], xtl[par][:, :, :].bitcast(F32)).then_inc(xt_out[par], 16)

            by_twos(sp, NQ, body)
            for i in range(2):
                sp.wait_ge(xt_out[i], 32 * (NQ // 2) + i * 32)
            sp.wait_ge(xn_out, 16 * NQ)
            sp.sem_inc(rows_stored, 1)
            sp.wait_ge(ct_copied, 4)
            sp.dma_start(cs_d.rearrange("t h l -> h t l"), cst_rows[:, :, :]).then_inc(cs_out, 16)
            sp.wait_ge(cs_out, 16)

        def gpsimd(pool):
            pool.memset(nhalf[:, :], -0.5).then_inc(nh_done, 1)
            pool.wait_ge(nh_done, 1)
            for i in range(2):
                pool.dma_start(gur[i][:, :, :], w_gu[i]).then_inc(w_in[i], 16)
                pool.dma_start(dr[i][:, :, :], w_down[i]).then_inc(w_in[i], 16)

            def body(q, par, r):
                pool.wait_ge(mv_done, q + 1)
                pool.tensor_tensor(rstd[:, :], veps[:, :], nhalf[:, :], ALU.pow).then_inc(rstd_done, 1)
                if not static(q, 0, NQ - 1):
                    pool.wait_ge(w_lo, q * 2)
                    pool.dma_start(gur[1 - par][:, :, :], w_gu[q + 1]).then_inc(w_in[1 - par], 16)
                    pool.dma_start(dr[1 - par][:, :, :], w_down[q + 1]).then_inc(w_in[1 - par], 16)

            by_twos(pool, NQ, body)

        def scalar(act):
            act.wait_ge(consts_in, 16 * 8)
            act.copy(wrh[:, :, :], wr[:, :, :]).then_inc(wrh_done, 1)
            act.activation(a_bc[:, :], alog_bc[:, :], ACT.Exp).then_inc(a_done, 1)

            def body(q, par, r):
                for j in range(2):
                    act.wait_ge(tr_done, q * 2 + j + 1)
                    if j == 0 and not static(q, 0, 1):
                        if static(q, 2) or not isinstance(q, int) or q > 2:
                            pass
                        act.wait_ge(r_done, q)
                    if j == 0 and not static(q, 0):
                        act.wait_ge(xt_out[par], r * 32) if par == 0 else act.wait_ge(xt_out[1], r * 32 + 32)
                    act.copy(xth[par][:, :, j * P:(j + 1) * P], pt[j][:, :, :]).then_inc(hi_done, 1)
                act.wait_ge(w_in[par], r * 32 + 32)
                act.copy(guh[:, bass.ds(q, 1), :, :].rearrange("p e k n -> p (e k) n"), gur[par][:, :, :]
                         ).then_inc(w_hi, 1)
                act.copy(dh[:, bass.ds(q, 1), :, :].rearrange("p e k n -> p (e k) n"), dr[par][:, :, :]
                         ).then_inc(w_hi, 1)

            by_twos(act, NQ, body)
            act.wait_ge(b1, 1)
            act.activation(t1[2][:, :], t1[2][:, :], ACT.Exp).then_inc(e1, 1)
            act.wait_ge(b1, 2)
            act.activation(big[1][:, :, :], big[1][:, :, :], ACT.Exp).then_inc(e1, 1)
            for k in range(4):
                act.wait_ge(ct_done, k + 1)
                act.copy(cst_rows[:, 4 * k:4 * k + 4, :], pct[:, :, :]).then_inc(ct_copied, 1)

        def vector(dve):
            dve.sem_inc(lo_done, 2)
            dve.sem_inc(xt_out[1], 32)
            n_chain = [0]

            def link(ins):
                n_chain[0] += 1
                ins.then_inc(chain, 1)
                dve.wait_ge(chain, n_chain[0])

            def statistics(q, par, r):
                dve.wait_ge(x_in[par], r * 16 + 16)
                for j in range(2):
                    dve.bn_stats(stats[par][:, j, :], xin[par][:, j, :]).then_inc(st_chain, 1)
                at = q * 6 + 2
                dve.wait_ge(st_chain, at)
                even, odd = stats[par][:, :, 1], stats[par][:, :, 4]
                dve.tensor_tensor(mv[:, :, 0], even, odd, ALU.add).then_inc(st_chain, 1)
                dve.tensor_tensor(mv[:, :, 1], even, odd, ALU.subtract).then_inc(st_chain, 1)
                dve.tensor_tensor(veps[:, :], stats[par][:, :, 2], stats[par][:, :, 5], ALU.add).then_inc(st_chain, 1)
                dve.wait_ge(st_chain, at + 3)
                dve.tensor_scalar(mv[:, :, 0], mv[:, :, 0], 0.5, None, ALU.mult)
                dve.scalar_tensor_tensor(out=mv[:, :, 1], in0=mv[:, :, 1], scalar=0.25, in1=mv[:, :, 1],
                                         op0=ALU.mult, op1=ALU.mult)
                dve.tensor_scalar(veps[:, :], veps[:, :], 1.0 / D, EPS, ALU.mult, ALU.add).then_inc(st_chain, 1)
                dve.wait_ge(st_chain, at + 4)
                dve.tensor_tensor(veps[:, :], veps[:, :], mv[:, :, 1], ALU.add).then_inc(mv_done, 1)

            def projected(q):
                dve.wait_ge(r_done, q + 1)
                dve.tensor_copy(rt[:, :], pr[:, :]).then_inc(rt_done, 1)
                dve.wait_ge(rtr_done, q + 1)
                dve.tensor_copy(rr[:, bass.ds(q * 2, 2), :], prt[:, :, :]).then_inc(rr_done, 1)

            def body(q, par, r):
                dve.wait_ge(rstd_done, q + 1)
                for j in range(2):
                    ins = dve.tensor_scalar(xin[par][:, j, :], xin[par][:, j, :], mv[:, j, 0:1], rstd[:, j:j + 1],
                                            ALU.subtract, ALU.mult)
                ins.then_inc(xn_done, 1)
                if not static(q, NQ - 1):
                    dve.wait_ge(xn_done, q + 1)
                    statistics(q + 1, 1 - par, r + par)
                for j in range(2):
                    dve.wait_ge(hi_done, q * 2 + j + 1)
                    dve.tensor_tensor(xtl[par][:, :, j * P:(j + 1) * P], pt[j][:, :, :],
                                      xth[par][:, :, j * P:(j + 1) * P].bitcast(F32), ALU.subtract).then_inc(lo_done, 1)
                dve.wait_ge(w_hi, q * 2 + 2)
                dve.tensor_tensor(gul[:, bass.ds(q, 1), :, :].rearrange("p e k n -> p (e k) n"), gur[par][:, :, :],
                                  guh[:, bass.ds(q, 1), :, :].rearrange("p e k n -> p (e k) n").bitcast(F32),
                                  ALU.subtract).then_inc(w_lo, 1)
                dve.tensor_tensor(dl[:, bass.ds(q, 1), :, :].rearrange("p e k n -> p (e k) n"), dr[par][:, :, :],
                                  dh[:, bass.ds(q, 1), :, :].rearrange("p e k n -> p (e k) n").bitcast(F32),
                                  ALU.subtract).then_inc(w_lo, 1)
                if not static(q, 0):
                    projected(q - 1)

            statistics(0, 0, 0)
            dve.wait_ge(wrh_done, 1)
            dve.tensor_tensor(wrl[:, :, :], wr[:, :, :], wrh[:, :, :].bitcast(F32), ALU.subtract).then_inc(setup, 1)
            by_twos(dve, NQ, body)
            projected(NQ - 1)
            dve.wait_ge(rr_done, NQ)
            dve.wait_ge(w_lo, 2 * E)
            dve.wait_ge(xt_out[0], 32 * (NQ // 2))
            dve.wait_ge(xt_out[1], 32 * (NQ // 2) + 32)
            dve.wait_ge(xn_out, 16 * NQ)

            def per_tile(ap, n):
                return ap.unsqueeze(2).broadcast_to([P, T, n])

            sc = rr[:, :, HEADS:C]
            rank3 = row[:, ROW["rank"]].unsqueeze(1).broadcast_to([P, T, E])
            one1, one2, w1, rest, w2 = e8
            m1, i1, m2, p1, p2, i2 = t1
            link(dve.memset(ones_b[:, :], 1.0))
            link(dve.tensor_copy(stri_b[:, :], stri[:, :]))
            link(dve.tensor_reduce(m1[:, :], sc, AX.X, ALU.max))
            link(dve.tensor_tensor(w1[:, :, :], sc, per_tile(m1[:, :], E), ALU.is_equal))
            link(dve.tensor_tensor(w2[:, :, :], w1[:, :, :], rank3, ALU.mult))
            link(dve.tensor_reduce(i1[:, :], w2[:, :, :], AX.X, ALU.max))
            link(dve.tensor_tensor(one1[:, :, :], rank3, per_tile(i1[:, :], E), ALU.is_equal))
            link(dve.scalar_tensor_tensor(out=rest[:, :, :], in0=one1[:, :, :], scalar=-BIG, in1=sc,
                                          op0=ALU.mult, op1=ALU.add))
            link(dve.tensor_reduce(p2[:, :], rest[:, :, :], AX.X, ALU.max))
            link(dve.tensor_tensor(w1[:, :, :], rest[:, :, :], per_tile(p2[:, :], E), ALU.is_equal))
            link(dve.tensor_tensor(w2[:, :, :], w1[:, :, :], rank3, ALU.mult))
            link(dve.tensor_reduce(i2[:, :], w2[:, :, :], AX.X, ALU.max))
            link(dve.tensor_tensor(one2[:, :, :], rank3, per_tile(i2[:, :], E), ALU.is_equal))
            dve.tensor_tensor(picks[:, :, :], one1[:, :, :], one2[:, :, :], ALU.add).then_inc(picks_done, 1)
            dve.tensor_tensor(m2[:, :], p2[:, :], m1[:, :], ALU.subtract).then_inc(b1, 1)
            dve.wait_ge(picks_done, 1)
            link(dve.memset(earlier[:, 0:1, :], 0.0))
            link(dve.tensor_copy(sums[0][:, :, :], picks[:, :, :]))
            step, at = 1, 0
            while step < T // 2:
                link(dve.tensor_copy(sums[1 - at][:, 0:step, :], sums[at][:, 0:step, :]))
                link(dve.tensor_tensor(sums[1 - at][:, step:, :], sums[at][:, step:, :],
                                       sums[at][:, 0:T - step, :], ALU.add))
                step, at = step * 2, 1 - at
            link(dve.tensor_copy(earlier[:, 1:step + 1, :], sums[at][:, 0:step, :]))
            dve.tensor_tensor(earlier[:, step + 1:, :], sums[at][:, step:T - 1, :], sums[at][:, 0:T - 1 - step, :],
                              ALU.add).then_inc(earlier_done, 1)

            dve.wait_ge(pos_done, 1)
            link(dve.tensor_copy(tot[:, :], ptot[:, 0:E]))
            link(dve.tensor_tensor(gt[:, :, :], tot[:, :].unsqueeze(2).broadcast_to([P, E, T]),
                                   row[:, ROW["full"]].unsqueeze(1).broadcast_to([P, E, T]), ALU.is_gt))
            link(dve.tensor_reduce(tiles[:, :], gt[:, :, :], AX.X, ALU.add))
            link(dve.tensor_tensor(gt[:, :, 0:E], tiles[:, :].unsqueeze(1).broadcast_to([P, E, E]),
                                   row[:, ROW["before"]].rearrange("p (a b) -> p a b", a=E), ALU.mult))
            link(dve.tensor_reduce(base[:, :], gt[:, :, 0:E], AX.X, ALU.add))
            link(dve.tensor_tensor(end[:, :], base[:, :], tiles[:, :], ALU.add))
            link(dve.scalar_tensor_tensor(out=rest[:, :, :], in0=base[:, :].unsqueeze(1).broadcast_to([P, T, E]),
                                          scalar=float(P), in1=ppos[:, :, :], op0=ALU.mult, op1=ALU.add))
            for n, one in enumerate((one1, one2)):
                link(dve.tensor_tensor(w1[:, :, :], one[:, :, :], rest[:, :, :], ALU.mult))
                link(dve.tensor_reduce(slots[:, n, :], w1[:, :, :], AX.X, ALU.add))
            link(dve.tensor_copy(slot_u[:, :, :], slots[:, :, :]))
            flat_u = slot_u[:, :, :].rearrange("p k t -> p (k t)")
            link(dve.tensor_scalar(hi_u[:, :], flat_u, 7, None, ALU.logical_shift_right))
            link(dve.tensor_scalar(lo_u[:, :], flat_u, P - 1, None, ALU.bitwise_and))
            link(dve.tensor_copy(hi_f[:, :], hi_u[:, :]))
            link(dve.tensor_copy(lo_f[:, :], lo_u[:, :]))
            n2 = 2 * T
            link(dve.tensor_tensor(in_tile[:, :, :], hi_f[:, :].unsqueeze(2).broadcast_to([P, n2, J]),
                                   row[:, ROW["tile"]].unsqueeze(1).broadcast_to([P, n2, J]), ALU.is_equal))
            dve.tensor_tensor(who[:, :, 0:J], in_tile[:, :, :],
                              row[:, ROW["tok_tile"]].unsqueeze(2).broadcast_to([P, n2, J]), ALU.mult)
            dve.tensor_scalar(who[:, :, J:2 * J], in_tile[:, :, :], part[:, 0:1], None, ALU.mult)
            dve.tensor_tensor(place[:, :, :], lo_f[:, :].unsqueeze(2).broadcast_to([P, n2, P]),
                              row[:, ROW["iota"]].unsqueeze(1).broadcast_to([P, n2, P]),
                              ALU.is_equal).then_inc(who_done, 1)
            link(dve.tensor_tensor(ecmp[:, :, :], row[0:1, ROW["tile"]].unsqueeze(2).broadcast_to([1, J, E]),
                                   end[0:1, :].unsqueeze(1).broadcast_to([1, J, E]), ALU.is_ge))
            link(dve.tensor_reduce(ef[:, :], ecmp[:, :, :], AX.X, ALU.add))
            link(dve.tensor_scalar(ef[:, :], ef[:, :], float(E - 1), None, ALU.min))
            link(dve.tensor_copy(eidx[:, :], ef[:, :]))
            dve.wait_ge(tok_done, 1)
            link(dve.tensor_scalar(tokf[:, :], ptok[:, 0:J], float(P), None, ALU.mult))
            link(dve.tensor_tensor(tokf[:, :], tokf[:, :], ptok[:, J:2 * J], ALU.add))
            dve.tensor_copy(idx[:, :], tokf[:, :]).then_inc(idx_done, 1)

            dve.wait_ge(e1, 1)
            link(dve.tensor_scalar(p1[:, :], m2[:, :], 1.0, None, ALU.add))
            link(dve.reciprocal(i1[:, :], p1[:, :]))
            link(dve.tensor_scalar(prob[:, 0, :], i1[:, :], 0.5, None, ALU.mult))
            link(dve.tensor_tensor(prob[:, 1, :], prob[:, 0, :], m2[:, :], ALU.mult))

            v, ex, s, s2, acc, den = big
            bias3 = bias_bc[:, :].unsqueeze(1).broadcast_to([P, T, HEADS])
            link(dve.tensor_tensor(v[:, :, :], rr[:, :, 0:HEADS], bias3, ALU.add))
            dve.scalar_tensor_tensor(out=ex[:, :, :], in0=v[:, :, :], scalar=-1.0, in1=v[:, :, :],
                                     op0=ALU.mult, op1=ALU.min).then_inc(b1, 1)
            dve.wait_ge(e1, 2)
            link(dve.tensor_scalar(den[:, :, :], ex[:, :, :], 2.0, None, ALU.add))
            link(dve.reciprocal(acc[:, :, :], den[:, :, :]))
            link(dve.tensor_tensor(s[:, :, :], ex[:, :, :], acc[:, :, :], ALU.mult))
            link(dve.tensor_tensor(s2[:, :, :], s[:, :, :], s[:, :, :], ALU.mult))
            link(dve.tensor_scalar(acc[:, :, :], s2[:, :, :], 1.0 / 17, None, ALU.mult))
            for k in (15, 13, 11, 9, 7, 5, 3):
                link(dve.scalar_tensor_tensor(out=acc[:, :, :], in0=acc[:, :, :], scalar=1.0 / k, in1=s2[:, :, :],
                                              op0=ALU.add, op1=ALU.mult))
            link(dve.scalar_tensor_tensor(out=acc[:, :, :], in0=acc[:, :, :], scalar=1.0, in1=s[:, :, :],
                                          op0=ALU.add, op1=ALU.mult))
            link(dve.tensor_scalar(den[:, :, :], v[:, :, :], 0.0, None, ALU.max))
            link(dve.scalar_tensor_tensor(out=dt_tok[:, :, :], in0=acc[:, :, :], scalar=2.0, in1=den[:, :, :],
                                          op0=ALU.mult, op1=ALU.add))
            dve.wait_ge(a_done, 1)
            dve.scalar_tensor_tensor(out=s[:, :, :], in0=dt_tok[:, :, :], scalar=-1.0,
                                     in1=a_bc[:, :].unsqueeze(1).broadcast_to([P, T, HEADS]),
                                     op0=ALU.mult, op1=ALU.mult).then_inc(decay_done, 1)
            dve.wait_ge(cs_ready, 1)
            dve.tensor_copy(cs_tok[:, :, :], pcs[:, :, :]).then_inc(cs_copied, 1)

        def tensor(pe):
            pe.wait_ge(consts_in, 16 * 8)
            pe.wait_ge(setup, 1)

            def project(q, par):
                pe.wait_ge(lo_done, q * 2 + 2 + 2)
                if not static(q, 0):
                    pe.wait_ge(rt_done, q)
                n = 0
                for wx, xx in ((wrh, xth), (wrl, xth), (wrh, xtl)):
                    for k in range(KD):
                        mm = pe.matmul(pr[:, :], wx[:, k, :], xx[par][:, k, :], start=n == 0, stop=n == 11)
                        n += 1
                mm.then_inc(r_done, 1)
                pe.wait_ge(rt_done, q + 1)
                if not static(q, 0):
                    pe.wait_ge(rr_done, q)
                pe.matmul(prt[:, 0, :], rt[:, 0:P], ident[0:C, 0:C], start=True, stop=True)
                pe.transpose(prt[:, 1, :], rt[:, P:2 * P], ident[0:C, 0:C]).then_inc(rtr_done, 1)

            def body(q, par, r):
                pe.wait_ge(xn_done, q + 1)
                for j in range(2):
                    pe.wait_ge(lo_done, q * 2 + j + 1)
                    for k in range(KD):
                        tr = pe.transpose(pt[j][:, k, :], xin[par][:, j, k * P:(k + 1) * P], ident[:, :])
                    tr.then_inc(tr_done, 1)
                if not static(q, 0):
                    project(q - 1, 1 - par)

            by_twos(pe, NQ, body)
            project(NQ - 1, 1)

            pe.wait_ge(picks_done, 1)
            pe.matmul(ppos[:, :, :].rearrange("p t e -> p (t e)"), stri_b[:, :],
                      picks[:, :, :].rearrange("p t e -> p (t e)"), start=True, stop=False)
            pe.wait_ge(earlier_done, 1)
            pe.matmul(ppos[:, :, :].rearrange("p t e -> p (t e)"), ones_b[:, :],
                      earlier[:, :, :].rearrange("p t e -> p (t e)"), start=False, stop=True)
            for t in range(T):
                mm = pe.matmul(ptot[:, 0:E], ones_b[:, :], picks[:, t, :], start=t == 0, stop=t == T - 1)
            mm.then_inc(pos_done, 1)
            pe.wait_ge(who_done, 1)
            for n in range(2 * T):
                mm = pe.matmul(ptok[:, 0:2 * J], place[:, n, :], who[:, n, :], start=n == 0, stop=n == 2 * T - 1)
            mm.then_inc(tok_done, 1)

            pe.wait_ge(decay_done, 1)
            pe.matmul(pcs[:, :, :].rearrange("p t h -> p (t h)"), tri[:, :],
                      big[2][:, :, :].rearrange("p t h -> p (t h)"), start=True, stop=True).then_inc(cs_ready, 1)
            pe.wait_ge(cs_copied, 1)
            for k in range(4):
                if k:
                    pe.wait_ge(ct_copied, k)
                for j in range(4):
                    tr = pe.transpose(pct[:, j, :], cs_tok[:, 4 * k + j, :], ident[:, :])
                tr.then_inc(ct_done, 1)

        front.rows_stored, front.idx_done, front.cs_out = rows_stored, idx_done, cs_out
        return {"sync": sync, "gpsimd": gpsimd, "scalar": scalar, "vector": vector, "tensor": tensor}


def experts(nc, area, sem, w_in, win_stage, stage_in, xn_d, y_d, ident, idx, eidx, guh, gul, dh, dl, front_done):
    with ExitStack() as ctx:
        sb = area

        def pb(name, shape):
            return ctx.enter_context(nc.psum_tensor(name, shape, F32))

        xg = [sb(f"xg{i}", [P, D]) for i in range(2)]
        xgh = [sb(f"xgh{i}", [P, KD, P], F32R) for i in range(2)]
        xgl = [sb(f"xgl{i}", [P, KD, P], F32R) for i in range(2)]
        ic = [sb(f"ic{i}", [P, 1], U32) for i in range(2)]
        th = sb("th", [P, F])
        hg = sb("hg", [P, F])
        h = sb("h", [P, F])
        hh = [sb(f"hh{i}", [FH, 2, P], F32R) for i in range(2)]
        hl = [sb(f"hl{i}", [FH, 2, P], F32R) for i in range(2)]
        yo = [sb(f"yo{i}", [P, D]) for i in range(2)]
        px = [pb(f"px{i}", [P, KD, P]) for i in range(2)]
        pg = [pb(f"pg{i}", [P, 2 * F]) for i in range(2)]
        ph = [pb(f"ph{i}", [FH, 2, P]) for i in range(2)]
        pd = [pb(f"pd{i}", [P, D]) for i in range(2)]

        ic_done = sem("ic_done")
        ic_ready = sem("ic_ready")
        xg_in = [sem(f"xg_in{i}") for i in range(2)]
        xtr = sem("xtr")
        x_hi = sem("x_hi")
        x_lo = sem("x_lo")
        gu = sem("gu")
        th_done = sem("th_done")
        hg_done = sem("hg_done")
        h_done = sem("h_done")
        htr = sem("htr")
        h_hi = sem("h_hi")
        h_lo = sem("h_lo")
        down = sem("down")
        y_done = sem("y_done")
        y_out = [sem(f"y_out{i}") for i in range(2)]
        y_t = y_d.rearrange("(j p) d -> j p d", p=P)

        def sync(sp):
            sp.wait_ge(front_done, 1)
            for k in range(PRE):
                sp.dma_start(win_stage[:, k, :], w_in[:, k, :]).then_inc(stage_in, 16)

            def body(j, par, r):
                sp.wait_ge(y_done, j + 1 + CR)
                sp.dma_start(y_t[j], yo[par][:, :]).then_inc(y_out[par], 16)

            by_twos(sp, J, body)
            for i in range(2):
                sp.wait_ge(y_out[i], 16 * (J // 2) + 16)

        def gpsimd(pool):
            pool.wait_ge(front.rows_stored, 1)
            pool.wait_ge(front.idx_done, 1)
            pool.wait_ge(front_done, 1)

            def body(j, par, r):
                pool.wait_ge(xtr, j + CR - 1) if not static(j, 0) else None
                pool.tensor_copy(ic[par][:, :], idx[:, bass.ds(j, 1)]).then_inc(ic_done, 1)
                pool.wait_ge(ic_done, j + 1)
                pool.sem_inc(ic_ready, 1)
                pool.indirect_dma_start(xg[par][:, :], None, xn_d,
                                        bass.IndirectOffsetOnAxis(ap=ic[par][:, 0:1], axis=0)).then_inc(xg_in[par], 16)

            by_twos(pool, J, body)

        def scalar(act):
            act.sem_inc(y_done, CR)

            def high(j, par):
                act.wait_ge(xtr, j + 1 + CR)
                act.copy(xgh[par][:, :, :], px[par][:, :, :]).then_inc(x_hi, 1)

            def result(j, par, r):
                act.wait_ge(down, j + 1 + CR)
                act.wait_ge(y_out[par], r * 16 + 16)
                act.copy(yo[par][:, :], pd[par][:, :]).then_inc(y_done, 1)

            def body(j, par, r):
                act.wait_ge(gu, j + 1)
                act.wait_ge(hg_done, j + CR)
                act.activation(th[:, :], pg[par][:, 0:F], ACT.Tanh, scale=0.5).then_inc(th_done, 1)
                if not static(j, J - 1):
                    high(j + 1, 1 - par)
                if not static(j, 0):
                    result(j - 1, 1 - par, r - 1 + par)
                act.wait_ge(htr, j + 1)
                act.copy(hh[par][:, :, :], ph[par][:, :, :]).then_inc(h_hi, 1)

            high(0, 0)
            by_twos(act, J, body)
            result(J - 1, 1, J // 2 - 1)

        def vector(dve):
            dve.wait_ge(front.cs_out, 16)
            dve.sem_inc(front_done, 1)
            for s in (hg_done, x_lo):
                dve.sem_inc(s, CR)
            dve.sem_inc(h_lo, 2)
            dve.sem_inc(h_done, 2)
            for i in range(2):
                dve.sem_inc(y_out[i], 16)

            def low(j, par):
                dve.wait_ge(x_hi, j + 1)
                dve.tensor_tensor(xgl[par][:, :, :], px[par][:, :, :], xgh[par][:, :, :].bitcast(F32),
                                  ALU.subtract).then_inc(x_lo, 1)

            def body(j, par, r):
                dve.wait_ge(th_done, j + 1)
                dve.scalar_tensor_tensor(out=hg[:, :], in0=th[:, :], scalar=1.0, in1=pg[par][:, 0:F],
                                         op0=ALU.add, op1=ALU.mult).then_inc(hg_done, 1)
                dve.wait_ge(hg_done, j + 1 + CR)
                dve.wait_ge(htr, j) if not static(j, 0) else None
                dve.tensor_tensor(h[:, :], hg[:, :], pg[par][:, F:2 * F], ALU.mult).then_inc(h_done, 1)
                if not static(j, J - 1):
                    low(j + 1, 1 - par)
                dve.wait_ge(h_hi, j + 1)
                dve.tensor_tensor(hl[par][:, :, :], ph[par][:, :, :], hh[par][:, :, :].bitcast(F32),
                                  ALU.subtract).then_inc(h_lo, 1)

            low(0, 0)
            by_twos(dve, J, body)

        def tensor(pe):
            pe.sem_inc(xtr, CR)
            pe.sem_inc(down, CR)
            pe.wait_ge(front_done, 1)

            def turn(j, par, r):
                pe.wait_ge(xg_in[par], r * 16 + 16)
                pe.wait_ge(x_lo, j - 1 + CR) if not static(j, 0) else None
                for k in range(KD):
                    tr = pe.transpose(px[par][:, k, :], xg[par][:, k * P:(k + 1) * P], ident[:, :])
                tr.then_inc(xtr, 1)

            def of(ww, e, k):
                return ww[:, bass.ds(e, 1), k, :].rearrange("p e n -> p (e n)")

            def gate_up(j, par, e):
                pe.wait_ge(x_lo, j + 1 + CR)
                pe.wait_ge(h_done, j + 1)
                n = 0
                for xx, ww in ((xgh, guh), (xgh, gul), (xgl, guh)):
                    for k in range(KD):
                        mm = pe.matmul(pg[par][:, :], xx[par][:, k, :], of(ww, e, k), start=n == 0, stop=n == 11)
                        n += 1
                mm.then_inc(gu, 1)

            def down_product(j, par, e):
                pe.wait_ge(h_lo, j + 3)
                pe.wait_ge(y_done, j - 1 + CR) if not static(j, 0) else None
                n = 0
                for xx, ww in ((hh, dh), (hh, dl), (hl, dh)):
                    for k in range(2):
                        mm = pe.matmul(pd[par][:, :], xx[par][:, k, :], of(ww, e, k), start=n == 0, stop=n == 5)
                        n += 1
                mm.then_inc(down, 1)

            def turn_hidden(j, par):
                pe.wait_ge(h_done, j + 3)
                pe.wait_ge(h_lo, j + 1)
                for k in range(2):
                    tr = pe.transpose(ph[par][:, k, :], h[:, k * FH:(k + 1) * FH], ident[:, :])
                tr.then_inc(htr, 1)

            def expert_of(j):
                return pe.value_load(eidx[0:1, bass.ds(j, 1)], min_val=0, max_val=E - 1)

            def body(j, par, r):
                gate_up(j, par, expert_of(j))
                if not static(j, J - 1):
                    turn(j + 1, 1 - par, r + par)
                if not static(j, 0):
                    down_product(j - 1, 1 - par, expert_of(j - 1))
                turn_hidden(j, par)

            turn(0, 0, 0)
            by_twos(pe, J, body)
            down_product(J - 1, 1, expert_of(J - 1))

        return {"sync": sync, "gpsimd": gpsimd, "scalar": scalar, "vector": vector, "tensor": tensor}


def mamba(nc, area, win_stage, stage_in, sem, x, w_in, w_out_in, conv_w_in, conv_b_in, d_skip_in, norm_w_in,
          xth_d, xtl_d, cs_d, y_d, ident, tri, cs_tok, dt_tok, slot_u, prob, out):
    NX, NZ = CB // 2, XB // 2
    NP = NX + NZ
    PAIRS = ((0, 1, 2, 3, 4), (5, 6, 7, 8))
    with ExitStack() as ctx:
        sb = area

        def pb(name, shape):
            return ctx.enter_context(nc.psum_tensor(name, shape, F32))

        flat = win_stage[:, :, :].rearrange("p k n -> p (k n)")
        sizes = (HEADS * P, INNER, INNER, INNER, INNER)
        starts = [sum(sizes[:n]) for n in range(len(sizes))]
        wh = sb("wh", [P, KD, (CB + XB) * P], F32R)
        wl = sb("wl", [P, KD, (CB + XB) * P], F32R)
        wo = sb("wo", [P, XB, D])
        conv_w = sb("conv_w", [P, CB, TAPS])
        conv_b = sb("conv_b", [P, CB])
        d_skip = sb("d_skip", [P, XB])
        norm_w = sb("norm_w", [P, XB])
        ones = sb("ones", [P, 1])
        nhalf = sb("nhalf1", [P, 1])
        xh = sb("xh", [P, KD, GT], F32R)
        xl = sb("xl", [P, KD, GT], F32R)
        HALO = TAPS - 1
        raw = sb("raw", [P, CB, HALO + GT])
        xs = [sb(f"xs{i}", [P, CB, GT]) for i in range(2)]
        zs = [sb(f"zs{i}", [P, XB, GT]) for i in range(2)]
        tx = [sb(f"tx{i}", [P, 2, GT]) for i in range(2)]
        tz = [sb(f"tz{i}", [P, 2, GT]) for i in range(2)]
        m = flat[:, starts[0]:starts[0] + HEADS * P].rearrange("p (h l) -> p h l", h=HEADS)
        e2 = sb("e2", [P, XB, P])
        cst = sb("cst", [P, HEADS])
        dec = sb("dec", [P, HEADS])
        cd = sb("cd", [P, HEADS])
        xdt = flat[:, starts[1]:starts[1] + INNER].rearrange("p (b a d) -> p b a d", b=XB, a=2)
        xdd = flat[:, starts[2]:starts[2] + INNER].rearrange("p (b a d) -> p b a d", b=XB, a=2)
        btok = sb("btok", [P, P])
        cbm = sb("cbm", [P, P])
        carry = sb("carry", [P, XB, 2, HD])
        y = flat[:, starts[3]:starts[3] + INNER].rearrange("p (b l) -> p b l", b=XB)
        ysq = flat[:, starts[4]:starts[4] + INNER].rearrange("p (b l) -> p b l", b=XB)
        var = sb("var", [P, 1])
        rstd = sb("rstdy", [P, 1])
        res = sb("res", [P, D])
        ya = [sb(f"ya{i}", [P, D]) for i in range(2)]
        pwt = sb("pwt", [P, 2])
        sidx = sb("sidx", [P, 2], U32)
        o = sb("o", [P, D])
        wlast = sb("wlast", [P, (CB + XB) * P])
        wraw = [win_stage[:, k, :] for k in range(KD - 1)] + [wlast[:, :]]
        pi = [pb(f"pi{i}", [P, 2, GT]) for i in range(2)]
        pxb = [pb(f"pxb{i}", [P, 4, P]) for i in range(2)]
        py = [pb(f"py{i}", [P, 4, P]) for i in range(2)]
        pk = pb("pk", [P, 4, P])
        po = pb("po", [P, D])

        w_in_s = [sem(f"w_in_s{k}") for k in range(PRE, KD)]
        w_hi = sem("w_hi")
        w_lo = sem("w_lo")
        c_in = sem("c_in")
        prep = sem("prep")
        nh_done = sem("nh_done_m")
        xg_in = sem("xg_in")
        bc_in = sem("bc_in")
        e2_in = sem("e2_in")
        res_in = sem("res_in")
        ya_in = [sem(f"ya_in{i}") for i in range(2)]
        sidx_done = sem("sidx_done")
        sidx_ready = sem("sidx_ready")
        pw_done = sem("pw_done")
        ra_done = sem("ra_done")
        in_full = sem("in_full")
        inx_free = sem("inx_free")
        tz_done = sem("tz_done")
        inz_free = sem("inz_free")
        halo = sem("halo")
        tap = sem("tap")
        ctap = sem("ctap")
        txd = sem("txd")
        xs_done = sem("xs_done")
        btr = sem("btr")
        btok_done = sem("btok_done")
        xtr = sem("xtr_m")
        xdt_done = sem("xdt_done")
        cst_done = sem("cst_done")
        dsub = sem("dsub")
        dec_done = sem("dec_done")
        seg = sem("seg")
        me = sem("me")
        e2_done = sem("e2_done")
        cbt = sem("cbt")
        cbm_done = sem("cbm_done")
        m_done = sem("m_done")
        xdd_done = sem("xdd_done")
        st = sem("st")
        yoff = sem("yoff")
        ydiag = sem("ydiag")
        ye = sem("ye")
        yd = sem("yd")
        cdec = sem("cdec")
        cadd = sem("cadd")
        yadd = sem("yadd")
        ygate = sem("ygate")
        ysqd = sem("ysqd")
        tree = sem("tree")
        op = sem("op")
        ss = sem("ss")
        var_done = sem("var_done")
        rstd_done = sem("rstd_done_m")
        res_done = sem("res_done")
        o_done = sem("o_done")
        o_out = sem("o_out")
        CR = 1
        block = ctx.enter_context(nc.Block())
        out_t = out.rearrange("(t p) d -> t p d", p=P)
        x_t = x.rearrange("(t p) d -> t p d", p=P)

        def groups(eng, body):
            body(0, 0)
            with eng.Fori(0, (G - 2) // 2) as i:
                body(i * 2 + 1, 1)
                body(i * 2 + 2, 0)
            body(G - 1, 1)

        def is_last(g):
            return isinstance(g, int) and g == G - 1

        @block.sync
        def _(sp):
            for k in range(PRE, KD):
                sp.dma_start(wraw[k], w_in[:, k, :]).then_inc(w_in_s[k - PRE], 16)
            sp.dma_start(wo[:, :, :], w_out_in).then_inc(c_in, 16)
            sp.dma_start(conv_w[:, :, :], conv_w_in).then_inc(c_in, 16)
            sp.dma_start(conv_b[:, :], conv_b_in).then_inc(c_in, 16)
            sp.dma_start(d_skip[:, :], d_skip_in).then_inc(c_in, 16)
            sp.dma_start(norm_w[:, :], norm_w_in).then_inc(c_in, 16)

            def load_x(g):
                sp.dma_start(xh[:, :, :].bitcast(F32), xth_d[g]).then_inc(xg_in, 16)
                sp.dma_start(xl[:, :, :].bitcast(F32), xtl_d[g]).then_inc(xg_in, 16)

            def load_decays(t):
                sp.dma_start(m[:, :, :], cs_d[t].unsqueeze(0).broadcast_to([P, HEADS, P])).then_inc(bc_in, 16)

            def load_decays2(t):
                for half in range(2):
                    sp.dma_start(e2[half * HD:(half + 1) * HD, :, :],
                                 cs_d[t][half * XB:(half + 1) * XB, :].unsqueeze(0).broadcast_to([HD, XB, P])
                                 ).then_inc(e2_in, 16)

            def store(t):
                sp.wait_ge(o_done, t + 1 + CR)
                sp.dma_start(out_t[t], o[:, :]).then_inc(o_out, 16)

            load_x(0)
            load_decays2(0)
            sp.wait_ge(w_lo, KD - 1)
            load_decays(0)
            sp.wait_ge(in_full, NP + CR)
            load_x(1)

            def body(g, par):
                for c in range(2):
                    t = g * 2 + c
                    if c == 0 and not (isinstance(g, int) and g in (0, G - 1)):
                        sp.wait_ge(in_full, g * NP + NP + CR)
                        load_x(g + 1)
                    if not (isinstance(t, int) and t == 0):
                        store(t - 1)
                    sp.dma_start(res[:, :], x_t[t]).then_inc(res_in, 16)
                    if is_last(g) and c == 1:
                        continue
                    sp.wait_ge(ydiag, t * 2 + 2 + CR)
                    load_decays(t + 1)
                    sp.wait_ge(yadd, t + 1 + CR)
                    load_decays2(t + 1)

            groups(sp, body)
            store(T - 1)
            sp.wait_ge(o_out, 16 * T + 16)

        @block.gpsimd
        def _(pool):
            for s in (yadd, ygate, xdd_done, cdec, rstd_done):
                pool.sem_inc(s, CR)
            pool.sem_inc(tree, 3)
            pool.memset(nhalf[:, :], -0.5).then_inc(nh_done, 1)
            pool.wait_ge(nh_done, 1)

            def out_parts(t):
                pool.wait_ge(ysqd, t + 1 + CR)
                pool.tensor_tensor(ysq[:, 0:4, :], ysq[:, 0:4, :], ysq[:, 4:8, :], ALU.add).then_inc(tree, 1)
                pool.wait_ge(tree, t * 3 + 4)
                pool.tensor_tensor(ysq[:, 0:2, :], ysq[:, 0:2, :], ysq[:, 2:4, :], ALU.add).then_inc(tree, 1)
                pool.wait_ge(tree, t * 3 + 5)
                pool.tensor_tensor(ysq[:, 0:1, :], ysq[:, 0:1, :], ysq[:, 1:2, :], ALU.add).then_inc(tree, 1)
                pool.wait_ge(var_done, t + 1 + CR)
                pool.wait_ge(o_done, t + CR)
                pool.tensor_tensor(rstd[:, :], var[:, :], nhalf[:, :], ALU.pow).then_inc(rstd_done, 1)

            def body(g, par):
                for c in range(2):
                    t = g * 2 + c
                    first = isinstance(t, int) and t == 0
                    pool.wait_ge(xdt_done, t * 2 + 2 + CR)
                    pool.wait_ge(dec_done, t + 1 + CR)
                    pool.wait_ge(st, t + CR)
                    pool.tensor_tensor(xdd[:, :, :, :], xdt[:, :, :, :],
                                       dec[:, :].rearrange("p (a b) -> p b a", a=2).unsqueeze(3)
                                       .broadcast_to([P, XB, 2, HD]), ALU.mult).then_inc(xdd_done, 1)
                    if not first:
                        out_parts(t - 1)
                    if not first:
                        pool.wait_ge(res_done, t + CR)
                    pool.tensor_copy(sidx[:, :], slot_u[:, :, bass.ds(t, 1)].rearrange("p k t -> p (k t)")
                                     ).then_inc(sidx_done, 1)
                    pool.wait_ge(sidx_done, t + 1)
                    pool.sem_inc(sidx_ready, 1)
                    for n in range(2):
                        pool.indirect_dma_start(ya[n][:, :], None, y_d, bass.IndirectOffsetOnAxis(ap=sidx[:, n:n + 1], axis=0)
                                                ).then_inc(ya_in[n], 16)
                    pool.wait_ge(yoff, t * 2 + 2 + CR)
                    pool.wait_ge(cadd, t * 2 + CR)
                    pool.tensor_tensor(carry[:, :, :, :], carry[:, :, :, :],
                                       cd[:, :].rearrange("p (a b) -> p b a", a=2).unsqueeze(3)
                                       .broadcast_to([P, XB, 2, HD]), ALU.mult).then_inc(cdec, 1)
                    pool.wait_ge(yd, t * 2 + 2 + CR)
                    pool.wait_ge(ye, t * 2 + 2 + CR)
                    pool.tensor_tensor(y[:, :, :], y[:, :, :], e2[:, :, :], ALU.add).then_inc(yadd, 1)
                    pool.wait_ge(yadd, t + 1 + CR)
                    pool.wait_ge(inz_free, g * NZ + NZ + CR)
                    pool.tensor_tensor(y[:, :, :], y[:, :, :], zs[par][:, :, c * P:(c + 1) * P],
                                       ALU.mult).then_inc(ygate, 1)

            groups(pool, body)
            out_parts(T - 1)

        def stage_x_act(act, g, i, par):
            act.wait_ge(in_full, g * NP + i + 1 + CR)
            if i == 0:
                act.wait_ge(ctap, g * (3 * CB) + CR)
                act.copy(raw[:, :, 0:HALO], raw[:, :, GT:GT + HALO]).then_inc(halo, 1)
                act.wait_ge(halo, g + 1)
            act.copy(raw[:, 2 * i:2 * i + 2, HALO:HALO + GT], pi[i % 2][:, :, :]).then_inc(inx_free, 1)
            act.wait_ge(inx_free, g * NX + i + 1 + CR)
            for b in (2 * i, 2 * i + 1):
                act.activation(xs[par][:, b, :], raw[:, b, 0:GT], ACT.Identity, bias=conv_b[:, b:b + 1],
                               scale=conv_w[:, b, 0:1]).then_inc(tap, 1)

        def tanh_x_act(act, g, i, par):
            act.wait_ge(ctap, g * (3 * CB) + 6 * i + 6 + CR)
            act.wait_ge(xs_done, g * NX + i - 1 + CR) if i >= 2 or not (isinstance(g, int) and g == 0) else None
            act.activation(tx[i % 2][:, :, :], xs[par][:, 2 * i:2 * i + 2, :], ACT.Tanh).then_inc(txd, 1)

        def stage_z_act(act, g, i):
            act.wait_ge(in_full, g * NP + i + 1 + CR)
            j = i - NX
            act.wait_ge(inz_free, g * NZ + j - 1 + CR) if j >= 2 or not (isinstance(g, int) and g == 0) else None
            act.activation(tz[j % 2][:, :, :], pi[i % 2][:, :, :], ACT.Tanh, scale=0.5).then_inc(tz_done, 1)

        def stage_act(act, g, i, par):
            if i < NX:
                stage_x_act(act, g, i, par)
            else:
                stage_z_act(act, g, i)
            if 1 <= i <= NX:
                tanh_x_act(act, g, i - 1, par)

        def stage_dve(dve, g, i, par):
            if i < NX:
                for k in range(1, TAPS):
                    for b in (2 * i, 2 * i + 1):
                        n = 6 * i + 2 * (k - 1) + (b - 2 * i)
                        if k == 1:
                            dve.wait_ge(tap, g * CB + b + 1)
                        else:
                            dve.wait_ge(ctap, g * (3 * CB) + n - 1 + CR)
                        dve.scalar_tensor_tensor(out=xs[par][:, b, :], in0=raw[:, b, k:k + GT],
                                                 scalar=conv_w[:, b, k:k + 1], in1=xs[par][:, b, :],
                                                 op0=ALU.mult, op1=ALU.add).then_inc(ctap, 1)
            else:
                j = i - NX
                dve.wait_ge(tz_done, g * NZ + j + 1)
                dve.scalar_tensor_tensor(out=zs[par][:, 2 * j:2 * j + 2, :], in0=tz[j % 2][:, :, :], scalar=1.0,
                                         in1=pi[i % 2][:, :, :], op0=ALU.add, op1=ALU.mult).then_inc(inz_free, 1)
            if 1 <= i <= NX:
                j = i - 1
                dve.wait_ge(txd, g * NX + j + 1)
                dve.scalar_tensor_tensor(out=xs[par][:, 2 * j:2 * j + 2, :], in0=tx[j % 2][:, :, :], scalar=1.0,
                                         in1=xs[par][:, 2 * j:2 * j + 2, :], op0=ALU.add,
                                         op1=ALU.mult).then_inc(xs_done, 1)

        def stage_pe(pe, g, i):
            first = isinstance(g, int) and g == 0
            if i == 0:
                pe.wait_ge(xg_in, g * 32 + 32)
            if i < 2:
                if not first:
                    pe.wait_ge(inz_free, g * NZ - (i == 1) + CR)
            elif i - 2 < NX:
                pe.wait_ge(inx_free, g * NX + i - 1 + CR)
            else:
                pe.wait_ge(inz_free, g * NZ + i - 2 - NX + 1 + CR)
            for h in range(2):
                n = 0
                cols = slice((2 * i + h) * P, (2 * i + h + 1) * P)
                for ww, xx in ((wh, xh), (wl, xh), (wh, xl)):
                    for k in range(KD):
                        mm = pe.matmul(pi[i % 2][:, h, :], ww[:, k, cols], xx[:, k, :], start=n == 0, stop=n == 11)
                        n += 1
            mm.then_inc(in_full, 1)

        @block.scalar
        def _(act):
            for s in (inx_free, btok_done, dec_done, me, e2_done, ysqd):
                act.sem_inc(s, CR)
            for k in range(KD):
                act.wait_ge(stage_in, 16 * PRE) if k < PRE else act.wait_ge(w_in_s[k - PRE], 16)
                act.copy(wh[:, k, :], wraw[k]).then_inc(w_hi, 1)
            act.wait_ge(prep, 5)
            for i in range(NP):
                stage_act(act, 0, i, 0)

            def square(t):
                act.wait_ge(ygate, t + 1 + CR)
                act.wait_ge(ss, t + CR)
                act.activation(ysq[:, :, :], y[:, :, :], ACT.Square).then_inc(ysqd, 1)

            def body(g, par):
                for c in range(2):
                    t = g * 2 + c
                    first = isinstance(t, int) and t == 0
                    act.wait_ge(btr, t + 1)
                    act.wait_ge(st, t + CR)
                    act.copy(btok[:, :], pk[:, 0, :]).then_inc(btok_done, 1)
                    act.wait_ge(dsub, t + 1)
                    act.wait_ge(xdd_done, t + CR)
                    act.activation(dec[:, :], dec[:, :], ACT.Exp)
                    act.wait_ge(cdec, t + CR)
                    act.activation(cd[:, :], m[:, :, P - 1], ACT.Exp).then_inc(dec_done, 1)
                    act.wait_ge(e2_in, t * 32 + 32)
                    act.activation(e2[:, :, :], e2[:, :, :], ACT.Exp).then_inc(e2_done, 1)
                    if not first:
                        square(t - 1)
                    act.wait_ge(dec_done, t + 1 + CR)
                    for h in range(HEADS):
                        act.activation(m[:, h, :], m[:, h, :], ACT.Relu, bias=cst[:, h:h + 1],
                                       scale=-1.0).then_inc(seg, 1)
                    act.wait_ge(seg, t * HEADS + HEADS)
                    act.activation(m[:, :, :], m[:, :, :], ACT.Exp, scale=-1.0).then_inc(me, 1)
                    if not is_last(g):
                        for i in PAIRS[c]:
                            stage_act(act, g + 1, i, 1 - par)

            groups(act, body)
            square(T - 1)

        @block.vector
        def _(dve):
            for s in (inz_free, xs_done, xdt_done, cbm_done, m_done, ye, yd, cadd, var_done, o_done, ctap, res_done):
                dve.sem_inc(s, CR)
            dve.sem_inc(o_out, 16)
            dve.memset(ones[:, :], 1.0).then_inc(prep, 1)
            dve.memset(carry[:, :, :, :], 0.0).then_inc(prep, 1)
            for k in range(KD):
                dve.wait_ge(w_hi, k + 1)
                dve.tensor_tensor(wl[:, k, :], wraw[k], wh[:, k, :].bitcast(F32), ALU.subtract).then_inc(w_lo, 1)
            dve.memset(raw[:, :, :], 0.0).then_inc(prep, 1)
            dve.wait_ge(c_in, 80)
            dve.tensor_scalar(conv_w[:, :, :], conv_w[:, :, :], 0.5, None, ALU.mult).then_inc(prep, 1)
            dve.tensor_scalar(conv_b[:, :], conv_b[:, :], 0.5, None, ALU.mult).then_inc(prep, 1)
            for b in range(XB):
                ins = dve.tensor_scalar(wo[:, b, :], wo[:, b, :], norm_w[:, b:b + 1], 0.5, ALU.mult, ALU.mult)
            ins.then_inc(prep, 1)
            for i in range(NP):
                stage_dve(dve, 0, i, 0)

            def body(g, par):
                for c in range(2):
                    t = g * 2 + c
                    tok = slice(c * P, (c + 1) * P)
                    first = isinstance(t, int) and t == 0
                    dve.wait_ge(bc_in, t * 16 + 16)
                    dve.wait_ge(me, t + CR)
                    dve.wait_ge(res_done, t + CR)
                    dve.tensor_copy(pwt[:, :], prob[:, :, bass.ds(t, 1)].rearrange("p k t -> p (k t)")
                                    ).then_inc(pw_done, 1)
                    dve.tensor_copy(cst[:, :], cs_tok[:, bass.ds(t, 1), :].rearrange("p t h -> p (t h)")
                                    ).then_inc(cst_done, 1)
                    dve.wait_ge(cst_done, t + 1)
                    dve.wait_ge(xdd_done, t + CR)
                    dve.tensor_tensor(dec[:, :], m[:, :, P - 1], cst[:, :], ALU.subtract).then_inc(dsub, 1)
                    dve.wait_ge(ydiag, t * 2 + CR)
                    for half in range(2):
                        dve.wait_ge(xtr, t * 2 + half + 1)
                        dve.tensor_tensor(
                            xdt[:, 4 * half:4 * half + 4, :, :],
                            pxb[half][:, :, :].rearrange("p b (a d) -> p b a d", a=2),
                            dt_tok[:, bass.ds(t, 1), :].rearrange("p t (a b) -> p (t b) a", a=2)
                            [:, 4 * half:4 * half + 4, :].unsqueeze(3).broadcast_to([P, 4, 2, HD]),
                            ALU.mult).then_inc(xdt_done, 1)
                    dve.wait_ge(cbt, t + 1)
                    dve.tensor_tensor(cbm[:, :], pk[:, 1, :], tri[:, :], ALU.mult).then_inc(cbm_done, 1)
                    pairs = PAIRS[c] if not is_last(g) else ()
                    for i in pairs[:2]:
                        stage_dve(dve, g + 1, i, 1 - par)
                    dve.wait_ge(me, t + 1 + CR)
                    dve.wait_ge(cbm_done, t + 1 + CR)
                    dve.tensor_tensor(m[:, :, :], m[:, :, :],
                                      cbm[:, :].unsqueeze(1).broadcast_to([P, HEADS, P]), ALU.mult).then_inc(m_done, 1)
                    if not first:
                        finish(t - 1)
                    dve.wait_ge(e2_done, t + 1 + CR)
                    dve.wait_ge(pw_done, t + 1)
                    dve.wait_ge(res_in, t * 16 + 16)
                    dve.wait_ge(ya_in[0], t * 16 + 16)
                    dve.scalar_tensor_tensor(out=res[:, :], in0=ya[0][:, :], scalar=pwt[:, 0:1], in1=res[:, :],
                                             op0=ALU.mult, op1=ALU.add).then_inc(ra_done, 1)
                    for half in range(2):
                        blocks = slice(4 * half, 4 * half + 4)
                        dve.wait_ge(yoff, t * 2 + half + 1 + CR)
                        dve.tensor_tensor(e2[:, blocks, :], py[0][:, :, :], e2[:, blocks, :], ALU.mult).then_inc(ye, 1)
                        dve.wait_ge(ydiag, t * 2 + half + 1 + CR)
                        dve.wait_ge(op, t + CR)
                        dve.wait_ge(ysqd, t + CR)
                        for b in range(4 * half, 4 * half + 4):
                            ins = dve.scalar_tensor_tensor(
                                out=y[:, b, :], in0=xs[par][:, b, tok], scalar=d_skip[:, b:b + 1],
                                in1=py[1][:, b - 4 * half, :], op0=ALU.mult, op1=ALU.add)
                        ins.then_inc(yd, 1)
                        if half == 0:
                            for i in pairs[2:3]:
                                stage_dve(dve, g + 1, i, 1 - par)
                    dve.wait_ge(ra_done, t + 1)
                    dve.wait_ge(ya_in[1], t * 16 + 16)
                    dve.scalar_tensor_tensor(out=res[:, :], in0=ya[1][:, :], scalar=pwt[:, 1:2], in1=res[:, :],
                                             op0=ALU.mult, op1=ALU.add).then_inc(res_done, 1)
                    dve.wait_ge(cdec, t + 1 + CR)
                    for half in range(2):
                        dve.wait_ge(st, t + 1 + CR)
                        sl = carry[:, 4 * half:4 * half + 4, :, :].rearrange("p b a d -> p (b a d)")
                        dve.tensor_tensor(sl, pxb[half][:, :, :].rearrange("p b l -> p (b l)"), sl,
                                          ALU.add).then_inc(cadd, 1)
                    for i in pairs[3:]:
                        stage_dve(dve, g + 1, i, 1 - par)

            def finish(t):
                dve.wait_ge(ss, t + 1 + CR)
                dve.tensor_scalar(var[:, :], pk[:, 2, 0:1], 0.25 / INNER, EPS, ALU.mult, ALU.add).then_inc(var_done, 1)
                dve.wait_ge(rstd_done, t + 1 + CR)
                dve.wait_ge(op, t + 1 + CR)
                dve.wait_ge(res_done, t + 1 + CR)
                dve.wait_ge(o_out, t * 16 + 16)
                dve.scalar_tensor_tensor(out=o[:, :], in0=po[:, :], scalar=rstd[:, 0:1], in1=res[:, :],
                                         op0=ALU.mult, op1=ALU.add).then_inc(o_done, 1)

            groups(dve, body)
            finish(T - 1)

        @block.tensor
        def _(pe):
            for s in (in_full, st, yoff, ydiag, op, ss):
                pe.sem_inc(s, CR)
            pe.wait_ge(w_lo, KD)
            for i in range(NP):
                stage_pe(pe, 0, i)
            pe.wait_ge(prep, 6)

            def project(t):
                pe.wait_ge(ygate, t + 1 + CR)
                pe.wait_ge(o_done, t + CR)
                for b in range(XB):
                    mm = pe.matmul(po[:, :], y[:, b, :], wo[:, b, :], start=b == 0, stop=b == XB - 1)
                mm.then_inc(op, 1)
                pe.wait_ge(tree, t * 3 + 6)
                pe.wait_ge(cbm_done, t + 2 + CR) if not (isinstance(t, int) and t == T - 1) else None
                pe.matmul(pk[:, 2, 0:1], ysq[:, 0, :], ones[:, :], start=True, stop=True).then_inc(ss, 1)

            def body(g, par):
                for c in range(2):
                    t = g * 2 + c
                    tok = slice(c * P, (c + 1) * P)
                    first = isinstance(t, int) and t == 0
                    pairs = PAIRS[c] if not is_last(g) else ()
                    pe.wait_ge(xs_done, g * NX + NX + CR)
                    pe.wait_ge(var_done, t - 1 + CR) if not first and not (isinstance(t, int) and t == 1) else None
                    pe.transpose(pk[:, 0, :], xs[par][:, XB, tok], ident[:, :]).then_inc(btr, 1)
                    pe.wait_ge(cadd, t * 2 + CR)
                    for half in range(2):
                        for b in range(4):
                            tr = pe.transpose(pxb[half][:, b, :], xs[par][:, 4 * half + b, tok], ident[:, :])
                        tr.then_inc(xtr, 1)
                    for i in pairs[:1]:
                        stage_pe(pe, g + 1, i)
                    pe.wait_ge(btok_done, t + 1 + CR)
                    pe.matmul(pk[:, 1, :], xs[par][:, XB, tok], xs[par][:, XB + 1, tok], start=True,
                              stop=True).then_inc(cbt, 1)
                    for i in pairs[1:2]:
                        stage_pe(pe, g + 1, i)
                    if not first:
                        project(t - 1)
                    for i in pairs[2:3]:
                        stage_pe(pe, g + 1, i)

                    def off(half):
                        pe.wait_ge(ye, t * 2 + half + CR)
                        for b in range(4):
                            cols = carry[:, 4 * half + b, :, :].rearrange("p a d -> p (a d)")
                            mm = pe.matmul(py[0][:, b, :], cols, xs[par][:, XB + 1, tok], start=True, stop=True)
                        mm.then_inc(yoff, 1)

                    def diag(half):
                        pe.wait_ge(yd, t * 2 + half + CR)
                        for b in range(4):
                            for a in range(2):
                                mm = pe.matmul(py[1][a * HD:(a + 1) * HD, b, :], xdt[:, 4 * half + b, a, :],
                                               m[:, a * XB + 4 * half + b, :], start=True, stop=True)
                        mm.then_inc(ydiag, 1)

                    off(0)
                    pe.wait_ge(xdd_done, t + 1 + CR)
                    for half in range(2):
                        mm = pe.matmul(pxb[half][:, :, :].rearrange("p b l -> p (b l)"), btok[:, :],
                                       xdd[:, 4 * half:4 * half + 4, :, :].rearrange("p b a d -> p (b a d)"),
                                       start=True, stop=True)
                    mm.then_inc(st, 1)
                    pe.wait_ge(m_done, t + 1 + CR)
                    diag(0)
                    for i in pairs[3:4]:
                        stage_pe(pe, g + 1, i)
                    off(1)
                    diag(1)
                    for i in pairs[4:]:
                        stage_pe(pe, g + 1, i)

            groups(pe, body)
            project(T - 1)


def kernel(**inputs):
    import numpy as np
    import concourse.bacc as bacc
    from concourse.bass_utils import run_bass_kernel_spmd as run

    a = {k: np.ascontiguousarray(v) for k, v in inputs.items()}
    w = a["L0_attn_in_proj_w"]
    zw, xw, dtw = w[:INNER], w[INNER:INNER + CB * P], w[INNER + CB * P:]

    def by_half(v):
        return v.reshape(XB, 2, -1).transpose(1, 0, 2).reshape(v.shape)

    def rows(wt, n):
        return np.ascontiguousarray(wt.reshape(n, P, -1).transpose(1, 0, 2))

    row = np.zeros((1, ROW_N), np.float32)
    row[0, ROW["rank"]] = np.arange(E, 0, -1)
    row[0, ROW["full"]] = np.arange(T) * P
    row[0, ROW["before"]] = np.tril(np.ones((E, E)), -1).reshape(-1)
    row[0, ROW["tile"]] = np.arange(J)
    row[0, ROW["iota"]] = np.arange(P)
    row[0, ROW["tok_tile"]] = np.tile(np.arange(T), 2)
    gu = np.concatenate([a["L0_ffn_w_gate_proj"], a["L0_ffn_w_up_proj"]], axis=1)
    arrays = {
        "x": a["L0_attn_u"].reshape(TOKENS, D),
        "w_in": rows(np.concatenate([xw, zw]).T, KD),
        "w_dtr": rows(np.concatenate([by_half(dtw), a["L0_ffn_w_gate_router"]]).T, KD),
        "w_out": rows(a["L0_attn_out_proj_w"].T, XB),
        "conv_w": rows(a["L0_attn_conv_w"], CB),
        "conv_b": np.ascontiguousarray(a["L0_attn_conv_b"].reshape(CB, P).T),
        "dt_bias": by_half(a["L0_attn_dt_bias"]).reshape(1, HEADS),
        "a_log": by_half(a["L0_attn_A_log"]).reshape(1, HEADS),
        "d_skip": np.ascontiguousarray(np.repeat(a["L0_attn_D_skip"], HD).reshape(XB, P).T),
        "norm_w": np.ascontiguousarray(a["L0_attn_norm_w"].reshape(XB, P).T),
        "w_gu": np.ascontiguousarray(gu.transpose(0, 2, 1).reshape(E, KD, P, 2 * F).transpose(0, 2, 1, 3)),
        "w_down": np.ascontiguousarray(a["L0_ffn_w_down_proj"].transpose(0, 2, 1).reshape(E, 2, FH, D)
                                       .transpose(0, 2, 1, 3)),
        "ident_in": np.eye(P, dtype=np.float32),
        "tri_in": np.triu(np.ones((P, P), np.float32)),
        "stri_in": np.triu(np.ones((P, P), np.float32), 1),
        "row_in": row,
        "part_in": np.arange(P, dtype=np.float32).reshape(P, 1),
    }
    nc = bacc.Bacc("TRN2", target_bir_lowering=False, num_devices=1)
    args = [nc.dram_tensor(f"in_{n}", v.shape, F32, kind="ExternalInput").ap() for n, v in arrays.items()]
    args.append(nc.dram_tensor("out", (TOKENS, D), F32, kind="ExternalOutput").ap())
    block(nc, *args)
    r = run(nc, [{f"in_{n}": v for n, v in arrays.items()}], core_ids=[0])
    return r.results[0]["out"].reshape(a["L0_attn_u"].shape)
```

```python
from contextlib import ExitStack

import concourse.bass as bass
from concourse import mybir

ALU = mybir.AluOpType
ACT = mybir.ActivationFunctionType
AX = mybir.AxisListType
F32 = mybir.dt.float32
F32R = mybir.dt.float32r
BF16 = mybir.dt.bfloat16
U32 = mybir.dt.uint32
I32 = mybir.dt.int32

P = 128
TOKENS, D = 2048, 512
KD = D // P
INNER, STATE, HEADS, HD, TAPS = 1024, 128, 16, 64, 4
XB = INNER // P
CB = XB + 2
E, F = 8, 192
FH = F // 2
T = TOKENS // P
G = T // 2
GT = 2 * P
C = HEADS + E
J = 2 * T + E - 1
SIZES = {F32: 4, F32R: 4, BF16: 2, U32: 4, I32: 4}

ROW = {}
for _name, _n in (("rank", E), ("full", T), ("before", E * E), ("tile", J), ("iota", P), ("tok_tile", 2 * T)):
    ROW[_name] = slice(sum(s.stop - s.start for s in ROW.values()), sum(s.stop - s.start for s in ROW.values()) + _n)
ROW_N = max(s.stop for s in ROW.values())
EPS = 1e-5
BIG = 1.0e30


class Area:

    def __init__(self, nc, start, end):
        self.nc, self.at, self.end = nc, start, end

    def __call__(self, name, shape, dt=F32):
        size = SIZES[dt]
        for n in shape[1:]:
            size *= n
        at, self.at = self.at, self.at + (size + 31) // 32 * 32
        assert self.at <= self.end, (name, self.at, self.end)
        return self.nc.alloc_sbuf_tensor_at(name, shape, dt, offset=at)


def block(nc, x, w_in, w_dtr, w_out, conv_w, conv_b, dt_bias, a_log, d_skip, norm_w,
          w_gu, w_down, ident_in, tri_in, stri_in, row_in, part_in, out):
    ctx = ExitStack()
    with ctx:
        def sem(name):
            return ctx.enter_context(nc.semaphore(name))

        def dram(name, shape):
            return nc.dram_tensor(name, shape, F32, kind="Internal").ap()

        xn_d = dram("xn_d", (TOKENS, D))
        xt_d = dram("xt_d", (G, P, KD, GT))
        cs_d = dram("cs_d", (T, HEADS, P))
        y_d = dram("y_d", (J * P, D))

        start = (nc.sbuf_base + 63) // 32 * 32
        top = nc.sbuf_usable_end // 32 * 32
        weights_size = E * (KD * 2 * F + 2 * D) * 2 * 4
        lasting = Area(nc, start, top)
        ident = lasting("ident", [P, P])
        tri = lasting("tri", [P, P])
        cs_tok = lasting("cs_tok", [P, T, HEADS])
        dt_tok = lasting("dt_tok", [P, T, HEADS])
        slot_u = lasting("slot_u", [P, 2, T], U32)
        prob = lasting("prob", [P, 2, T])
        idx = lasting("idx", [P, J], U32)
        eidx = lasting("eidx", [1, J], I32)
        packed = lasting("packed", [1, (J - 3) // 2], I32)
        wts = Area(nc, top - weights_size, top)
        guh = wts("guh", [P, E, KD, 2 * F], F32R)
        gul = wts("gul", [P, E, KD, 2 * F], F32R)
        dh = wts("dh", [FH, E, 2, D], F32R)
        dl = wts("dl", [FH, E, 2, D], F32R)
        gu_size, d_size = KD * 2 * F * 4, 2 * D * 4
        odd_stage = (Area(nc, top - weights_size + E * gu_size + (E - 1) * gu_size, top)("gur1", [P, KD, 2 * F]),
                     Area(nc, top - d_size, top)("dr1", [FH, 2, D]))
        win_stage = Area(nc, lasting.at, top)("win_stage", [P, KD - 1, (CB + XB) * P])
        slice_size = (CB + XB) * P * 4
        stage_in = sem("stage_in")
        front_done = sem("front_done")

        with nc.Block() as engines:
            front_parts = front(nc, Area(nc, lasting.at, top - weights_size), sem, x, w_dtr, dt_bias, a_log,
                                w_gu, w_down, ident_in, tri_in, stri_in, row_in, part_in, xn_d, xt_d, cs_d,
                                ident, tri, cs_tok, dt_tok, slot_u, prob, idx, eidx, packed, guh, gul, dh, dl, odd_stage, front_done)
            expert_parts = experts(nc, Area(nc, lasting.at + PRE * slice_size, top - weights_size), sem, w_in, win_stage, stage_in,
                                   xn_d, y_d, ident, idx, eidx, packed, guh, gul, dh, dl, front_done)
            for name in ("sync", "gpsimd", "scalar", "vector", "tensor"):
                def both(eng, name=name):
                    front_parts[name](eng)
                    expert_parts[name](eng)
                {"sync": engines.sync, "gpsimd": engines.gpsimd, "scalar": engines.scalar,
                 "vector": engines.vector, "tensor": engines.tensor}[name](both)
        mamba(nc, Area(nc, lasting.at + (KD - 1) * slice_size, top), lasting.at, win_stage, stage_in, sem, x, w_in, w_out, conv_w, conv_b, d_skip,
              norm_w, xt_d, cs_d, y_d, ident, tri, cs_tok, dt_tok, slot_u, prob, out)


PRE = 2
CR = 1


def by_twos(eng, n, body, last=1):
    body(0, 0, 0)
    with eng.Fori(0, (n - 1 - last) // 2) as i:
        body(i * 2 + 1, 1, i)
        body(i * 2 + 2, 0, i + 1)
    for i in range(n - last, n):
        body(i, i % 2, i // 2)


class Chain:

    def __init__(self, eng, semaphore):
        self.eng, self.semaphore, self.n = eng, semaphore, 0

    def after(self):
        if self.n:
            self.eng.wait_ge(self.semaphore, self.n)

    def step(self, ins):
        ins.then_inc(self.semaphore, 1)
        self.n += 1


def static(i, *values):
    return isinstance(i, int) and i in values


def front(nc, area, sem, x, w_dtr_in, dt_bias, a_log, w_gu, w_down, ident_in, tri_in, stri_in, row_in, part_in,
          xn_d, xt_d, cs_d, ident, tri, cs_tok, dt_tok, slot_u, prob, idx, eidx, packed, guh, gul, dh, dl,
          odd_stage, front_done):
    with ExitStack() as ctx:
        sb = area

        def pb(name, shape):
            return ctx.enter_context(nc.psum_tensor(name, shape, F32))

        row = sb("row", [P, ROW_N])
        part = sb("part", [P, 1])
        stri = sb("stri", [P, P])
        stats = [sb(f"stats{i}", [P, 2, 6]) for i in range(2)]
        mv = sb("mv", [P, 2, 2])
        veps = sb("veps", [P, 2])
        rstd = sb("rstd", [P, 2])
        nhalf = sb("nhalf", [P, 2])
        wr = sb("wr", [P, KD, C])
        rt = sb("rt", [C, GT])
        rr = sb("rr", [P, T, C])
        bias_bc = sb("bias_bc", [P, HEADS])
        alog_bc = sb("alog_bc", [P, HEADS])
        a_bc = sb("a_bc", [P, HEADS])
        over = Area(nc, area.at, area.end)
        xin = [sb(f"xin{i}", [P, 2, D]) for i in range(2)]
        xt = [sb(f"xt{i}", [P, KD, GT]) for i in range(2)]
        gur, dr = [sb("gur0", [P, KD, 2 * F]), odd_stage[0]], [sb("dr0", [FH, 2, D]), odd_stage[1]]
        big = [over(f"sp{i}", [P, T, HEADS]) for i in range(6)]
        e8 = [over(f"rt8_{i}", [P, T, E]) for i in range(5)]
        t1 = [over(f"rt1_{i}", [P, T]) for i in range(6)]
        cst_rows = over("cst_rows", [HEADS, T, P])
        ones_b = over("ones_b", [P, P], BF16)
        earlier = over("earlier", [P, T, E], BF16)
        sums = [over(f"sums{i}", [P, T, E], BF16) for i in range(2)]
        stri_b = over("stri_b", [P, P], BF16)
        picks = over("picks", [P, T, E], BF16)
        tot = over("tot", [P, E])
        gt = over("gt", [P, E, T])
        tiles = over("tiles", [P, E])
        base = over("base", [P, E])
        end = over("end", [P, E])
        slots = over("slots", [P, 2, T])
        hi_u = over("hi_u", [P, 2 * T], U32)
        lo_u = over("lo_u", [P, 2 * T], U32)
        hi_f = over("hi_f", [P, 2 * T])
        lo_f = over("lo_f", [P, 2 * T])
        in_tile = over("in_tile", [P, 2 * T, J], BF16)
        who = over("who", [P, 2 * T, 2 * J], BF16)
        place = over("place", [P, 2 * T, P], BF16)
        tokf = over("tokf", [P, J])
        ecmp = over("ecmp", [1, J, E])
        ef = over("ef", [1, J + 1])
        pf = over("pf", [1, (J - 3) // 2])
        pt = [pb(f"pt{i}", [P, KD, P]) for i in range(2)]
        pr = pb("pr", [C, GT])
        prt = pb("prt", [P, 2, C])
        pcs = pb("pcs", [P, T, HEADS])
        pct = pb("pct", [HEADS, 4, P])
        ppos = pb("ppos", [P, T, E])
        ptot = pb("ptot", [P, 128])
        ptok = ptot

        consts_in = sem("consts_in")
        x_in = [sem(f"x_in{i}") for i in range(2)]
        w_in = [sem(f"ew_in{i}") for i in range(2)]
        w_hi = sem("ew_hi")
        w_lo = sem("ew_lo")
        mv_done = sem("mv_done")
        rstd_done = sem("rstd_done")
        xn_done = sem("xn_done")
        xn_out = sem("xn_out")
        tr_done = sem("tr_done")
        xt_done = sem("xt_done")
        xt_out = [sem(f"xt_out{i}") for i in range(2)]
        r_done = sem("r_done")
        rt_done = sem("rt_done")
        rtr_done = sem("rtr_done")
        rr_done = sem("rr_done")
        st_chain = sem("st_chain")
        a_done = sem("a_done")
        nh_done = sem("nh_done")
        e1, e2 = sem("e1"), sem("e2")
        b1, b2 = sem("b1"), sem("b2")
        rows_stored = sem("rows_stored")
        idx_done = sem("idx_done")
        picks_done = sem("picks_done")
        pos_done = sem("pos_done")
        who_done = sem("who_done")
        tok_done = sem("tok_done")
        decay_done = sem("decay_done")
        cs_ready = sem("cs_ready")
        cs_copied = sem("cs_copied")
        ct_done = sem("ct_done")
        ct_copied = sem("ct_copied")
        cs_out = sem("cs_out")
        route_sem, time_sem = sem("route"), sem("time")
        NQ = T // 2
        assert NQ == E
        xr = x.rearrange("(q t p) d -> q p t d", p=P, t=2)
        xnr = xn_d.rearrange("(q t p) d -> q p t d", p=P, t=2)

        def sync(sp):
            sp.dma_start(xin[0][:, :, :], xr[0]).then_inc(x_in[0], 16)
            sp.dma_start(ident[:, :], ident_in).then_inc(consts_in, 16)
            sp.dma_start(wr[:, :, :], w_dtr_in).then_inc(consts_in, 16)
            sp.dma_start(row[:, :], row_in.broadcast_to([P, ROW_N])).then_inc(consts_in, 16)
            sp.dma_start(bias_bc[:, :], dt_bias.broadcast_to([P, HEADS])).then_inc(consts_in, 16)
            sp.dma_start(alog_bc[:, :], a_log.broadcast_to([P, HEADS])).then_inc(consts_in, 16)
            sp.dma_start(tri[:, :], tri_in).then_inc(consts_in, 16)
            sp.dma_start(stri[:, :], stri_in).then_inc(consts_in, 16)
            sp.dma_start(part[:, :], part_in).then_inc(consts_in, 16)
            sp.dma_start(xin[1][:, :, :], xr[1]).then_inc(x_in[1], 16)

            def body(q, par):
                sp.wait_ge(xn_done, q + 1)
                sp.dma_start(xnr[q], xin[par][:, :, :]).then_inc(xn_out, 16)
                sp.wait_ge(xt_done, q * 2 + 2)
                sp.dma_start(xt_d[q], xt[par][:, :, :]).then_inc(xt_out[par], 16)
                if not static(q, NQ - 2, NQ - 1):
                    sp.wait_ge(xn_out, q * 16 + 16)
                    sp.dma_start(xin[par][:, :, :], xr[q + 2]).then_inc(x_in[par], 16)

            body(0, 0)
            body(1, 1)
            with sp.Fori(0, (NQ - 4) // 2) as i:
                body(i * 2 + 2, 0)
                body(i * 2 + 3, 1)
            body(NQ - 2, 0)
            body(NQ - 1, 1)
            for i in range(2):
                sp.wait_ge(xt_out[i], 16 * (NQ // 2) + i * 16)
            sp.wait_ge(xn_out, 16 * NQ)
            sp.sem_inc(rows_stored, 1)
            sp.wait_ge(ct_copied, 4)
            sp.dma_start(cs_d.rearrange("t h l -> h t l"), cst_rows[:, :, :]).then_inc(cs_out, 16)
            sp.wait_ge(cs_out, 16)

        def gpsimd(pool):
            pool.memset(nhalf[:, :], -0.5).then_inc(nh_done, 1)
            pool.wait_ge(nh_done, 1)
            for i in range(2):
                pool.dma_start(gur[i][:, :, :], w_gu[i]).then_inc(w_in[i], 16)
                pool.dma_start(dr[i][:, :, :], w_down[i]).then_inc(w_in[i], 16)

            def body(q, par, r):
                pool.wait_ge(mv_done, q + 1)
                pool.tensor_tensor(rstd[:, :], veps[:, :], nhalf[:, :], ALU.pow).then_inc(rstd_done, 1)
                if not static(q, 0, NQ - 1):
                    pool.wait_ge(w_lo, q * 2)
                    pool.dma_start(gur[1 - par][:, :, :], w_gu[q + 1]).then_inc(w_in[1 - par], 16)
                    pool.dma_start(dr[1 - par][:, :, :], w_down[q + 1]).then_inc(w_in[1 - par], 16)

            by_twos(pool, NQ, body)

        def scalar(act):
            act.wait_ge(consts_in, 16 * 8)
            act.activation(a_bc[:, :], alog_bc[:, :], ACT.Exp).then_inc(a_done, 1)

            def body(q, par, r):
                act.wait_ge(w_in[par], r * 32 + 32)
                act.copy(guh[:, bass.ds(q, 1), :, :].rearrange("p e k n -> p (e k) n"), gur[par][:, :, :]
                         ).then_inc(w_hi, 1)
                act.copy(dh[:, bass.ds(q, 1), :, :].rearrange("p e k n -> p (e k) n"), dr[par][:, :, :]
                         ).then_inc(w_hi, 1)
                if not static(q, 0):
                    act.wait_ge(r_done, q - 1 + CR)
                    act.wait_ge(xt_out[par], r * 16 + par * 16)
                for j in range(2):
                    act.wait_ge(tr_done, q * 2 + j + 1)
                    act.copy(xt[par][:, :, j * P:(j + 1) * P], pt[j][:, :, :]).then_inc(xt_done, 1)

            by_twos(act, NQ, body)
            act.wait_ge(b1, 1)
            act.activation(big[1][:, :, :], big[1][:, :, :], ACT.Exp).then_inc(e1, 1)
            act.wait_ge(b2, 1)
            act.activation(t1[2][:, :], t1[2][:, :], ACT.Exp).then_inc(e2, 1)
            act.wait_ge(cs_ready, 1)
            act.copy(cs_tok[:, :, :], pcs[:, :, :]).then_inc(cs_copied, 1)
            for k in range(4):
                act.wait_ge(ct_done, k + 1)
                act.copy(cst_rows[:, 4 * k:4 * k + 4, :], pct[:, :, :]).then_inc(ct_copied, 1)

        def vector(dve):
            dve.sem_inc(xt_out[1], 16)
            def statistics(q, par, r):
                dve.wait_ge(x_in[par], r * 16 + 16)
                for j in range(2):
                    dve.bn_stats(stats[par][:, j, :], xin[par][:, j, :]).then_inc(st_chain, 1)
                at = q * 6 + 2
                dve.wait_ge(st_chain, at)
                even, odd = stats[par][:, :, 1], stats[par][:, :, 4]
                dve.tensor_tensor(mv[:, :, 0], even, odd, ALU.add).then_inc(st_chain, 1)
                dve.tensor_tensor(mv[:, :, 1], even, odd, ALU.subtract).then_inc(st_chain, 1)
                dve.tensor_tensor(veps[:, :], stats[par][:, :, 2], stats[par][:, :, 5], ALU.add).then_inc(st_chain, 1)
                dve.wait_ge(st_chain, at + 3)
                dve.tensor_scalar(mv[:, :, 0], mv[:, :, 0], 0.5, None, ALU.mult)
                dve.scalar_tensor_tensor(out=mv[:, :, 1], in0=mv[:, :, 1], scalar=0.25, in1=mv[:, :, 1],
                                         op0=ALU.mult, op1=ALU.mult)
                dve.tensor_scalar(veps[:, :], veps[:, :], 1.0 / D, EPS, ALU.mult, ALU.add).then_inc(st_chain, 1)
                dve.wait_ge(st_chain, at + 4)
                dve.tensor_tensor(veps[:, :], veps[:, :], mv[:, :, 1], ALU.add).then_inc(mv_done, 1)

            def projected(q):
                dve.wait_ge(r_done, q + 1 + CR)
                dve.tensor_copy(rt[:, :], pr[:, :]).then_inc(rt_done, 1)
                dve.wait_ge(rtr_done, q + 1)
                dve.tensor_copy(rr[:, bass.ds(q * 2, 2), :], prt[:, :, :]).then_inc(rr_done, 1)

            def body(q, par, r):
                dve.wait_ge(rstd_done, q + 1)
                for j in range(2):
                    ins = dve.tensor_scalar(xin[par][:, j, :], xin[par][:, j, :], mv[:, j, 0:1], rstd[:, j:j + 1],
                                            ALU.subtract, ALU.mult)
                ins.then_inc(xn_done, 1)
                if not static(q, NQ - 1):
                    dve.wait_ge(xn_done, q + 1)
                    statistics(q + 1, 1 - par, r + par)
                dve.wait_ge(w_hi, q * 2 + 2)
                dve.tensor_tensor(gul[:, bass.ds(q, 1), :, :].rearrange("p e k n -> p (e k) n"), gur[par][:, :, :],
                                  guh[:, bass.ds(q, 1), :, :].rearrange("p e k n -> p (e k) n").bitcast(F32),
                                  ALU.subtract).then_inc(w_lo, 1)
                dve.tensor_tensor(dl[:, bass.ds(q, 1), :, :].rearrange("p e k n -> p (e k) n"), dr[par][:, :, :],
                                  dh[:, bass.ds(q, 1), :, :].rearrange("p e k n -> p (e k) n").bitcast(F32),
                                  ALU.subtract).then_inc(w_lo, 1)
                if not static(q, 0):
                    projected(q - 1)

            statistics(0, 0, 0)
            by_twos(dve, NQ, body)
            projected(NQ - 1)
            dve.wait_ge(rr_done, NQ)
            dve.wait_ge(w_lo, 2 * E)
            dve.wait_ge(xt_out[0], 16 * (NQ // 2))
            dve.wait_ge(xt_out[1], 16 * (NQ // 2) + 16)
            dve.wait_ge(xn_out, 16 * NQ)

            def per_tile(ap, n):
                return ap.unsqueeze(2).broadcast_to([P, T, n])

            route, time = Chain(dve, route_sem), Chain(dve, time_sem)
            v, ex, s, s2, acc, den = big
            one1, one2, w1, rest, w2 = e8
            m1, i1, m2, p1, p2, i2 = t1
            sc = rr[:, :, HEADS:C]
            rank3 = row[:, ROW["rank"]].unsqueeze(1).broadcast_to([P, T, E])

            def per_tile(ap, n):
                return ap.unsqueeze(2).broadcast_to([P, T, n])

            def series(k):
                time.after()
                time.step(dve.scalar_tensor_tensor(out=acc[:, :, :], in0=acc[:, :, :], scalar=1.0 / k,
                                                   in1=s2[:, :, :], op0=ALU.add, op1=ALU.mult))

            time.step(dve.tensor_tensor(v[:, :, :], rr[:, :, 0:HEADS],
                                        bias_bc[:, :].unsqueeze(1).broadcast_to([P, T, HEADS]), ALU.add))
            route.step(dve.tensor_reduce(m1[:, :], sc, AX.X, ALU.max))
            time.after()
            dve.scalar_tensor_tensor(out=ex[:, :, :], in0=v[:, :, :], scalar=-1.0, in1=v[:, :, :],
                                     op0=ALU.mult, op1=ALU.min).then_inc(b1, 1)
            route.after()
            route.step(dve.tensor_tensor(w1[:, :, :], sc, per_tile(m1[:, :], E), ALU.is_equal))
            dve.memset(ones_b[:, :], 1.0)
            route.after()
            route.step(dve.tensor_tensor(w2[:, :, :], w1[:, :, :], rank3, ALU.mult))
            dve.tensor_copy(stri_b[:, :], stri[:, :])
            route.after()
            route.step(dve.tensor_reduce(i1[:, :], w2[:, :, :], AX.X, ALU.max))
            dve.wait_ge(e1, 1)
            time.step(dve.tensor_scalar(den[:, :, :], ex[:, :, :], 2.0, None, ALU.add))
            route.after()
            route.step(dve.tensor_tensor(one1[:, :, :], rank3, per_tile(i1[:, :], E), ALU.is_equal))
            time.after()
            time.step(dve.reciprocal(acc[:, :, :], den[:, :, :]))
            route.after()
            route.step(dve.scalar_tensor_tensor(out=rest[:, :, :], in0=one1[:, :, :], scalar=-BIG, in1=sc,
                                                op0=ALU.mult, op1=ALU.add))
            time.after()
            time.step(dve.tensor_tensor(s[:, :, :], ex[:, :, :], acc[:, :, :], ALU.mult))
            route.after()
            route.step(dve.tensor_reduce(p2[:, :], rest[:, :, :], AX.X, ALU.max))
            time.after()
            time.step(dve.tensor_tensor(s2[:, :, :], s[:, :, :], s[:, :, :], ALU.mult))
            route.after()
            route.step(dve.tensor_tensor(w1[:, :, :], rest[:, :, :], per_tile(p2[:, :], E), ALU.is_equal))
            time.after()
            time.step(dve.tensor_scalar(acc[:, :, :], s2[:, :, :], 1.0 / 17, None, ALU.mult))
            route.after()
            route.step(dve.tensor_tensor(w2[:, :, :], w1[:, :, :], rank3, ALU.mult))
            series(15)
            route.after()
            route.step(dve.tensor_reduce(i2[:, :], w2[:, :, :], AX.X, ALU.max))
            series(13)
            route.after()
            route.step(dve.tensor_tensor(one2[:, :, :], rank3, per_tile(i2[:, :], E), ALU.is_equal))
            series(11)
            route.after()
            route.step(dve.tensor_tensor(picks[:, :, :], one1[:, :, :], one2[:, :, :], ALU.add))
            dve.tensor_tensor(m2[:, :], p2[:, :], m1[:, :], ALU.subtract).then_inc(b2, 1)
            dve.memset(earlier[:, 0:1, :], 0.0)
            route.after()
            route.step(dve.tensor_copy(sums[0][:, :, :], picks[:, :, :]))
            step, at = 1, 0
            for k in (9, 7, 5):
                series(k)
                route.after()
                dve.tensor_copy(sums[1 - at][:, 0:step, :], sums[at][:, 0:step, :])
                route.step(dve.tensor_tensor(sums[1 - at][:, step:, :], sums[at][:, step:, :],
                                             sums[at][:, 0:T - step, :], ALU.add))
                step, at = step * 2, 1 - at
            assert step == T // 2
            series(3)
            route.after()
            dve.tensor_copy(earlier[:, 1:step + 1, :], sums[at][:, 0:step, :])
            dve.tensor_tensor(earlier[:, step + 1:, :], sums[at][:, step:T - 1, :], sums[at][:, 0:T - 1 - step, :],
                              ALU.add).then_inc(picks_done, 1)
            time.after()
            time.step(dve.scalar_tensor_tensor(out=acc[:, :, :], in0=acc[:, :, :], scalar=1.0, in1=s[:, :, :],
                                               op0=ALU.add, op1=ALU.mult))
            time.step(dve.tensor_scalar(den[:, :, :], v[:, :, :], 0.0, None, ALU.max))

            dve.wait_ge(pos_done, 1)
            route.step(dve.tensor_copy(tot[:, :], ptot[:, 0:E]))
            time.after()
            time.step(dve.scalar_tensor_tensor(out=dt_tok[:, :, :], in0=acc[:, :, :], scalar=2.0, in1=den[:, :, :],
                                               op0=ALU.mult, op1=ALU.add))
            route.after()
            route.step(dve.tensor_tensor(gt[:, :, :], tot[:, :].unsqueeze(2).broadcast_to([P, E, T]),
                                         row[:, ROW["full"]].unsqueeze(1).broadcast_to([P, E, T]), ALU.is_gt))
            dve.wait_ge(a_done, 1)
            time.after()
            dve.scalar_tensor_tensor(out=s[:, :, :], in0=dt_tok[:, :, :], scalar=-1.0,
                                     in1=a_bc[:, :].unsqueeze(1).broadcast_to([P, T, HEADS]),
                                     op0=ALU.mult, op1=ALU.mult).then_inc(decay_done, 1)
            dve.wait_ge(e2, 1)
            time.step(dve.tensor_scalar(p1[:, :], m2[:, :], 1.0, None, ALU.add))
            route.after()
            route.step(dve.tensor_reduce(tiles[:, :], gt[:, :, :], AX.X, ALU.add))
            time.after()
            time.step(dve.reciprocal(i1[:, :], p1[:, :]))
            route.after()
            route.step(dve.tensor_tensor(gt[:, :, 0:E], tiles[:, :].unsqueeze(1).broadcast_to([P, E, E]),
                                         row[:, ROW["before"]].rearrange("p (a b) -> p a b", a=E), ALU.mult))
            time.after()
            time.step(dve.tensor_scalar(prob[:, 0, :], i1[:, :], 0.5, None, ALU.mult))
            route.after()
            route.step(dve.tensor_reduce(base[:, :], gt[:, :, 0:E], AX.X, ALU.add))
            time.after()
            time.step(dve.tensor_tensor(prob[:, 1, :], prob[:, 0, :], m2[:, :], ALU.mult))
            route.after()
            route.step(dve.tensor_tensor(end[:, :], base[:, :], tiles[:, :], ALU.add))
            route.step(dve.scalar_tensor_tensor(out=rest[:, :, :], in0=base[:, :].unsqueeze(1).broadcast_to([P, T, E]),
                                                scalar=float(P), in1=ppos[:, :, :], op0=ALU.mult, op1=ALU.add))
            route.after()
            route.step(dve.tensor_tensor(w1[:, :, :], one1[:, :, :], rest[:, :, :], ALU.mult))
            route.step(dve.tensor_tensor(w2[:, :, :], one2[:, :, :], rest[:, :, :], ALU.mult))
            time.step(dve.tensor_tensor(ecmp[:, :, :], row[0:1, ROW["tile"]].unsqueeze(2).broadcast_to([1, J, E]),
                                        end[0:1, :].unsqueeze(1).broadcast_to([1, J, E]), ALU.is_ge))
            route.after()
            route.step(dve.tensor_reduce(slots[:, 0, :], w1[:, :, :], AX.X, ALU.add))
            route.step(dve.tensor_reduce(slots[:, 1, :], w2[:, :, :], AX.X, ALU.add))
            time.after()
            time.step(dve.tensor_reduce(ef[:, 0:J], ecmp[:, :, :], AX.X, ALU.add))
            route.after()
            route.step(dve.tensor_copy(slot_u[:, :, :], slots[:, :, :]))
            time.after()
            time.step(dve.tensor_scalar(ef[:, 0:J], ef[:, 0:J], float(E - 1), None, ALU.min))
            flat_u = slot_u[:, :, :].rearrange("p k t -> p (k t)")
            route.after()
            route.step(dve.tensor_scalar(hi_u[:, :], flat_u, 7, None, ALU.logical_shift_right))
            route.step(dve.tensor_scalar(lo_u[:, :], flat_u, P - 1, None, ALU.bitwise_and))
            time.after()
            dve.tensor_copy(eidx[:, :], ef[:, 0:J])
            by_step = ef[:, :].rearrange("o (i two) -> o two i", two=2)
            low, high = slice(0, (J - 3) // 2), slice(1, (J - 1) // 2)
            time.step(dve.scalar_tensor_tensor(out=pf[:, :], in0=by_step[:, 1, high], scalar=float(E),
                                               in1=by_step[:, 0, high], op0=ALU.mult, op1=ALU.add))
            route.after()
            route.step(dve.tensor_copy(hi_f[:, :], hi_u[:, :]))
            route.step(dve.tensor_copy(lo_f[:, :], lo_u[:, :]))
            time.after()
            time.step(dve.scalar_tensor_tensor(out=pf[:, :], in0=pf[:, :], scalar=float(E),
                                               in1=by_step[:, 1, low], op0=ALU.mult, op1=ALU.add))
            route.after()
            n2 = 2 * T
            route.step(dve.tensor_tensor(in_tile[:, :, :], hi_f[:, :].unsqueeze(2).broadcast_to([P, n2, J]),
                                         row[:, ROW["tile"]].unsqueeze(1).broadcast_to([P, n2, J]), ALU.is_equal))
            dve.tensor_tensor(place[:, :, :], lo_f[:, :].unsqueeze(2).broadcast_to([P, n2, P]),
                              row[:, ROW["iota"]].unsqueeze(1).broadcast_to([P, n2, P]), ALU.is_equal)
            time.after()
            time.step(dve.scalar_tensor_tensor(out=pf[:, :], in0=pf[:, :], scalar=float(E),
                                               in1=by_step[:, 0, low], op0=ALU.mult, op1=ALU.add))
            route.after()
            dve.tensor_tensor(who[:, :, 0:J], in_tile[:, :, :],
                              row[:, ROW["tok_tile"]].unsqueeze(2).broadcast_to([P, n2, J]), ALU.mult)
            dve.tensor_scalar(who[:, :, J:2 * J], in_tile[:, :, :], part[:, 0:1], None, ALU.mult).then_inc(who_done, 1)
            time.after()
            dve.tensor_copy(packed[:, :], pf[:, :])
            dve.wait_ge(tok_done, 1)
            route.step(dve.tensor_scalar(tokf[:, :], ptok[:, 0:J], float(P), None, ALU.mult))
            route.after()
            route.step(dve.tensor_tensor(tokf[:, :], tokf[:, :], ptok[:, J:2 * J], ALU.add))
            route.after()
            dve.tensor_copy(idx[:, :], tokf[:, :]).then_inc(idx_done, 1)

        def tensor(pe):
            pe.wait_ge(consts_in, 16 * 8)
            pe.sem_inc(r_done, CR)

            def project(q, par):
                pe.wait_ge(xt_done, q * 2 + 2)
                if not static(q, 0):
                    pe.wait_ge(rt_done, q)
                for k in range(KD):
                    mm = pe.matmul(pr[:, :], wr[:, k, :], xt[par][:, k, :], start=k == 0, stop=k == KD - 1)
                mm.then_inc(r_done, 1)
                pe.wait_ge(rt_done, q + 1)
                if not static(q, 0):
                    pe.wait_ge(rr_done, q)
                pe.matmul(prt[:, 0, :], rt[:, 0:P], ident[0:C, 0:C], start=True, stop=True)
                pe.transpose(prt[:, 1, :], rt[:, P:2 * P], ident[0:C, 0:C]).then_inc(rtr_done, 1)

            def body(q, par, r):
                pe.wait_ge(xn_done, q + 1)
                for j in range(2):
                    if not static(q, 0):
                        pe.wait_ge(xt_done, q * 2 + j - 1)
                    for k in range(KD):
                        tr = pe.transpose(pt[j][:, k, :], xin[par][:, j, k * P:(k + 1) * P], ident[:, :])
                    tr.then_inc(tr_done, 1)
                if not static(q, 0):
                    project(q - 1, 1 - par)

            by_twos(pe, NQ, body)
            project(NQ - 1, 1)

            def decay_rows(k):
                if k:
                    pe.wait_ge(ct_copied, k)
                for j in range(4):
                    tr = pe.transpose(pct[:, j, :], cs_tok[:, 4 * k + j, :], ident[:, :])
                tr.then_inc(ct_done, 1)

            pe.wait_ge(picks_done, 1)
            pe.matmul(ppos[:, :, :].rearrange("p t e -> p (t e)"), stri_b[:, :],
                      picks[:, :, :].rearrange("p t e -> p (t e)"), start=True, stop=False)
            pe.matmul(ppos[:, :, :].rearrange("p t e -> p (t e)"), ones_b[:, :],
                      earlier[:, :, :].rearrange("p t e -> p (t e)"), start=False, stop=True)
            for t in range(T):
                mm = pe.matmul(ptot[:, 0:E], ones_b[:, :], picks[:, t, :], start=t == 0, stop=t == T - 1)
            mm.then_inc(pos_done, 1)
            pe.wait_ge(decay_done, 1)
            pe.matmul(pcs[:, :, :].rearrange("p t h -> p (t h)"), tri[:, :],
                      big[2][:, :, :].rearrange("p t h -> p (t h)"), start=True, stop=True).then_inc(cs_ready, 1)
            pe.wait_ge(cs_copied, 1)
            for k in range(4):
                decay_rows(k)
            pe.wait_ge(who_done, 1)
            for n in range(2 * T):
                mm = pe.matmul(ptok[:, 0:2 * J], place[:, n, :], who[:, n, :], start=n == 0, stop=n == 2 * T - 1)
            mm.then_inc(tok_done, 1)

        front.rows_stored, front.idx_done, front.cs_out = rows_stored, idx_done, cs_out
        return {"sync": sync, "gpsimd": gpsimd, "scalar": scalar, "vector": vector, "tensor": tensor}


def experts(nc, area, sem, w_in, win_stage, stage_in, xn_d, y_d, ident, idx, eidx, packed, guh, gul, dh, dl, front_done):
    with ExitStack() as ctx:
        sb = area

        def pb(name, shape):
            return ctx.enter_context(nc.psum_tensor(name, shape, F32))

        xg = [sb(f"xg{i}", [P, D]) for i in range(2)]
        xgh = [sb(f"xgh{i}", [P, KD, P], F32R) for i in range(2)]
        xgl = [sb(f"xgl{i}", [P, KD, P], F32R) for i in range(2)]
        ic = [sb(f"ic{i}", [P, 1], U32) for i in range(2)]
        th = sb("th", [P, F])
        hg = sb("hg", [P, F])
        h = sb("h", [P, F])
        hh = [sb(f"hh{i}", [FH, 2, P], F32R) for i in range(2)]
        hl = [sb(f"hl{i}", [FH, 2, P], F32R) for i in range(2)]
        yo = [sb(f"yo{i}", [P, D]) for i in range(2)]
        px = [pb(f"px{i}", [P, KD, P]) for i in range(2)]
        pg = [pb(f"pg{i}", [P, 2 * F]) for i in range(2)]
        ph = [pb(f"ph{i}", [FH, 2, P]) for i in range(2)]
        pd = [pb(f"pd{i}", [P, D]) for i in range(2)]

        ic_done = sem("ic_done")
        ic_ready = sem("ic_ready")
        xg_in = [sem(f"xg_in{i}") for i in range(2)]
        xtr = sem("xtr")
        x_hi = sem("x_hi")
        x_lo = sem("x_lo")
        gu = sem("gu")
        th_done = sem("th_done")
        hg_done = sem("hg_done")
        h_done = sem("h_done")
        htr = sem("htr")
        h_hi = sem("h_hi")
        h_lo = sem("h_lo")
        down = sem("down")
        y_done = sem("y_done")
        y_out = [sem(f"y_out{i}") for i in range(2)]
        y_t = y_d.rearrange("(j p) d -> j p d", p=P)

        def sync(sp):
            sp.wait_ge(front_done, 1)

            def body(j, par, r):
                sp.wait_ge(y_done, j + 1 + CR)
                sp.dma_start(y_t[j], yo[par][:, :]).then_inc(y_out[par], 16)
                if static(j, 0):
                    for k in range(PRE):
                        sp.dma_start(win_stage[:, k, :], w_in[:, k, :]).then_inc(stage_in, 16)

            by_twos(sp, J, body, 2)
            for i in range(2):
                sp.wait_ge(y_out[i], 16 * ((J + 1 - i) // 2) + 16)

        def gpsimd(pool):
            pool.wait_ge(front.rows_stored, 1)
            pool.wait_ge(front.idx_done, 1)
            pool.wait_ge(front_done, 1)

            def body(j, par, r):
                pool.wait_ge(xtr, j + CR - 1) if not static(j, 0) else None
                pool.tensor_copy(ic[par][:, :], idx[:, bass.ds(j, 1)]).then_inc(ic_done, 1)
                pool.wait_ge(ic_done, j + 1)
                pool.sem_inc(ic_ready, 1)
                pool.indirect_dma_start(xg[par][:, :], None, xn_d,
                                        bass.IndirectOffsetOnAxis(ap=ic[par][:, 0:1], axis=0)).then_inc(xg_in[par], 16)

            by_twos(pool, J, body, 2)

        def scalar(act):
            act.sem_inc(y_done, CR)

            def high(j, par):
                act.wait_ge(xtr, j + 1 + CR)
                act.copy(xgh[par][:, :, :], px[par][:, :, :]).then_inc(x_hi, 1)

            def result(j, par, r):
                act.wait_ge(down, j + 1 + CR)
                act.wait_ge(y_out[par], r * 16 + 16)
                act.copy(yo[par][:, :], pd[par][:, :]).then_inc(y_done, 1)

            def body(j, par, r):
                act.wait_ge(gu, j + 1)
                act.wait_ge(hg_done, j + CR)
                act.activation(th[:, :], pg[par][:, 0:F], ACT.Tanh, scale=0.5).then_inc(th_done, 1)
                if not static(j, J - 2, J - 1):
                    high(j + 2, par)
                if not static(j, 0):
                    result(j - 1, 1 - par, r - 1 + par)
                act.wait_ge(htr, j + 1)
                act.copy(hh[par][:, :, :], ph[par][:, :, :]).then_inc(h_hi, 1)

            high(0, 0)
            high(1, 1)
            by_twos(act, J, body, 2)
            result(J - 1, (J - 1) % 2, (J - 1) // 2)

        def vector(dve):
            dve.wait_ge(front.cs_out, 16)
            dve.sem_inc(front_done, 1)
            for s in (hg_done, x_lo):
                dve.sem_inc(s, CR)
            dve.sem_inc(h_lo, 2)
            dve.sem_inc(h_done, 2)
            for i in range(2):
                dve.sem_inc(y_out[i], 16)

            def low(j, par):
                dve.wait_ge(x_hi, j + 1)
                dve.tensor_tensor(xgl[par][:, :, :], px[par][:, :, :], xgh[par][:, :, :].bitcast(F32),
                                  ALU.subtract).then_inc(x_lo, 1)

            def body(j, par, r):
                dve.wait_ge(th_done, j + 1)
                dve.scalar_tensor_tensor(out=hg[:, :], in0=th[:, :], scalar=1.0, in1=pg[par][:, 0:F],
                                         op0=ALU.add, op1=ALU.mult).then_inc(hg_done, 1)
                dve.wait_ge(hg_done, j + 1 + CR)
                dve.wait_ge(htr, j) if not static(j, 0) else None
                dve.tensor_tensor(h[:, :], hg[:, :], pg[par][:, F:2 * F], ALU.mult).then_inc(h_done, 1)
                if not static(j, J - 2, J - 1):
                    low(j + 2, par)
                dve.wait_ge(h_hi, j + 1)
                dve.tensor_tensor(hl[par][:, :, :], ph[par][:, :, :], hh[par][:, :, :].bitcast(F32),
                                  ALU.subtract).then_inc(h_lo, 1)

            low(0, 0)
            low(1, 1)
            by_twos(dve, J, body, 2)

        def tensor(pe):
            pe.sem_inc(xtr, CR)
            pe.sem_inc(down, CR)
            pe.wait_ge(front_done, 1)

            def turn(j, par, r):
                pe.wait_ge(xg_in[par], r * 16 + 16)
                pe.wait_ge(x_lo, j - 1 + CR) if not static(j, 0) else None
                for k in range(KD):
                    tr = pe.transpose(px[par][:, k, :], xg[par][:, k * P:(k + 1) * P], ident[:, :])
                tr.then_inc(xtr, 1)

            def of(ww, e, k):
                return ww[:, bass.ds(e, 1), k, :].rearrange("p e n -> p (e n)")

            def gate_up(j, par, e):
                pe.wait_ge(x_lo, j + 1 + CR)
                pe.wait_ge(h_done, j + 1)
                n = 0
                for xx, ww in ((xgh, guh), (xgh, gul), (xgl, guh)):
                    for k in range(KD):
                        mm = pe.matmul(pg[par][:, :], xx[par][:, k, :], of(ww, e, k), start=n == 0, stop=n == 11)
                        n += 1
                mm.then_inc(gu, 1)

            def down_product(j, par, e):
                pe.wait_ge(h_lo, j + 3)
                pe.wait_ge(y_done, j - 1 + CR) if not static(j, 0) else None
                n = 0
                for xx, ww in ((hh, dh), (hh, dl), (hl, dh)):
                    for k in range(2):
                        mm = pe.matmul(pd[par][:, :], xx[par][:, k, :], of(ww, e, k), start=n == 0, stop=n == 5)
                        n += 1
                mm.then_inc(down, 1)

            def turn_hidden(j, par):
                pe.wait_ge(h_done, j + 3)
                pe.wait_ge(h_lo, j + 1)
                for k in range(2):
                    tr = pe.transpose(ph[par][:, k, :], h[:, k * FH:(k + 1) * FH], ident[:, :])
                tr.then_inc(htr, 1)

            def expert_of(j):
                return pe.value_load(eidx[0:1, bass.ds(j, 1)], min_val=0, max_val=E - 1)

            def body(j, par, r):
                if static(j, 0):
                    following = expert_of(1)
                elif static(j, J - 2):
                    before, following = expert_of(j - 1), expert_of(j + 1)
                elif static(j, J - 1):
                    before = expert_of(j - 1)
                elif par == 1:
                    both[:] = [pe.value_load(packed[0:1, bass.ds(r, 1)], min_val=0, max_val=E ** 4 - 1)]
                    before, following = both[0] & (E - 1), (both[0] >> 6) & (E - 1)
                else:
                    before, following = (both[0] >> 3) & (E - 1), (both[0] >> 9) & (E - 1)
                if not static(j, J - 2, J - 1):
                    turn(j + 2, par, r + 1)
                if not static(j, 0):
                    down_product(j - 1, 1 - par, before)
                turn_hidden(j, par)
                if not static(j, J - 1):
                    gate_up(j + 1, 1 - par, following)

            both = []
            first = expert_of(0)
            turn(0, 0, 0)
            turn(1, 1, 0)
            gate_up(0, 0, first)
            by_twos(pe, J, body, 2)
            down_product(J - 1, (J - 1) % 2, expert_of(J - 1))

        return {"sync": sync, "gpsimd": gpsimd, "scalar": scalar, "vector": vector, "tensor": tensor}


def mamba(nc, area, stage_at, win_stage, stage_in, sem, x, w_in, w_out_in, conv_w_in, conv_b_in, d_skip_in, norm_w_in,
          xt_d, cs_d, y_d, ident, tri, cs_tok, dt_tok, slot_u, prob, out):
    NX, NZ = CB // 2, XB // 2
    PAIRS = ((True, 0), (True, 1), (True, 2), (False, 0), (True, 3), (True, 4), (False, 1), (False, 2), (False, 3))
    NP = len(PAIRS)
    assert NP == NX + NZ
    TAKEN = ((0, 1, 2, 3), (4, 5, 6, 7, 8))
    with ExitStack() as ctx:
        sb = area

        def pb(name, shape):
            return ctx.enter_context(nc.psum_tensor(name, shape, F32))

        wlast = sb("wlast", [P, (CB + XB) * P])
        wraw = [win_stage[:, k, :] for k in range(KD - 1)] + [wlast[:, :]]
        over = Area(nc, stage_at, sb.at)
        m = [over(f"m{i}", [P, HEADS, P]) for i in range(2)]
        xdt = over("xdt", [P, XB, 2, HD])
        xdd = over("xdd", [P, XB, 2, HD])
        y = over("y", [P, XB, P])
        ysq = over("ysq", [P, XB, P])
        xl1 = over("xl1", [P, KD, GT], F32R)
        wh = sb("wh", [P, KD, (CB + XB) * P], F32R)
        wl = sb("wl", [P, KD, (CB + XB) * P], F32R)
        wo = sb("wo", [P, XB, D])
        conv_w = sb("conv_w", [P, CB, TAPS])
        conv_b = sb("conv_b", [P, CB])
        d_skip = sb("d_skip", [P, XB])
        norm_w = sb("norm_w", [P, XB])
        ones = sb("ones", [P, 1])
        nhalf = sb("nhalf1", [P, 1])
        xh = [sb(f"xh{i}", [P, KD, GT], F32R) for i in range(2)]
        xl = [sb("xl0", [P, KD, GT], F32R), xl1]
        HALO = TAPS - 1
        raw = sb("raw", [P, CB, HALO + GT])
        xs = [sb(f"xs{i}", [P, CB, GT]) for i in range(2)]
        zs = [sb(f"zs{i}", [P, XB, GT]) for i in range(2)]
        tx = [sb(f"tx{i}", [P, 2, GT]) for i in range(2)]
        e2 = sb("e2", [P, XB, P])
        cst = [sb(f"cst{i}", [P, HEADS]) for i in range(2)]
        dec = [sb(f"dec{i}", [P, HEADS]) for i in range(2)]
        cd = [sb(f"cd{i}", [P, HEADS]) for i in range(2)]
        btok = sb("btok", [P, P])
        cbm = sb("cbm", [P, P])
        carry = sb("carry", [P, XB, 2, HD])
        var = sb("var", [P, 1])
        rstd = sb("rstdy", [P, 1])
        res = sb("res", [P, D])
        ya = [sb(f"ya{i}", [P, D]) for i in range(2)]
        pwt = sb("pwt", [P, 2])
        sidx = sb("sidx", [P, 2], U32)
        o = sb("o", [P, D])
        pi = [pb(f"pi{i}", [P, 2, GT]) for i in range(2)]
        pxb = [pb(f"pxb{i}", [P, 4, P]) for i in range(2)]
        py = [pb(f"py{i}", [P, 4, P]) for i in range(2)]
        pk = pb("pk", [P, 4, P])
        po = pb("po", [P, D])

        w_in_s = [sem(f"w_in_s{k}") for k in range(PRE, KD)]
        w_hi = sem("w_hi")
        w_lo = sem("w_lo")
        c_in = sem("c_in")
        prep = sem("prep")
        nh_done = sem("nh_done_m")
        xg_in = [sem(f"xt_in{i}") for i in range(2)]
        xh_done = sem("xh_done")
        xl_done = sem("xl_done")
        bc_in = [sem(f"bc_in{i}") for i in range(2)]
        e2_in = sem("e2_in")
        res_in = sem("res_in")
        ya_in = [sem(f"ya_in{i}") for i in range(2)]
        sidx_done = sem("sidx_done")
        sidx_ready = sem("sidx_ready")
        pw_done = sem("pw_done")
        ra_done = sem("ra_done")
        in_full = sem("in_full")
        inx_free = sem("inx_free")
        tz_done = sem("tz_done")
        inz_free = sem("inz_free")
        halo = sem("halo")
        tap = sem("tap")
        ctap = sem("ctap")
        txd = sem("txd")
        xs_done = sem("xs_done")
        btr = sem("btr")
        btok_done = sem("btok_done")
        xtr = sem("xtr_m")
        xdt_done = sem("xdt_done")
        cst_done = sem("cst_done")
        dsub = sem("dsub")
        dec_done = sem("dec_done")
        seg = sem("seg")
        me = sem("me")
        e2_done = sem("e2_done")
        cbt = sem("cbt")
        cbm_done = sem("cbm_done")
        m_done = sem("m_done")
        xdd_done = sem("xdd_done")
        st = sem("st")
        yoff = sem("yoff")
        ydiag = sem("ydiag")
        ye = sem("ye")
        yd = sem("yd")
        cdec = sem("cdec")
        cadd = sem("cadd")
        yadd = sem("yadd")
        ygate = sem("ygate")
        ysqd = sem("ysqd")
        tree = sem("tree")
        op = sem("op")
        ss = sem("ss")
        var_done = sem("var_done")
        rstd_done = sem("rstd_done_m")
        res_done = sem("res_done")
        o_done = sem("o_done")
        o_out = sem("o_out")
        block = ctx.enter_context(nc.Block())
        out_t = out.rearrange("(t p) d -> t p d", p=P)
        x_t = x.rearrange("(t p) d -> t p d", p=P)

        def groups(eng, body):
            by_twos(eng, G, lambda g, par, r: body(g, par))

        @block.sync
        def _(sp):
            for k in range(PRE, KD):
                sp.dma_start(wraw[k], w_in[:, k, :]).then_inc(w_in_s[k - PRE], 16)
            sp.dma_start(conv_w[:, :, :], conv_w_in).then_inc(c_in, 16)
            sp.dma_start(conv_b[:, :], conv_b_in).then_inc(c_in, 16)
            sp.dma_start(d_skip[:, :], d_skip_in).then_inc(c_in, 16)
            sp.dma_start(norm_w[:, :], norm_w_in).then_inc(c_in, 16)

            def load_x(g, par):
                sp.dma_start(xl[par][:, :, :].bitcast(F32), xt_d[g]).then_inc(xg_in[par], 16)

            def load_decays(t, c):
                sp.dma_start(m[c][:, :, :], cs_d[t].unsqueeze(0).broadcast_to([P, HEADS, P])).then_inc(bc_in[c], 16)

            def load_decays2(t):
                for half in range(2):
                    sp.dma_start(e2[half * HD:(half + 1) * HD, :, :],
                                 cs_d[t][half * XB:(half + 1) * XB, :].unsqueeze(0).broadcast_to([HD, XB, P])
                                 ).then_inc(e2_in, 16)

            def store(t):
                sp.wait_ge(o_done, t + 1 + CR)
                sp.dma_start(out_t[t], o[:, :]).then_inc(o_out, 16)

            load_x(0, 0)
            sp.dma_start(wo[:, :, :], w_out_in).then_inc(c_in, 16)
            sp.wait_ge(w_lo, KD)
            load_decays(0, 0)
            load_x(1, 1)

            def body(g, par):
                for c in range(2):
                    t = g * 2 + c
                    if not static(t, T - 1):
                        sp.wait_ge(ydiag, t * 2 + CR)
                        load_decays(t + 1, 1 - c)
                    if c == 0 and not static(g, G - 2, G - 1):
                        sp.wait_ge(in_full, g * NP + NP + CR)
                        load_x(g + 2, par)
                    elif c == 0 and static(g, G - 2):
                        sp.wait_ge(in_full, g * NP + NP + CR)
                        sp.sem_inc(xg_in[par], 16)
                    sp.wait_ge(yadd, t + CR)
                    load_decays2(t)
                    if not static(t, 0):
                        store(t - 1)
                    sp.dma_start(res[:, :], x_t[t]).then_inc(res_in, 16)

            body(0, 0)
            body(1, 1)
            with sp.Fori(0, (G - 4) // 2) as i:
                body(i * 2 + 2, 0)
                body(i * 2 + 3, 1)
            body(G - 2, 0)
            body(G - 1, 1)
            store(T - 1)
            sp.wait_ge(o_out, 16 * T + 16)

        @block.gpsimd
        def _(pool):
            for s in (yadd, ygate, xdd_done, cdec, rstd_done):
                pool.sem_inc(s, CR)
            pool.sem_inc(tree, 3)
            pool.memset(nhalf[:, :], -0.5).then_inc(nh_done, 1)
            pool.wait_ge(nh_done, 1)

            def sums(t):
                pool.wait_ge(ysqd, t + 1 + CR)
                pool.tensor_tensor(ysq[:, 0:4, :], ysq[:, 0:4, :], ysq[:, 4:8, :], ALU.add).then_inc(tree, 1)
                pool.wait_ge(tree, t * 3 + 4)
                pool.tensor_tensor(ysq[:, 0:2, :], ysq[:, 0:2, :], ysq[:, 2:4, :], ALU.add).then_inc(tree, 1)
                pool.wait_ge(tree, t * 3 + 5)
                pool.tensor_tensor(ysq[:, 0:1, :], ysq[:, 0:1, :], ysq[:, 1:2, :], ALU.add).then_inc(tree, 1)

            def factor(t):
                pool.wait_ge(var_done, t + 1 + CR)
                pool.wait_ge(o_done, t + CR)
                pool.tensor_tensor(rstd[:, :], var[:, :], nhalf[:, :], ALU.pow).then_inc(rstd_done, 1)

            def body(g, par):
                for c in range(2):
                    t = g * 2 + c
                    first = static(t, 0)
                    pool.wait_ge(xdt_done, t * 2 + 2 + CR)
                    pool.wait_ge(dec_done, t + 1 + CR)
                    pool.wait_ge(st, t + CR)
                    pool.tensor_tensor(xdd[:, :, :, :], xdt[:, :, :, :],
                                       dec[c][:, :].rearrange("p (a b) -> p b a", a=2).unsqueeze(3)
                                       .broadcast_to([P, XB, 2, HD]), ALU.mult).then_inc(xdd_done, 1)
                    if not first:
                        sums(t - 1)
                    if not first:
                        pool.wait_ge(res_done, t + CR)
                    pool.tensor_copy(sidx[:, :], slot_u[:, :, bass.ds(t, 1)].rearrange("p k t -> p (k t)")
                                     ).then_inc(sidx_done, 1)
                    pool.wait_ge(sidx_done, t + 1)
                    pool.sem_inc(sidx_ready, 1)
                    for n in range(2):
                        pool.indirect_dma_start(ya[n][:, :], None, y_d, bass.IndirectOffsetOnAxis(ap=sidx[:, n:n + 1], axis=0)
                                                ).then_inc(ya_in[n], 16)
                    if not first:
                        factor(t - 1)
                    pool.wait_ge(yoff, t * 2 + 2 + CR)
                    pool.wait_ge(cadd, t * 2 + CR)
                    pool.tensor_tensor(carry[:, :, :, :], carry[:, :, :, :],
                                       cd[c][:, :].rearrange("p (a b) -> p b a", a=2).unsqueeze(3)
                                       .broadcast_to([P, XB, 2, HD]), ALU.mult).then_inc(cdec, 1)
                    pool.wait_ge(yd, t * 2 + 2 + CR)
                    pool.wait_ge(ye, t * 2 + 2 + CR)
                    pool.tensor_tensor(y[:, :, :], y[:, :, :], e2[:, :, :], ALU.add).then_inc(yadd, 1)
                    pool.wait_ge(yadd, t + 1 + CR)
                    pool.wait_ge(inz_free, g * NZ + NZ + CR)
                    pool.tensor_tensor(y[:, :, :], y[:, :, :], zs[par][:, :, c * P:(c + 1) * P],
                                       ALU.mult).then_inc(ygate, 1)

            groups(pool, body)
            sums(T - 1)
            factor(T - 1)

        def stage_act(act, g, n, par):
            convolved, i = PAIRS[n]
            act.wait_ge(in_full, g * NP + n + 1 + CR)
            if convolved:
                if i == 0:
                    act.wait_ge(ctap, g * (3 * CB) + CR)
                    act.copy(raw[:, :, 0:HALO], raw[:, :, GT:GT + HALO]).then_inc(halo, 1)
                    act.wait_ge(halo, g + 1)
                act.copy(raw[:, 2 * i:2 * i + 2, HALO:HALO + GT], pi[n % 2][:, :, :]).then_inc(inx_free, 1)
                act.wait_ge(inx_free, g * NX + i + 1 + CR)
                for b in (2 * i, 2 * i + 1):
                    act.activation(xs[par][:, b, :], raw[:, b, 0:GT], ACT.Identity, bias=conv_b[:, b:b + 1],
                                   scale=conv_w[:, b, 0:1]).then_inc(tap, 1)
            else:
                act.activation(zs[par][:, 2 * i:2 * i + 2, :], pi[n % 2][:, :, :], ACT.Tanh, scale=0.5
                               ).then_inc(tz_done, 1)
            convolved, i = PAIRS[n - 1]
            if n and convolved:
                act.wait_ge(ctap, g * (3 * CB) + 6 * i + 6 + CR)
                if i >= 2 or not static(g, 0):
                    act.wait_ge(xs_done, g * NX + i - 1 + CR)
                act.activation(tx[i % 2][:, :, :], xs[par][:, 2 * i:2 * i + 2, :], ACT.Tanh).then_inc(txd, 1)

        def stage_dve(dve, g, n, par):
            convolved, i = PAIRS[n]
            if convolved:
                for k in range(1, TAPS):
                    for b in (2 * i, 2 * i + 1):
                        if k == 1:
                            dve.wait_ge(tap, g * CB + b + 1)
                        else:
                            dve.wait_ge(ctap, g * (3 * CB) + 6 * i + 2 * (k - 1) + (b - 2 * i) - 1 + CR)
                        dve.scalar_tensor_tensor(out=xs[par][:, b, :], in0=raw[:, b, k:k + GT],
                                                 scalar=conv_w[:, b, k:k + 1], in1=xs[par][:, b, :],
                                                 op0=ALU.mult, op1=ALU.add).then_inc(ctap, 1)
            else:
                dve.wait_ge(tz_done, g * NZ + i + 1)
                zz = zs[par][:, 2 * i:2 * i + 2, :]
                dve.scalar_tensor_tensor(out=zz, in0=zz, scalar=1.0, in1=pi[n % 2][:, :, :],
                                         op0=ALU.add, op1=ALU.mult).then_inc(inz_free, 1)
            convolved, i = PAIRS[n - 1]
            if n and convolved:
                dve.wait_ge(txd, g * NX + i + 1)
                xx = xs[par][:, 2 * i:2 * i + 2, :]
                dve.scalar_tensor_tensor(out=xx, in0=tx[i % 2][:, :, :], scalar=1.0, in1=xx, op0=ALU.add,
                                         op1=ALU.mult).then_inc(xs_done, 1)

        def split_act(act, g, par, r):
            act.wait_ge(xg_in[par], r * 16 + 16)
            act.copy(xh[par][:, :, :], xl[par][:, :, :].bitcast(F32)).then_inc(xh_done, 1)

        def split_dve(dve, g, par):
            dve.wait_ge(xh_done, g + 1)
            dve.tensor_tensor(xl[par][:, :, :], xl[par][:, :, :].bitcast(F32), xh[par][:, :, :].bitcast(F32),
                              ALU.subtract).then_inc(xl_done, 1)

        def stage_pe(pe, g, n, par):
            convolved, i = PAIRS[n]
            if n == 0:
                pe.wait_ge(xl_done, g + 1)
            if n >= 2:
                conv2, i2 = PAIRS[n - 2]
                pe.wait_ge(inx_free, g * NX + i2 + 1 + CR) if conv2 else pe.wait_ge(inz_free, g * NZ + i2 + 1 + CR)
            elif not static(g, 0):
                pe.wait_ge(inz_free, g * NZ - n + CR)
            for h in range(2):
                at = (2 * i + h + (0 if convolved else CB)) * P
                k3 = 0
                for ww, xx in ((wh, xh[par]), (wl, xh[par]), (wh, xl[par])):
                    for k in range(KD):
                        mm = pe.matmul(pi[n % 2][:, h, :], ww[:, k, at:at + P], xx[:, k, :], start=k3 == 0, stop=k3 == 11)
                        k3 += 1
            mm.then_inc(in_full, 1)

        @block.scalar
        def _(act):
            for s in (inx_free, btok_done, dec_done, me, e2_done, ysqd):
                act.sem_inc(s, CR)
            for k in range(KD):
                act.wait_ge(stage_in, 16 * PRE) if k < PRE else act.wait_ge(w_in_s[k - PRE], 16)
                act.copy(wh[:, k, :], wraw[k]).then_inc(w_hi, 1)
            split_act(act, 0, 0, 0)
            act.wait_ge(prep, 4)

            def decay_factors(t, c):
                act.wait_ge(dsub, t + 1)
                if not static(t, 0):
                    act.wait_ge(cdec, t - 1 + CR)
                act.activation(dec[c][:, :], dec[c][:, :], ACT.Exp)
                act.activation(cd[c][:, :], m[c][:, :, P - 1], ACT.Exp).then_inc(dec_done, 1)
                act.wait_ge(dec_done, t + 1 + CR)

            def kernel_part(t, c, part, parts):
                for h in range(HEADS * part // parts, HEADS * (part + 1) // parts):
                    act.activation(m[c][:, h, :], m[c][:, h, :], ACT.Relu, bias=cst[c][:, h:h + 1],
                                   scale=-1.0).then_inc(seg, 1)
                if part == parts - 1:
                    act.wait_ge(seg, t * HEADS + HEADS)
                    act.activation(m[c][:, :, :], m[c][:, :, :], ACT.Exp, scale=-1.0).then_inc(me, 1)

            def square(t):
                act.wait_ge(ygate, t + 1 + CR)
                act.wait_ge(ss, t + CR)
                act.activation(ysq[:, :, :], y[:, :, :], ACT.Square).then_inc(ysqd, 1)

            for n in range(NP):
                stage_act(act, 0, n, 0)
                if n == 3:
                    split_act(act, 1, 1, 0)
                    decay_factors(0, 0)
                if n > 3:
                    kernel_part(0, 0, n - 4, NP - 4)

            def body(g, par, r):
                for c in range(2):
                    t = g * 2 + c
                    taken = TAKEN[c] if not static(g, G - 1) else ()
                    more = not static(t, T - 1)
                    act.wait_ge(btr, t + 1)
                    act.wait_ge(st, t + CR)
                    act.copy(btok[:, :], pk[:, 0, :]).then_inc(btok_done, 1)
                    for n in taken[:1]:
                        stage_act(act, g + 1, n, 1 - par)
                    act.wait_ge(e2_in, t * 32 + 32)
                    act.activation(e2[:, :, :], e2[:, :, :], ACT.Exp).then_inc(e2_done, 1)
                    if more:
                        decay_factors(t + 1, 1 - c)
                        kernel_part(t + 1, 1 - c, 0, 4)
                    if not static(t, 0):
                        square(t - 1)
                    for n in taken[1:2]:
                        stage_act(act, g + 1, n, 1 - par)
                    if more:
                        kernel_part(t + 1, 1 - c, 1, 4)
                        kernel_part(t + 1, 1 - c, 2, 4)
                    for n in taken[2:3]:
                        stage_act(act, g + 1, n, 1 - par)
                    if more:
                        kernel_part(t + 1, 1 - c, 3, 4)
                    if c == 1 and taken:
                        split_act(act, g + 2, par, r + 1)
                    for n in taken[3:]:
                        stage_act(act, g + 1, n, 1 - par)

            by_twos(act, G, body)
            square(T - 1)

        @block.vector
        def _(dve):
            for s in (inz_free, xs_done, xdt_done, cbm_done, m_done, ye, yd, cadd, var_done, o_done, ctap, res_done):
                dve.sem_inc(s, CR)
            dve.sem_inc(o_out, 16)
            dve.memset(ones[:, :], 1.0).then_inc(prep, 1)
            dve.memset(carry[:, :, :, :], 0.0).then_inc(prep, 1)
            for k in range(KD):
                dve.wait_ge(w_hi, k + 1)
                dve.tensor_tensor(wl[:, k, :], wraw[k], wh[:, k, :].bitcast(F32), ALU.subtract).then_inc(w_lo, 1)
            split_dve(dve, 0, 0)
            dve.memset(raw[:, :, GT:GT + HALO], 0.0).then_inc(prep, 1)
            dve.wait_ge(c_in, 80)
            dve.tensor_scalar(conv_w[:, :, :], conv_w[:, :, :], 0.5, None, ALU.mult)
            dve.tensor_scalar(conv_b[:, :], conv_b[:, :], 0.5, None, ALU.mult).then_inc(prep, 1)

            def decay_differences(t, g, c):
                dve.wait_ge(bc_in[c], g * 16 + 16)
                if not static(t, 0):
                    dve.wait_ge(me, t - 1 + CR)
                    dve.wait_ge(xdd_done, t - 1 + CR)
                dve.tensor_copy(cst[c][:, :], cs_tok[:, bass.ds(t, 1), :].rearrange("p t h -> p (t h)")
                                ).then_inc(cst_done, 1)
                dve.wait_ge(cst_done, t + 1)
                dve.tensor_tensor(dec[c][:, :], m[c][:, :, P - 1], cst[c][:, :], ALU.subtract).then_inc(dsub, 1)

            for n in range(NP):
                stage_dve(dve, 0, n, 0)
                if n == 1:
                    decay_differences(0, 0, 0)
                if n == 4:
                    split_dve(dve, 1, 1)
            for b in range(XB):
                ins = dve.tensor_scalar(wo[:, b, :], wo[:, b, :], norm_w[:, b:b + 1], 0.5, ALU.mult, ALU.mult)
            ins.then_inc(prep, 1)

            def body(g, par):
                for c in range(2):
                    t = g * 2 + c
                    tok = slice(c * P, (c + 1) * P)
                    first = static(t, 0)
                    taken = TAKEN[c] if not static(g, G - 1) else ()

                    def decayed(half):
                        blocks = slice(4 * half, 4 * half + 4)
                        dve.wait_ge(yoff, t * 2 + half + 1 + CR)
                        dve.wait_ge(e2_done, t + 1 + CR)
                        dve.tensor_tensor(e2[:, blocks, :], py[0][:, :, :], e2[:, blocks, :], ALU.mult).then_inc(ye, 1)

                    def own(half):
                        dve.wait_ge(ydiag, t * 2 + half + 1 + CR)
                        if half == 0:
                            dve.wait_ge(op, t + CR)
                            dve.wait_ge(ysqd, t + CR)
                        for b in range(4 * half, 4 * half + 4):
                            ins = dve.scalar_tensor_tensor(
                                out=y[:, b, :], in0=xs[par][:, b, tok], scalar=d_skip[:, b:b + 1],
                                in1=py[1][:, b - 4 * half, :], op0=ALU.mult, op1=ALU.add)
                        ins.then_inc(yd, 1)

                    dve.wait_ge(ydiag, t * 2 + CR)
                    for half in range(2):
                        dve.wait_ge(xtr, t * 2 + half + 1)
                        dve.tensor_tensor(
                            xdt[:, 4 * half:4 * half + 4, :, :],
                            pxb[half][:, :, :].rearrange("p b (a d) -> p b a d", a=2),
                            dt_tok[:, bass.ds(t, 1), :].rearrange("p t (a b) -> p (t b) a", a=2)
                            [:, 4 * half:4 * half + 4, :].unsqueeze(3).broadcast_to([P, 4, 2, HD]),
                            ALU.mult).then_inc(xdt_done, 1)
                    dve.wait_ge(cbt, t + 1)
                    dve.tensor_tensor(cbm[:, :], pk[:, 1, :], tri[:, :], ALU.mult).then_inc(cbm_done, 1)
                    dve.wait_ge(me, t + 1 + CR)
                    dve.wait_ge(cbm_done, t + 1 + CR)
                    dve.tensor_tensor(m[c][:, :, :], m[c][:, :, :],
                                      cbm[:, :].unsqueeze(1).broadcast_to([P, HEADS, P]), ALU.mult).then_inc(m_done, 1)
                    if not static(t, T - 1):
                        decay_differences(t + 1, g + c, 1 - c)
                    if not first:
                        residual(t - 1)
                    for n in taken[:2]:
                        stage_dve(dve, g + 1, n, 1 - par)
                    if not first:
                        variance(t - 1)
                    decayed(0)
                    if not first:
                        finish(t - 1)
                    decayed(1)
                    own(0)
                    for n in taken[2:3]:
                        stage_dve(dve, g + 1, n, 1 - par)
                    if c == 1 and taken:
                        split_dve(dve, g + 2, par)
                    own(1)
                    dve.wait_ge(cdec, t + 1 + CR)
                    for half in range(2):
                        dve.wait_ge(st, t + 1 + CR)
                        sl = carry[:, 4 * half:4 * half + 4, :, :].rearrange("p b a d -> p (b a d)")
                        dve.tensor_tensor(sl, pxb[half][:, :, :].rearrange("p b l -> p (b l)"), sl,
                                          ALU.add).then_inc(cadd, 1)
                    for n in taken[3:4]:
                        stage_dve(dve, g + 1, n, 1 - par)
                    for n in taken[4:]:
                        stage_dve(dve, g + 1, n, 1 - par)

            def residual(t):
                if not static(t, 0):
                    dve.wait_ge(res_done, t + CR)
                dve.tensor_copy(pwt[:, :], prob[:, :, bass.ds(t, 1)].rearrange("p k t -> p (k t)")
                                ).then_inc(pw_done, 1)
                dve.wait_ge(pw_done, t + 1)
                dve.wait_ge(res_in, t * 16 + 16)
                dve.wait_ge(ya_in[0], t * 16 + 16)
                dve.scalar_tensor_tensor(out=res[:, :], in0=ya[0][:, :], scalar=pwt[:, 0:1], in1=res[:, :],
                                         op0=ALU.mult, op1=ALU.add).then_inc(ra_done, 1)
                dve.wait_ge(ra_done, t + 1)
                dve.wait_ge(ya_in[1], t * 16 + 16)
                dve.scalar_tensor_tensor(out=res[:, :], in0=ya[1][:, :], scalar=pwt[:, 1:2], in1=res[:, :],
                                         op0=ALU.mult, op1=ALU.add).then_inc(res_done, 1)

            def variance(t):
                dve.wait_ge(ss, t + 1 + CR)
                dve.tensor_scalar(var[:, :], pk[:, 2, 0:1], 0.25 / INNER, EPS, ALU.mult, ALU.add).then_inc(var_done, 1)

            def finish(t):
                dve.wait_ge(rstd_done, t + 1 + CR)
                dve.wait_ge(op, t + 1 + CR)
                dve.wait_ge(res_done, t + 1 + CR)
                dve.wait_ge(o_out, t * 16 + 16)
                dve.scalar_tensor_tensor(out=o[:, :], in0=po[:, :], scalar=rstd[:, 0:1], in1=res[:, :],
                                         op0=ALU.mult, op1=ALU.add).then_inc(o_done, 1)

            groups(dve, body)
            residual(T - 1)
            variance(T - 1)
            finish(T - 1)

        @block.tensor
        def _(pe):
            for s in (in_full, st, yoff, ydiag, op, ss):
                pe.sem_inc(s, CR)
            pe.wait_ge(w_lo, KD)
            for n in range(NP):
                stage_pe(pe, 0, n, 0)
            pe.wait_ge(prep, 5)

            def project(t):
                pe.wait_ge(ygate, t + 1 + CR)
                pe.wait_ge(o_done, t + CR)
                for b in range(XB):
                    mm = pe.matmul(po[:, :], y[:, b, :], wo[:, b, :], start=b == 0, stop=b == XB - 1)
                mm.then_inc(op, 1)
                pe.wait_ge(tree, t * 3 + 6)
                if not static(t, T - 1):
                    pe.wait_ge(cbm_done, t + 2 + CR)
                pe.matmul(pk[:, 2, 0:1], ysq[:, 0, :], ones[:, :], start=True, stop=True).then_inc(ss, 1)

            def body(g, par):
                for c in range(2):
                    t = g * 2 + c
                    tok = slice(c * P, (c + 1) * P)
                    taken = TAKEN[c] if not static(g, G - 1) else ()

                    def stage(n):
                        for k in taken[n:n + 1]:
                            stage_pe(pe, g + 1, k, 1 - par)

                    def off(half):
                        pe.wait_ge(ye, t * 2 + half + CR)
                        for b in range(4):
                            cols = carry[:, 4 * half + b, :, :].rearrange("p a d -> p (a d)")
                            mm = pe.matmul(py[0][:, b, :], cols, xs[par][:, XB + 1, tok], start=True, stop=True)
                        mm.then_inc(yoff, 1)

                    def diag(half):
                        pe.wait_ge(yd, t * 2 + half + CR)
                        for b in range(4):
                            for a in range(2):
                                mm = pe.matmul(py[1][a * HD:(a + 1) * HD, b, :], xdt[:, 4 * half + b, a, :],
                                               m[c][:, a * XB + 4 * half + b, :], start=True, stop=True)
                        mm.then_inc(ydiag, 1)

                    pe.wait_ge(xs_done, g * NX + NX + CR)
                    if not static(t, 0, 1):
                        pe.wait_ge(var_done, t - 1 + CR)
                    pe.wait_ge(cbm_done, t + CR)
                    pe.transpose(pk[:, 0, :], xs[par][:, XB, tok], ident[:, :]).then_inc(btr, 1)
                    pe.wait_ge(cadd, t * 2 + CR)
                    for half in range(2):
                        for b in range(4):
                            tr = pe.transpose(pxb[half][:, b, :], xs[par][:, 4 * half + b, tok], ident[:, :])
                        tr.then_inc(xtr, 1)
                    stage(0)
                    pe.wait_ge(btok_done, t + 1 + CR)
                    pe.matmul(pk[:, 1, :], xs[par][:, XB, tok], xs[par][:, XB + 1, tok], start=True,
                              stop=True).then_inc(cbt, 1)
                    stage(1)
                    if not static(t, 0):
                        project(t - 1)
                    off(0)
                    stage(2)
                    off(1)
                    pe.wait_ge(m_done, t + 1 + CR)
                    diag(0)
                    pe.wait_ge(xdd_done, t + 1 + CR)
                    for half in range(2):
                        mm = pe.matmul(pxb[half][:, :, :].rearrange("p b l -> p (b l)"), btok[:, :],
                                       xdd[:, 4 * half:4 * half + 4, :, :].rearrange("p b a d -> p (b a d)"),
                                       start=True, stop=True)
                    mm.then_inc(st, 1)
                    diag(1)
                    stage(3)
                    stage(4)

            groups(pe, body)
            project(T - 1)


def kernel(**inputs):
    import numpy as np
    import concourse.bacc as bacc
    from concourse.bass_utils import run_bass_kernel_spmd as run

    a = {k: np.ascontiguousarray(v) for k, v in inputs.items()}
    w = a["L0_attn_in_proj_w"]
    zw, xw, dtw = w[:INNER], w[INNER:INNER + CB * P], w[INNER + CB * P:]

    def by_half(v):
        return v.reshape(XB, 2, -1).transpose(1, 0, 2).reshape(v.shape)

    def rows(wt, n):
        return np.ascontiguousarray(wt.reshape(n, P, -1).transpose(1, 0, 2))

    row = np.zeros((1, ROW_N), np.float32)
    row[0, ROW["rank"]] = np.arange(E, 0, -1)
    row[0, ROW["full"]] = np.arange(T) * P
    row[0, ROW["before"]] = np.tril(np.ones((E, E)), -1).reshape(-1)
    row[0, ROW["tile"]] = np.arange(J)
    row[0, ROW["iota"]] = np.arange(P)
    row[0, ROW["tok_tile"]] = np.tile(np.arange(T), 2)
    gu = np.concatenate([a["L0_ffn_w_gate_proj"], a["L0_ffn_w_up_proj"]], axis=1)
    arrays = {
        "x": a["L0_attn_u"].reshape(TOKENS, D),
        "w_in": rows(np.concatenate([xw, zw]).T, KD),
        "w_dtr": rows(np.concatenate([by_half(dtw), a["L0_ffn_w_gate_router"]]).T, KD),
        "w_out": rows(a["L0_attn_out_proj_w"].T, XB),
        "conv_w": rows(a["L0_attn_conv_w"], CB),
        "conv_b": np.ascontiguousarray(a["L0_attn_conv_b"].reshape(CB, P).T),
        "dt_bias": by_half(a["L0_attn_dt_bias"]).reshape(1, HEADS),
        "a_log": by_half(a["L0_attn_A_log"]).reshape(1, HEADS),
        "d_skip": np.ascontiguousarray(np.repeat(a["L0_attn_D_skip"], HD).reshape(XB, P).T),
        "norm_w": np.ascontiguousarray(a["L0_attn_norm_w"].reshape(XB, P).T),
        "w_gu": np.ascontiguousarray(gu.transpose(0, 2, 1).reshape(E, KD, P, 2 * F).transpose(0, 2, 1, 3)),
        "w_down": np.ascontiguousarray(a["L0_ffn_w_down_proj"].transpose(0, 2, 1).reshape(E, 2, FH, D)
                                       .transpose(0, 2, 1, 3)),
        "ident_in": np.eye(P, dtype=np.float32),
        "tri_in": np.triu(np.ones((P, P), np.float32)),
        "stri_in": np.triu(np.ones((P, P), np.float32), 1),
        "row_in": row,
        "part_in": np.arange(P, dtype=np.float32).reshape(P, 1),
    }
    nc = bacc.Bacc("TRN2", target_bir_lowering=False, num_devices=1)
    args = [nc.dram_tensor(f"in_{n}", v.shape, F32, kind="ExternalInput").ap() for n, v in arrays.items()]
    args.append(nc.dram_tensor("out", (TOKENS, D), F32, kind="ExternalOutput").ap())
    block(nc, *args)
    r = run(nc, [{f"in_{n}": v for n, v in arrays.items()}], core_ids=[0])
    return r.results[0]["out"].reshape(a["L0_attn_u"].shape)
```
